# Optimizing a Trainium2 kernel written in Bass

```python
import numpy as np
import jax
import jax.numpy as jnp

def _softmax(x, axis=-1):
    return jax.nn.softmax(x, axis=axis)

def _gelu(x):
    return jax.nn.gelu(x, approximate=True)

def _silu(x):
    return jax.nn.silu(x)

def _sigmoid(x):
    return jax.nn.sigmoid(x)

def _layernorm(x, axis=-1, eps=1e-05):
    m = jnp.mean(x, axis=axis, keepdims=True)
    v = jnp.var(x, axis=axis, keepdims=True)
    return (x - m) / jnp.sqrt(v + eps)

def _scatter_add(tgt, idx, src, axis=0):
    return tgt.at[idx].add(src)

def _segment_sum(src, seg, n):
    return jax.ops.segment_sum(src, seg, n)
kernel_name = 'mk_audio_tower_d1_tok_audfeat512_r4_466a31'

def setup_inputs(seed: int=0):
    np.random.seed(seed)
    _w = jnp.asarray

    def _rec_inputs():
        import jax
        import jax.numpy as jnp
        _rk = jax.random.key(seed)
        x = -0.000392918 + 0.999932 * jax.random.normal(jax.random.fold_in(_rk, 1), (8, 750, 128), jnp.float32)
        return x
    x = _rec_inputs()

    def _L0_tok_setup():
        import jax, jax.numpy as jnp
        import numpy as np
        B, T, C, H = (16, 512, 128, 512)
        FACTOR = 2

        def _warp(X, new_lens, new_T):
            cs = jnp.cumsum(new_lens, axis=1)
            grid = jnp.arange(new_T, dtype=X.dtype)
            P = jnp.maximum(cs[:, :, None] - grid[None, None, :], 0.0)
            Pm1 = jnp.pad(P, ((0, 0), (1, 0), (0, 0)))[:, :-1, :]
            shiftc = lambda A: jnp.pad(A, ((0, 0), (0, 0), (0, 1)))[:, :, 1:]
            Wt = -Pm1 + shiftc(Pm1) + P - shiftc(P)
            interp_weights = jnp.swapaxes(Wt, 1, 2)
            Xnew = interp_weights @ X
            return (Xnew, interp_weights)
        key = jax.random.key(seed)
        ks = jax.random.split(key, 7)
        w = lambda k, shape, fan_in: jax.random.normal(k, shape, jnp.float32) / np.sqrt(fan_in)
        return {'features': jax.random.normal(ks[0], (B, T, C), jnp.float32), 'W1': w(ks[1], (C, H), C), 'b1': jnp.zeros((H,), jnp.float32), 'W2': w(ks[2], (H, H), H), 'b2': jnp.zeros((H,), jnp.float32), 'W3': w(ks[3], (H, 1), H), 'b3': jnp.zeros((1,), jnp.float32)}
    _L0_tok_all = _L0_tok_setup()
    _L0_tok_in = {k: v for k, v in _L0_tok_all.items() if k in ('W1', 'b1', 'W2', 'b2', 'W3', 'b3')}
    del _L0_tok_all

    def _L0_attn_setup():
        import jax, jax.numpy as jnp
        import numpy as np
        DIM = 128
        H = 8
        C = 64
        HID = H * C
        NMEM = H

        def _rmsnorm_seq(x, w):
            n = jnp.sqrt(jnp.sum(x * x, axis=2, keepdims=True))
            return x / jnp.maximum(n, 1e-12) * w * jnp.asarray(DIM ** 0.5, x.dtype)
        key = jax.random.key(seed)
        ks = jax.random.split(key, 7)
        b, n = (4, 1024)
        x = jax.random.normal(ks[0], (b, n, DIM), dtype=jnp.float32)
        norm_w = jnp.ones((1, 1, DIM), dtype=jnp.float32)
        w_qkv = jax.random.normal(ks[1], (DIM, 3 * HID), dtype=jnp.float32) / np.sqrt(DIM)
        mem_kv = jax.random.normal(ks[2], (2, H, C, NMEM), dtype=jnp.float32)
        w_out = jax.random.normal(ks[3], (HID, DIM), dtype=jnp.float32) / np.sqrt(HID)
        b_out = jax.random.normal(ks[4], (DIM,), dtype=jnp.float32) * 0.01
        out_norm_w = jnp.ones((1, 1, DIM), dtype=jnp.float32)
        return {'x': x, 'norm_w': norm_w, 'w_qkv': w_qkv, 'mem_kv': mem_kv, 'w_out': w_out, 'b_out': b_out, 'out_norm_w': out_norm_w}
    _L0_attn_all = _L0_attn_setup()
    _L0_attn_in = {k: v for k, v in _L0_attn_all.items() if k in ('norm_w', 'w_qkv', 'mem_kv', 'w_out', 'b_out', 'out_norm_w')}
    del _L0_attn_all

    def _L0_ffn_setup():
        import jax, jax.numpy as jnp
        import numpy as np
        CAPACITY_FACTOR = 1.2
        key = jax.random.key(seed)
        k1, k2, k3 = jax.random.split(key, 3)
        B, S, D, E = (8, 1024, 128, 16)
        x = jax.random.normal(k1, (B, S, D), dtype=jnp.float32)
        switch_w = jax.random.normal(k2, (E, D), dtype=jnp.float32) * 0.02
        switch_b = jnp.zeros((E,), dtype=jnp.float32)
        expert_w = jax.random.normal(k3, (E, D, D), dtype=jnp.float32) * 0.02
        expert_b = jnp.zeros((E, D), dtype=jnp.float32)
        return {'x': x, 'switch_w': switch_w, 'switch_b': switch_b, 'expert_w': expert_w, 'expert_b': expert_b}
    _L0_ffn_all = _L0_ffn_setup()
    _L0_ffn_in = {k: v for k, v in _L0_ffn_all.items() if k in ('switch_w', 'switch_b', 'expert_w', 'expert_b')}
    del _L0_ffn_all
    return {'x': x, 'L0_tok_W1': _L0_tok_in['W1'], 'L0_tok_b1': _L0_tok_in['b1'], 'L0_tok_W2': _L0_tok_in['W2'], 'L0_tok_b2': _L0_tok_in['b2'], 'L0_tok_W3': _L0_tok_in['W3'], 'L0_tok_b3': _L0_tok_in['b3'], 'L0_attn_norm_w': _L0_attn_in['norm_w'], 'L0_attn_w_qkv': _L0_attn_in['w_qkv'], 'L0_attn_mem_kv': _L0_attn_in['mem_kv'], 'L0_attn_w_out': _L0_attn_in['w_out'], 'L0_attn_b_out': _L0_attn_in['b_out'], 'L0_attn_out_norm_w': _L0_attn_in['out_norm_w'], 'L0_ffn_switch_w': _L0_ffn_in['switch_w'], 'L0_ffn_switch_b': _L0_ffn_in['switch_b'], 'L0_ffn_expert_w': _L0_ffn_in['expert_w'], 'L0_ffn_expert_b': _L0_ffn_in['expert_b']}

def reference(x, L0_tok_W1, L0_tok_b1, L0_tok_W2, L0_tok_b2, L0_tok_W3, L0_tok_b3, L0_attn_norm_w, L0_attn_w_qkv, L0_attn_mem_kv, L0_attn_w_out, L0_attn_b_out, L0_attn_out_norm_w, L0_ffn_switch_w, L0_ffn_switch_b, L0_ffn_expert_w, L0_ffn_expert_b):
    import jax
    import jax.numpy as jnp

    def _L0_tok_ref(features, W1, b1, W2, b2, W3, b3):
        import jax, jax.numpy as jnp
        import numpy as np
        B, T, C, H = (16, 512, 128, 512)
        FACTOR = 2

        def _warp(X, new_lens, new_T):
            cs = jnp.cumsum(new_lens, axis=1)
            grid = jnp.arange(new_T, dtype=X.dtype)
            P = jnp.maximum(cs[:, :, None] - grid[None, None, :], 0.0)
            Pm1 = jnp.pad(P, ((0, 0), (1, 0), (0, 0)))[:, :-1, :]
            shiftc = lambda A: jnp.pad(A, ((0, 0), (0, 0), (0, 1)))[:, :, 1:]
            Wt = -Pm1 + shiftc(Pm1) + P - shiftc(P)
            interp_weights = jnp.swapaxes(Wt, 1, 2)
            Xnew = interp_weights @ X
            return (Xnew, interp_weights)
        Bq, Tq, Cq = features.shape
        h = jax.nn.gelu(features @ W1 + b1, approximate=False)
        h = jax.nn.gelu(h @ W2 + b2, approximate=False)
        new_lens = jax.nn.sigmoid((h @ W3 + b3)[..., 0])
        new_lens = new_lens / jnp.sum(new_lens, axis=1, keepdims=True) * (Tq / FACTOR)
        new_T = Tq // FACTOR
        Xnew, _ = _warp(features, new_lens, new_T)
        return Xnew

    def _L0_attn_ref(x, norm_w, w_qkv, mem_kv, w_out, b_out, out_norm_w):
        import jax, jax.numpy as jnp
        import numpy as np
        DIM = 128
        H = 8
        C = 64
        HID = H * C
        NMEM = H

        def _rmsnorm_seq(x, w):
            n = jnp.sqrt(jnp.sum(x * x, axis=2, keepdims=True))
            return x / jnp.maximum(n, 1e-12) * w * jnp.asarray(DIM ** 0.5, x.dtype)
        b, n, _ = x.shape
        scale = jnp.asarray(C ** (-0.5), x.dtype)
        xn = _rmsnorm_seq(x, norm_w)
        qkv = xn @ w_qkv
        q, k, v = jnp.split(qkv, 3, axis=2)

        def to_heads(t):
            return t.reshape(b, n, H, C).transpose(0, 2, 3, 1)
        q, k, v = map(to_heads, (q, k, v))
        mk = jnp.broadcast_to(mem_kv[0], (b, H, C, NMEM))
        mv = jnp.broadcast_to(mem_kv[1], (b, H, C, NMEM))
        k = jnp.concatenate([mk, k], axis=-1)
        v = jnp.concatenate([mv, v], axis=-1)
        q = jax.nn.softmax(q, axis=-2) * scale
        k = jax.nn.softmax(k, axis=-1)
        context = jnp.einsum('bhdn,bhen->bhde', k, v)
        out = jnp.einsum('bhde,bhdn->bhen', context, q)
        out = out.transpose(0, 3, 1, 2).reshape(b, n, HID)
        out = out @ w_out + b_out
        return _rmsnorm_seq(out, out_norm_w)

    def _L0_ffn_ref(x, switch_w, switch_b, expert_w, expert_b):
        import jax, jax.numpy as jnp
        import numpy as np
        CAPACITY_FACTOR = 1.2
        B, S, D = x.shape
        E = switch_w.shape[0]
        N = B * S
        xf = x.reshape(N, D)
        logits = xf @ switch_w.T + switch_b
        probs = jax.nn.softmax(logits, axis=-1)
        route_probs = jnp.max(probs, axis=-1)
        routes = jnp.argmax(probs, axis=-1)
        oh = jax.nn.one_hot(routes, E, dtype=jnp.int32)
        pos = jnp.take_along_axis(jnp.cumsum(oh, axis=0), routes[:, None], axis=1)[:, 0] - 1
        capacity = int(CAPACITY_FACTOR * N / E)
        keep = pos < capacity
        buf = jnp.zeros((E, capacity, D), dtype=xf.dtype).at[routes, pos].set(xf)
        y = jnp.einsum('ecd,efd->ecf', buf, expert_w) + expert_b[:, None, :]
        gathered = y[routes, jnp.minimum(pos, capacity - 1)]
        out = jnp.where(keep[:, None], gathered, xf) * route_probs[:, None]
        return out.reshape(B, S, D)
    h = _L0_tok_ref(x, L0_tok_W1, L0_tok_b1, L0_tok_W2, L0_tok_b2, L0_tok_W3, L0_tok_b3)
    h = h + _L0_attn_ref(_layernorm(h, axis=-1), L0_attn_norm_w, L0_attn_w_qkv, L0_attn_mem_kv, L0_attn_w_out, L0_attn_b_out, L0_attn_out_norm_w)
    h = h + _L0_ffn_ref(_layernorm(h, axis=-1), L0_ffn_switch_w, L0_ffn_switch_b, L0_ffn_expert_w, L0_ffn_expert_b)
    return h

_drawn_inputs = setup_inputs


def setup_inputs(seed=0):
    import zlib

    import numpy as np

    out = dict(_drawn_inputs(seed))
    spreads = {'L0_tok_b1': (0.0, 0.1),
     'L0_tok_b2': (0.0, 0.1),
     'L0_attn_norm_w': (1.0, 0.2),
     'L0_attn_out_norm_w': (1.0, 0.2),
     'L0_ffn_switch_b': (0.0, 0.1),
     'L0_ffn_expert_b': (0.0, 0.8)}
    factors = {'L0_ffn_expert_w': 4.549}
    for name, (base, spread) in spreads.items():
        noise = np.random.default_rng([zlib.crc32(name.encode()), seed]).standard_normal(out[name].shape)
        drawn = base * np.exp(spread * noise) if base else spread * noise
        out[name] = jnp.asarray(drawn.astype(out[name].dtype))
    for name, factor in factors.items():
        out[name] = (out[name] * factor).astype(out[name].dtype)
    return out
```

```python
from contextlib import ExitStack

import numpy as np

import concourse.bass as bass
from concourse import mybir

F32 = mybir.dt.float32
F32R = mybir.dt.float32r
BF16 = mybir.dt.bfloat16
U32 = mybir.dt.uint32
I32 = mybir.dt.int32
ALU = mybir.AluOpType
ACT = mybir.ActivationFunctionType
AX = mybir.AxisListType


class Counted:

    def __init__(self, sem, per):
        self.sem, self.per = sem, per

    def count(self, b, k):
        return b * self.per + k


def after(eng, counted, b, k):
    eng.wait_ge(counted.sem, counted.count(b, k))


def audio_tower(nc, x, W1, b1, W2, b2, W3, b3, norm_w, w_qkv, mem_kv, w_out, b_out, out_norm_w,
                switch_w, switch_b, expert_w, expert_b, out):
    B, T, C = x.shape
    H = W1.shape[1]
    G = T // 2
    TP = 125
    TJ, GJ = T // TP, G // TP
    HK = H // 128
    HALF = T // 2
    HP = HALF + 1
    HEADS, D = mem_kv.shape[1], mem_kv.shape[2]
    NM = mem_kv.shape[3]
    HID = HEADS * D
    PAIRS = HID // 128
    NK = G + NM
    E = switch_w.shape[0]
    N = B * G
    CAP = int(1.2 * N / E)
    SLOTS = E * CAP
    SA = (CAP + 1) // 2
    SB = CAP - SA
    EPS = 1e-5
    ROOT_C = float(C) ** 0.5
    LAST = B - 1

    with ExitStack() as ctx:
        def sb(name, shape, dt=F32):
            return ctx.enter_context(nc.sbuf_tensor(name, shape, dt))

        def counted(name, per):
            return Counted(ctx.enter_context(nc.semaphore(name)), per)

        def sem(name):
            return ctx.enter_context(nc.semaphore(name))

        slot_x = nc.dram_tensor("slot_x", [SLOTS + N, C], F32, kind="Internal").ap()
        slot_y = nc.dram_tensor("slot_y", [SLOTS, C], F32, kind="Internal").ap()

        psA = [ctx.enter_context(nc.psum_tensor(f"psA{i}", [128, 512], F32)) for i in range(2)]
        psB = [ctx.enter_context(nc.psum_tensor(f"psB{i}", [128, 512], F32)) for i in range(2)]
        psC = [ctx.enter_context(nc.psum_tensor(f"psC{i}", [128, 512], F32)) for i in range(4)]

        ident = sb("ident", [128, 128])
        ones = sb("ones", [128, 128])
        tri = sb("tri", [TP, TP])
        ones_b = sb("ones_b", [TP, TP], BF16)
        tri_b = sb("tri_b", [TP, TP], BF16)
        neg_g = sb("neg_g", [TP, G])
        p_half = sb("p_half", [TP, GJ])
        m_half = sb("m_half", [TP, GJ])
        m_one = sb("m_one", [TP, TJ])
        euler = sb("euler", [TP, GJ * E])
        rank = sb("rank", [TP, E])
        tok = sb("tok", [TP, GJ])

        W1f = sb("W1f", [C, H]); W1h = sb("W1h", [C, H], F32R); W1l = sb("W1l", [C, H], F32R)
        W2h = sb("W2h", [128, HK, H], F32R); W2l = sb("W2l", [128, HK, H], F32R)
        b1c = sb("b1c", [128, HK])
        b2r = sb("b2r", [TP, H])
        W3r = sb("W3r", [TP, H])
        b3r = sb("b3r", [TP, 1])
        nwc = sb("nwc", [C, 1])
        Wqh = sb("Wqh", [C, 3 * HID], F32R); Wql = sb("Wql", [C, 3 * HID], F32R)
        mkv = sb("mkv", [128, 2, PAIRS, NM])
        mvT = sb("mvT", [NM, HID])
        wo = sb("wo", [128, PAIRS, C])
        bor = sb("bor", [TP, C])
        onr = sb("onr", [TP, C])
        swf = sb("swf", [E, C]); swT = sb("swT", [C, E])
        swbr = sb("swbr", [TP, E])
        ewf = sb("ewf", [128, E, C]); ewT = sb("ewT", [C, E, 128])
        ebr = sb("ebr", [128, E, C])
        zero = ebr[0:120, 0:15, :]

        xt = sb("xt", [TP, TJ, C])
        xs = sb("xs", [TP, TJ, C])
        dx = sb("dx", [TP, TJ, C])
        xTh = sb("xTh", [C, 2, HP], F32R); xTl = sb("xTl", [C, 2, HP], F32R)
        h1 = sb("h1", [128, HK, 2, HP])
        h1h = sb("h1h", [128, HK, 2, HP], F32R); h1l = sb("h1l", [128, HK, 2, HP], F32R)
        h2b = sb("h2b", [TP, 4, H])
        h2p, h2g = h2b[:, 0:2, :], h2b[:, 2:4, :]
        z = sb("z", [TP, TJ])

        sg = sb("sg", [TP, TJ, 3])
        sx = sb("sx", [TP, TJ + 1])
        pre = sb("pre", [TP, TJ + 1])
        rt = sb("rt", [TP, 1])
        cs = sb("cs", [TP, TJ])
        A = sb("A", [TP, TJ, G])

        h = sb("h", [TP, GJ, C])
        st = sb("st", [TP, GJ, 6])
        mv1 = sb("mv1", [TP, GJ, 2])
        rs1 = sb("rs1", [TP, 8, GJ])
        xn = sb("xn", [TP, GJ, C])
        xh = sb("xh", [C, G + 1], F32R); xl = sb("xl", [C, G + 1], F32R)
        v = sb("v", [TP, GJ, HID])
        qm = sb("qm", [TP, GJ, HEADS])
        qa = sb("qa", [128, GJ, HID])
        q = qa[0:TP]
        Wqf = qa[:].rearrange("p j d -> p (j d)")
        qsum = sb("qsum", [TP, GJ * HEADS])
        rq = sb("rq", [TP, GJ * HEADS])
        nkm = sb("nkm", [128, PAIRS])
        ek = sb("ek", [128, PAIRS, NK])
        ksum = sb("ksum", [128, PAIRS])
        rk = sb("rk", [128, PAIRS])
        kT = sb("kT", [TP, GJ, HID])
        kTm = sb("kTm", [NM, HID])
        qT = sb("qT", [128, GJ, PAIRS, TP])
        cbd = sb("cbd", [128, PAIRS, 128])
        m = sb("m", [128, PAIRS, C])
        o = sb("o", [TP, GJ, C])
        osq = sb("osq", [TP, GJ, C])
        ss = sb("ss", [TP, GJ])
        rs2 = sb("rs2", [TP, 3, GJ])
        h2 = sb("h2", [TP, GJ, C])

        st2 = sb("st2", [TP, GJ, 6])
        mv2 = sb("mv2", [TP, GJ, 2])
        rs3 = sb("rs3", [TP, 2, GJ])
        xf = sb("xf", [TP, GJ, C])
        xfT = sb("xfT", [C, G])
        lg = sb("lg", [TP, GJ, E])
        mx = sb("mx", [TP, GJ])
        eq = sb("eq", [TP, GJ, E])
        rm = sb("rm", [TP, GJ])
        oh = sb("oh", [TP, GJ, E], BF16)
        le = sb("le", [TP, GJ, E])
        sume = sb("sume", [TP, GJ])
        rp = sb("rp", [TP, GJ])
        cnt = sb("cnt", [TP, GJ + 1, E], BF16)
        pp = sb("pp", [TP, GJ, E])
        pos = sb("pos", [TP, GJ])
        keep = sb("keep", [TP, GJ])
        place = sb("place", [TP, 5, GJ])
        idx_s = sb("idx_s", [TP, GJ], U32)
        nk = sb("nk", [TP, GJ])
        basef = sb("basef", [128, B * GJ, C])
        base = basef[0:TP]
        W2f = basef[:].rearrange("p j c -> p (j c)")[:, 0:HK * H].rearrange("p (k n) -> p k n", k=HK)
        ck = sb("ck", [TP, B * GJ])
        idx_g = sb("idx_g", [TP, B * GJ], U32)

        sx_a = ewf[0:SA]
        sx_b = h2b[0:SB].rearrange("p k n -> p (k n)").rearrange("p (e c) -> p e c", e=E)
        ya = h1[0:SA].rearrange("p k i t -> p (k i t)")[:, 0:E * C].rearrange("p (e c) -> p e c", e=E)
        yb = A[0:SB].rearrange("p j g -> p (j g)")[:, 0:E * C].rearrange("p (e c) -> p e c", e=E)
        sxT = sb("sxT", [C, 2, CAP])
        yg = [q[:, 0, i * C:(i + 1) * C] for i in range(4)]
        res = xt

        s_w = sem("s_w")
        s_w2 = sem("s_w2")
        s_const = sem("s_const")
        s_csel = sem("s_csel")
        s_prep = sem("s_prep")
        s_prept = sem("s_prept")
        s_prepc = sem("s_prepc")
        s_zero = sem("s_zero"); s_zfill = sem("s_zfill"); s_eb = sem("s_eb")

        c_x = counted("c_x", 16); c_xs = counted("c_xs", 32)
        c_xt = counted("c_xt", 2); c_xth = counted("c_xth", 2); c_xtl = counted("c_xtl", 2)
        c_dx = counted("c_dx", 1)
        c_l1 = counted("c_l1", 8); c_g1 = counted("c_g1", 8); c_h1h = counted("c_h1h", 2); c_h1l = counted("c_h1l", 2)
        c_l2 = counted("c_l2", 6); c_b2 = counted("c_b2", 6); c_g2 = counted("c_g2", 6); c_z = counted("c_z", 6)
        c_sig = counted("c_sig", 4); c_scan = counted("c_scan", 1); c_cs = counted("c_cs", 1)
        c_rt = counted("c_rt", 1); c_csn = counted("c_csn", 1)
        c_rel = counted("c_rel", 1); c_clip = counted("c_clip", 1); c_warp = counted("c_warp", 1)
        c_h = counted("c_h", 1); c_bn = counted("c_bn", 3); c_mv = counted("c_mv", 1); c_rs1 = counted("c_rs1", 8)
        c_xn = counted("c_xn", 1); c_xnt = counted("c_xnt", 1); c_xh = counted("c_xh", 1); c_xl = counted("c_xl", 1)
        c_v = counted("c_v", 3); c_vc = counted("c_vc", 3)
        c_q = counted("c_q", 3); c_qm = counted("c_qm", 3); c_qs = counted("c_qs", 3)
        c_k = counted("c_k", 4); c_km = counted("c_km", 4); c_ke = counted("c_ke", 4)
        c_qe = counted("c_qe", 1); c_qsum = counted("c_qsum", 1); c_rq = counted("c_rq", 1); c_qn = counted("c_qn", 1)
        c_kt = counted("c_kt", 4); c_kta = counted("c_kta", 2); c_ktd = counted("c_ktd", 2)
        c_qt = counted("c_qt", 3); c_qtc = counted("c_qtc", 3)
        c_ctx = counted("c_ctx", 1); c_cba = counted("c_cba", 1); c_cbd = counted("c_cbd", 1)
        c_m = counted("c_m", 1); c_rk = counted("c_rk", 1); c_ms = counted("c_ms", 1)
        c_fin = counted("c_fin", 1); c_o = counted("c_o", 1); c_ss = counted("c_ss", 3); c_rs2 = counted("c_rs2", 3)
        c_on = counted("c_on", 3); c_h2 = counted("c_h2", 1)
        c_bn2 = counted("c_bn2", 3); c_mv2 = counted("c_mv2", 1); c_rs3 = counted("c_rs3", 2); c_xf = counted("c_xf", 1)
        c_xft = counted("c_xft", 1); c_xfc = counted("c_xfc", 1); c_lg = counted("c_lg", 1); c_lb = counted("c_lb", 1)
        c_mx = counted("c_mx", 1); c_eq = counted("c_eq", 2); c_rm = counted("c_rm", 1); c_oh = counted("c_oh", 1)
        c_ls = counted("c_ls", 1); c_le = counted("c_le", 1); c_sume = counted("c_sume", 1); c_rp = counted("c_rp", 1)
        c_cnt = counted("c_cnt", 4); c_pos = counted("c_pos", 1); c_pp = counted("c_pp", 2)
        c_idx = counted("c_idx", 10); c_sct = counted("c_sct", 48)
        c_ck = counted("c_ck", 2); c_base = counted("c_base", 3)

        s_sx = [sem(f"s_sx{i}") for i in range(4)]
        s_ext = sem("s_ext"); s_exc = sem("s_exc"); s_ey = sem("s_ey"); s_eyb = sem("s_eyb")
        s_yst = sem("s_yst"); s_yg = [sem(f"s_yg{i}") for i in range(4)]
        s_res = sem("s_res"); s_out = [sem(f"s_out{i}") for i in range(2)]

        block = ctx.enter_context(nc.Block())

        def half_cols(j):
            c = (j % GJ) * TP
            return j // GJ, slice(c, c + TP)

        @block.sync
        def _(sp):
            sp.dma_start(W1f[:], W1).then_inc(s_w, 16)
            sp.dma_start(b1c[:], b1.rearrange("(k p) -> p k", p=128), allow_slow_non_contiguous=True).then_inc(s_w, 16)
            sp.dma_start(W2f, W2.rearrange("(k p) n -> p k n", p=128)).then_inc(s_w, 16)

            def load_row(b, prev):
                if prev is not None:
                    after(sp, c_xt, prev, 2)
                    after(sp, c_dx, prev, 1)
                sp.dma_start(xt[:], x[bass.ds(b, 1)].rearrange("o (j p) c -> p (o j) c", p=TP)).then_inc(c_x.sem, 16)
                sp.dma_start(xs[:, 0:TJ - 1, :],
                             x[bass.ds(b, 1), 1:1 + (TJ - 1) * TP].rearrange("o (j p) c -> p (o j) c", p=TP)).then_inc(c_xs.sem, 16)
                sp.dma_start(xs[0:TP - 1, TJ - 1, :],
                             x[bass.ds(b, 1), 1 + (TJ - 1) * TP:T].rearrange("o p c -> p (o c)")).then_inc(c_xs.sem, 16)

            sp.wait_ge(s_zero, 2)
            load_row(0, None)
            for dst, src in ((b2r[:], b2.partition_broadcast(TP)), (W3r[:], W3.rearrange("h o -> (o h)").partition_broadcast(TP)),
                             (b3r[:], b3.partition_broadcast(TP)),
                             (nwc[:], norm_w.rearrange("a b c -> c (a b)")), (Wqf, w_qkv),
                             (mkv[:, 0], mem_kv[0].rearrange("(p a) d n -> (a d) p n", a=2)),
                             (mkv[:, 1], mem_kv[1].rearrange("(p a) d n -> (a d) p n", a=2)),
                             (wo[:], w_out.rearrange("(p k) c -> k p c", k=128)),
                             (bor[:], b_out.partition_broadcast(TP)),
                             (onr[:], out_norm_w.rearrange("a b c -> (a b c)").partition_broadcast(TP)),
                             (swf[:], switch_w), (swbr[:], switch_b.partition_broadcast(TP)),
                             (ewf[:], expert_w.rearrange("e f d -> f e d"))):
                sp.dma_start(dst, src, allow_slow_non_contiguous=True).then_inc(s_w2, 16)
            for i in range(2):
                rows = SLOTS // 2
                sp.dma_start(slot_x[i * rows:(i + 1) * rows].rearrange("(p r) c -> p r c", r=15), zero).then_inc(s_zfill, 16)
            load_row(1, 0)
            sp.wait_ge(s_zfill, 32)
            sp.dma_start(ebr[:].rearrange("p e c -> p (e c)"),
                         expert_b.rearrange("e c -> (e c)").partition_broadcast(128)).then_inc(s_eb, 16)
            for b in range(2, B):
                load_row(b, b - 1)

            after(sp, c_sct, LAST, 48)
            for i in range(4):
                part = slot_x[i * 4 * CAP:(i + 1) * 4 * CAP].rearrange("(e s) c -> s e c", s=CAP)
                sp.dma_start(sx_a[:, 4 * i:4 * i + 4, :], part[0:SA]).then_inc(s_sx[i], 16)
                sp.dma_start(sx_b[:, 4 * i:4 * i + 4, :], part[SA:CAP]).then_inc(s_sx[i], 16)
            for i in range(4):
                sp.wait_ge(s_eyb, 4 * (i + 1))
                part = slot_y[i * 4 * CAP:(i + 1) * 4 * CAP].rearrange("(e s) c -> s e c", s=CAP)
                sp.dma_start(part[0:SA], ya[:, 4 * i:4 * i + 4, :]).then_inc(s_yst, 16)
                sp.dma_start(part[SA:CAP], yb[:, 4 * i:4 * i + 4, :]).then_inc(s_yst, 16)
            for b in range(B):
                sp.wait_ge(s_res, GJ * (b + 1))
                sp.dma_start(out[b].rearrange("(j p) c -> p j c", p=TP),
                             res[:, (b % 2) * GJ:(b % 2 + 1) * GJ, :]).then_inc(s_out[b % 2], 16)
            for i in range(2):
                sp.wait_ge(s_out[i], 16 * B // 2)

        @block.gpsimd
        def _(pool):
            pool.memset(ebr[:], 0.0).then_inc(s_zero, 1)
            pool.memset(xs[:], 0.0).then_inc(s_zero, 1)
            pool.memset(ident[:], 0.0).then_inc(s_csel, 1)
            pool.memset(ones[:], 1.0).then_inc(s_csel, 1)
            pool.memset(ones_b[:], 1.0).then_inc(s_csel, 1)
            pool.wait_ge(s_csel, 3)
            pool.affine_select(out=ident[:], in_=ident[:], compare_op=ALU.not_equal, fill=1.0, base=0,
                               pattern=[[-1, 128]], channel_multiplier=1).then_inc(s_const, 1)
            pool.affine_select(out=tri[:], in_=ones[0:TP, 0:TP], compare_op=ALU.is_ge, fill=0.0, base=0,
                               pattern=[[1, TP]], channel_multiplier=-1).then_inc(s_const, 1)
            pool.affine_select(out=tri_b[:], in_=ones_b[:], compare_op=ALU.is_ge, fill=0.0, base=0,
                               pattern=[[1, TP]], channel_multiplier=-1).then_inc(s_const, 1)
            pool.iota(neg_g[:], pattern=[[-1, G]], base=0, channel_multiplier=0,
                      allow_small_or_imprecise_dtypes=True).then_inc(s_const, 1)
            pool.iota(rank[:], pattern=[[-1, E]], base=E, channel_multiplier=0,
                      allow_small_or_imprecise_dtypes=True).then_inc(s_const, 1)
            pool.iota(tok[:], pattern=[[TP, GJ]], base=SLOTS, channel_multiplier=1,
                      allow_small_or_imprecise_dtypes=True).then_inc(s_const, 1)
            pool.memset(p_half[:], 0.5).then_inc(s_const, 1)
            pool.memset(m_half[:], -0.5).then_inc(s_const, 1)
            pool.memset(m_one[:], -1.0).then_inc(s_const, 1)
            pool.memset(euler[:], float(np.e)).then_inc(s_const, 1)
            pool.memset(sx[:], 0.0).then_inc(s_const, 1)
            pool.memset(pre[:], 0.0).then_inc(s_const, 1)
            pool.memset(cbd[:], 0.0).then_inc(s_const, 1)
            pool.memset(cnt[:], 0.0).then_inc(s_const, 1)
            pool.memset(xTh[:, :, HALF:HP].bitcast(F32), 0.0).then_inc(s_const, 1)
            pool.memset(xTl[:, :, HALF:HP].bitcast(F32), 0.0).then_inc(s_const, 1)
            pool.memset(xh[:, G:G + 1].bitcast(F32), 0.0).then_inc(s_const, 1)
            pool.memset(xl[:, G:G + 1].bitcast(F32), 0.0).then_inc(s_const, 1)
            pool.wait_ge(s_const, N_CONST)
            pool.wait_ge(s_w2, 16 * N_W2)

            def differences(b, prev):
                after(pool, c_x, b, 16)
                after(pool, c_xs, b, 32)
                if prev is not None:
                    after(pool, c_warp, prev, 1)
                pool.tensor_tensor(dx[:], xt[:], xs[:], ALU.subtract).then_inc(c_dx.sem, 1)

            def sigmoid(b, prev):
                after(pool, c_z, b, TJ)
                pool.tensor_scalar(sg[:, :, 0], z[:], b3r[:, 0:1], -1.0, ALU.add, ALU.mult).then_inc(c_sig.sem, 1)
                after(pool, c_sig, b, 1)
                pool.tensor_tensor(sg[:, :, 1], euler[:, 0:TJ], sg[:, :, 0], ALU.pow).then_inc(c_sig.sem, 1)
                after(pool, c_sig, b, 2)
                pool.tensor_scalar(sg[:, :, 2], sg[:, :, 1], 1.0, None, ALU.add).then_inc(c_sig.sem, 1)
                after(pool, c_sig, b, 3)
                if prev is not None:
                    after(pool, c_cs, prev, 1)
                pool.tensor_tensor(sx[:, 0:TJ], sg[:, :, 2], m_one[:], ALU.pow).then_inc(c_sig.sem, 1)

            def norm1(b, prev):
                after(pool, c_mv, b, 1)
                if prev is not None:
                    after(pool, c_xn, prev, 1)
                var = mv1[:, :, 1]
                pool.tensor_scalar(rs1[:, 0], var, EPS, None, ALU.add).then_inc(c_rs1.sem, 1)
                pool.tensor_scalar(rs1[:, 1], var, float(C), None, ALU.mult).then_inc(c_rs1.sem, 1)
                after(pool, c_rs1, b, 2)
                pool.tensor_tensor(rs1[:, 2], rs1[:, 0], m_half[:], ALU.pow).then_inc(c_rs1.sem, 1)
                pool.tensor_tensor(rs1[:, 3], rs1[:, 1], p_half[:], ALU.pow).then_inc(c_rs1.sem, 1)
                after(pool, c_rs1, b, 4)
                pool.tensor_tensor(rs1[:, 4], rs1[:, 2], rs1[:, 3], ALU.mult).then_inc(c_rs1.sem, 1)
                after(pool, c_rs1, b, 5)
                pool.tensor_scalar(rs1[:, 5], rs1[:, 4], 1e-12, None, ALU.max).then_inc(c_rs1.sem, 1)
                after(pool, c_rs1, b, 6)
                pool.tensor_tensor(rs1[:, 6], rs1[:, 5], m_one[:, 0:GJ], ALU.pow).then_inc(c_rs1.sem, 1)
                after(pool, c_rs1, b, 7)
                pool.tensor_tensor(rs1[:, 7], rs1[:, 6], rs1[:, 2], ALU.mult).then_inc(c_rs1.sem, 1)

            def norm2(b, prev):
                after(pool, c_ss, b, 3)
                if prev is not None:
                    after(pool, c_on, prev, 3)
                pool.tensor_tensor(rs2[:, 0], ss[:], p_half[:], ALU.pow).then_inc(c_rs2.sem, 1)
                after(pool, c_rs2, b, 1)
                pool.tensor_scalar(rs2[:, 1], rs2[:, 0], 1e-12, None, ALU.max).then_inc(c_rs2.sem, 1)
                after(pool, c_rs2, b, 2)
                pool.tensor_tensor(rs2[:, 2], rs2[:, 1], m_one[:, 0:GJ], ALU.pow).then_inc(c_rs2.sem, 1)

            def norm3(b, prev):
                after(pool, c_mv2, b, 1)
                if prev is not None:
                    after(pool, c_xf, prev, 1)
                pool.tensor_scalar(rs3[:, 0], mv2[:, :, 1], EPS, None, ALU.add).then_inc(c_rs3.sem, 1)
                after(pool, c_rs3, b, 1)
                pool.tensor_tensor(rs3[:, 1], rs3[:, 0], m_half[:], ALU.pow).then_inc(c_rs3.sem, 1)

            def route_exp(b, prev):
                after(pool, c_ls, b, 1)
                pool.tensor_tensor(le[:].rearrange("p j e -> p (j e)"), euler[:], le[:].rearrange("p j e -> p (j e)"),
                                   ALU.pow).then_inc(c_le.sem, 1)

            def counts(b, prev):
                if prev is not None:
                    after(pool, c_cnt, prev, 4)
                    after(pool, c_pos, prev, 1)
                pool.tensor_copy(cnt[:, 0, :], cnt[:, GJ, :]).then_inc(c_cnt.sem, 1)
                after(pool, c_oh, b, 1)
                for j in range(GJ):
                    after(pool, c_cnt, b, j + 1)
                    pool.tensor_tensor(cnt[:, j + 1, :], cnt[:, j, :], oh[:, j, :], ALU.add).then_inc(c_cnt.sem, 1)

            def scatter(b, prev):
                after(pool, c_pp, b, 2)
                after(pool, c_rm, b, 1)
                if prev is not None:
                    after(pool, c_sct, prev, 48)
                    after(pool, c_ck, prev, 2)
                    after(pool, c_idx, prev, 10)
                pool.tensor_scalar(keep[:], pos[:], float(CAP), None, ALU.is_le).then_inc(c_idx.sem, 1)
                pool.tensor_scalar(place[:, 0], rm[:], -float(CAP), float(SLOTS - 1), ALU.mult, ALU.add).then_inc(c_idx.sem, 1)
                after(pool, c_idx, b, 2)
                pool.tensor_tensor(place[:, 1], place[:, 0], pos[:], ALU.add).then_inc(c_idx.sem, 1)
                after(pool, c_idx, b, 3)
                pool.tensor_tensor(place[:, 2], place[:, 1], tok[:], ALU.subtract).then_inc(c_idx.sem, 1)
                after(pool, c_idx, b, 4)
                pool.tensor_tensor(place[:, 3], place[:, 2], keep[:], ALU.mult).then_inc(c_idx.sem, 1)
                after(pool, c_idx, b, 5)
                pool.tensor_tensor(place[:, 4], place[:, 3], tok[:], ALU.add).then_inc(c_idx.sem, 1)
                after(pool, c_idx, b, 6)
                pool.tensor_copy(idx_s[:], place[:, 4]).then_inc(c_idx.sem, 1)
                pool.tensor_scalar(place[:, 2], place[:, 4], float(SLOTS - 1), None, ALU.min).then_inc(c_idx.sem, 1)
                pool.tensor_scalar(tok[:], tok[:], float(G), None, ALU.add).then_inc(c_idx.sem, 1)
                after(pool, c_idx, b, 9)
                pool.tensor_copy(idx_g[:, bass.ds(b * GJ, GJ)], place[:, 2]).then_inc(c_idx.sem, 1)
                for j in range(GJ):
                    pool.indirect_dma_start(out=slot_x, out_offset=bass.IndirectOffsetOnAxis(ap=idx_s[:, j:j + 1], axis=0),
                                            in_=xf[:, j, :], in_offset=None,
                                            bounds_check=SLOTS + N - 1, oob_is_err=True).then_inc(c_sct.sem, 16)

            def row(b, prev):
                differences(b, prev)
                sigmoid(b, prev)
                norm1(b, prev)
                norm2(b, prev)
                norm3(b, prev)
                counts(b, prev)
                route_exp(b, prev)
                scatter(b, prev)

            pool.wait_ge(s_zfill, 32)
            row(0, None)
            for b in range(1, B):
                row(b, b - 1)

            after(pool, c_idx, LAST, 10)
            pool.wait_ge(s_yst, 128)
            for i in range(B * GJ):
                if i >= 4:
                    pool.wait_ge(s_res, i - 3)
                pool.indirect_dma_start(out=yg[i % 4], out_offset=None, in_=slot_y,
                                        in_offset=bass.IndirectOffsetOnAxis(ap=idx_g[:, i:i + 1], axis=0),
                                        bounds_check=SLOTS - 1, oob_is_err=True).then_inc(s_yg[i % 4], 16)

        @block.scalar
        def _(act):
            def copy(out_, in_):
                return nc.scalar.activation(out_, in_, ACT.Copy)

            act.wait_ge(s_prept, 1)
            copy(mvT[:], psC[0][0:NM, 0:HID]).then_inc(s_prepc, 1)
            act.wait_ge(s_prept, 2)
            copy(swT[:], psC[1][:, 0:E]).then_inc(s_prepc, 1)
            for i in range(4):
                act.wait_ge(s_prept, 3 + i)
                copy(ewT[:, 4 * i:4 * i + 4, :], psC[2 + i % 2][:].rearrange("p (e f) -> p e f", e=4)).then_inc(s_prepc, 1)

            def x_hi(b, prev, i):
                after(act, c_xt, b, i + 1)
                if prev is not None:
                    after(act, c_l1, prev, 8)
                copy(xTh[:, i, 0:HALF], psA[i][:, 0:HALF]).then_inc(c_xth.sem, 1)

            def gelu1(b, prev, i, k):
                n = i * HK + k
                after(act, c_l1, b, n + 1)
                if prev is not None and k == 0:
                    after(act, c_h1l, prev, i + 1)
                nc.scalar.activation(h1[:, k, i, :], psA[n % 2][:, 0:HP], ACT.Gelu, bias=b1c[:, k:k + 1]).then_inc(c_g1.sem, 1)

            def gelu2(b, prev, j):
                after(act, c_b2, b, j + 1)
                if j >= 2:
                    after(act, c_z, b, j - 1)
                elif prev is not None:
                    after(act, c_z, prev, TJ - 1 + j)
                nc.scalar.activation(h2g[:, j % 2, :], h2p[:, j % 2, :], ACT.Gelu).then_inc(c_g2.sem, 1)

            def relu(b, prev):
                after(act, c_csn, b, 1)
                if prev is not None:
                    after(act, c_warp, prev, 1)
                for j in range(TJ):
                    last = nc.scalar.activation(A[:, j, :], neg_g[:], ACT.Relu, bias=cs[:, j:j + 1])
                last.then_inc(c_rel.sem, 1)

            def take_h(b, prev):
                after(act, c_warp, b, 1)
                if prev is not None:
                    after(act, c_h2, prev, 1)
                copy(h[:].rearrange("p j c -> p (j c)"), psC[1][0:TP, 0:GJ * C]).then_inc(c_h.sem, 1)

            def xn_hi(b, prev):
                after(act, c_xnt, b, 1)
                if prev is not None:
                    after(act, c_k, prev, 4)
                copy(xh[:, 0:G], psC[2][:, 0:G]).then_inc(c_xh.sem, 1)

            def take_v(b, prev, j):
                after(act, c_v, b, j + 1)
                if prev is not None:
                    after(act, c_ctx, prev, 1)
                copy(v[:, j, :], psC[(3 + j) % 4][0:TP, :]).then_inc(c_vc.sem, 1)

            def exps(b, prev):
                after(act, c_qs, b, GJ)
                nc.scalar.activation(q.rearrange("p j d -> p (j d)"), q.rearrange("p j d -> p (j d)"),
                                     ACT.Exp).then_inc(c_qe.sem, 1)
                if prev is not None:
                    after(act, c_kt, prev, 4)
                    after(act, c_rk, prev, 1)
                for p in range(PAIRS):
                    after(act, c_km, b, p + 1)
                    nc.scalar.activation(ek[:, p, :], psC[(1 + p) % 4][:, 0:NK], ACT.Exp, bias=nkm[:, p:p + 1],
                                         accum_out=ksum[:, p:p + 1]).then_inc(c_ke.sem, 1)

            def take_kt(b, prev, j):
                after(act, c_kt, b, j + 1)
                if prev is not None:
                    after(act, c_ctx, prev, 1)
                copy(kT[:, j, :], psC[(1 + j) % 4][0:TP, :]).then_inc(c_kta.sem, 1)

            def take_qt(b, prev, j):
                after(act, c_qt, b, j + 1)
                if prev is not None:
                    after(act, c_fin, prev, 1)
                copy(qT[:, j, :, :].rearrange("p a t -> p (a t)"), psC[1 + j][:, 0:PAIRS * TP]).then_inc(c_qtc.sem, 1)

            def take_ctx(b, prev):
                after(act, c_ctx, b, 1)
                if prev is not None:
                    after(act, c_m, prev, 1)
                copy(cbd[D:128, :, D:128], psC[0][D:128, :].rearrange("p (a d) -> p a d", a=PAIRS)[:, :, D:128]).then_inc(c_cba.sem, 1)

            def take_xft(b, prev):
                after(act, c_xft, b, 1)
                if prev is not None:
                    after(act, c_lg, prev, 1)
                copy(xfT[:], psC[3][:, 0:G]).then_inc(c_xfc.sem, 1)

            def row(b, prev):
                for i in range(2):
                    x_hi(b, prev, i)
                for i in range(2):
                    for k in range(HK):
                        gelu1(b, prev, i, k)
                for j in range(TJ):
                    gelu2(b, prev, j)
                relu(b, prev)
                take_h(b, prev)
                xn_hi(b, prev)
                for j in range(GJ):
                    take_v(b, prev, j)
                exps(b, prev)
                take_kt(b, prev, 0)
                take_kt(b, prev, 2)
                for j in range(GJ):
                    take_qt(b, prev, j)
                take_ctx(b, prev)
                take_xft(b, prev)

            act.wait_ge(s_w, 48)
            act.wait_ge(s_const, N_CONST)
            row(0, None)
            for b in range(1, B):
                row(b, b - 1)

            for e in range(E):
                act.wait_ge(s_ext, e + 1)
                if e >= 2:
                    act.wait_ge(s_ey, e - 1)
                copy(sxT[:, e % 2, :], psA[e % 2][:, 0:CAP]).then_inc(s_exc, 1)

        @block.tensor
        def _(pe):
            mm = nc.tensor.matmul

            def split(ps, wh, wl, mh, ml):
                mm(ps, wh, ml, start=True, stop=False)
                mm(ps, wl, mh, start=False, stop=False)
                return mm(ps, wh, mh, start=False, stop=True)

            pe.wait_ge(s_const, N_CONST)
            pe.wait_ge(s_w2, 16 * N_W2)
            for p in range(PAIRS):
                last = nc.tensor.transpose(psC[0][0:NM, p * 128:(p + 1) * 128], mkv[:, 1, p, :], ident[:])
            last.then_inc(s_prept, 1)
            nc.tensor.transpose(psC[1][:, 0:E], swf[:], ident[0:E, 0:E]).then_inc(s_prept, 1)
            for i in range(4):
                if i >= 2:
                    pe.wait_ge(s_prepc, 1 + i)
                for k in range(4):
                    last = nc.tensor.transpose(psC[2 + i % 2][:, k * 128:(k + 1) * 128], ewf[:, 4 * i + k, :], ident[:])
                last.then_inc(s_prept, 1)

            def x_transposed(b, prev, i):
                after(pe, c_x, b, 16)
                if prev is not None:
                    after(pe, c_g1, prev, 7 + i)
                for j in range(GJ):
                    last = nc.tensor.transpose(psA[i][:, j * TP:(j + 1) * TP], xt[:, GJ * i + j, :], ident[0:TP, 0:TP])
                last.then_inc(c_xt.sem, 1)

            def layer1(b, prev, i, k):
                n = i * HK + k
                after(pe, c_xtl, b, i + 1)
                if n < 2:
                    after(pe, c_xtl, b, n + 1)
                else:
                    after(pe, c_g1, b, n - 1)
                w = slice(k * 128, (k + 1) * 128)
                split(psA[n % 2][:, 0:HP], W1h[:, w], W1l[:, w], xTh[:, i, :], xTl[:, i, :]).then_inc(c_l1.sem, 1)

            def layer2(b, prev, j):
                i, cols = half_cols(j)
                after(pe, c_h1l, b, i + 1)
                if j >= 2:
                    after(pe, c_b2, b, j - 1)
                elif prev is not None:
                    after(pe, c_b2, prev, TJ - 1 + j)
                ps = psB[j % 2][0:TP, :]
                for k in range(HK):
                    hi, lo = h1h[:, k, i, cols], h1l[:, k, i, cols]
                    mm(ps, lo, W2h[:, k, :], start=k == 0, stop=False)
                    mm(ps, hi, W2l[:, k, :], start=False, stop=False)
                    last = mm(ps, hi, W2h[:, k, :], start=False, stop=k == HK - 1)
                last.then_inc(c_l2.sem, 1)

            def sums(b, prev):
                after(pe, c_sig, b, 4)
                after(pe, c_scan, b, 1)
                if prev is not None:
                    after(pe, c_lb, prev, 1)
                mm(psC[0][0:TP, 0:TJ + 1], tri[:], sx[:], start=True, stop=False)
                mm(psC[0][0:TP, 0:TJ + 1], ones[0:TP, 0:TP], pre[:], start=False, stop=True).then_inc(c_cs.sem, 1)

            def warp(b, prev):
                after(pe, c_clip, b, 1)
                after(pe, c_dx, b, 1)
                if prev is not None:
                    after(pe, c_pp, prev, 1)
                for g in range(GJ):
                    for j in range(TJ):
                        last = mm(psC[1][0:TP, g * C:(g + 1) * C], A[:, j, g * TP:(g + 1) * TP], dx[:, j, :],
                                  start=j == 0, stop=j == TJ - 1)
                last.then_inc(c_warp.sem, 1)

            def xn_transposed(b, prev):
                after(pe, c_xn, b, 1)
                if prev is not None:
                    after(pe, c_o, prev, 1)
                for j in range(GJ):
                    last = nc.tensor.transpose(psC[2][:, j * TP:(j + 1) * TP], xn[:, j, :], ident[0:TP, 0:TP])
                last.then_inc(c_xnt.sem, 1)

            def values(b, prev, j):
                after(pe, c_xl, b, 1)
                if j == 0:
                    if prev is not None:
                        after(pe, c_xfc, prev, 1)
                elif j == 1:
                    after(pe, c_csn, b, 1)
                else:
                    after(pe, c_h, b, 1)
                ps = psC[(3 + j) % 4][0:TP, :]
                cols, w = slice(j * TP, (j + 1) * TP), slice(2 * HID, 3 * HID)
                split(ps, xh[:, cols], xl[:, cols], Wqh[:, w], Wql[:, w]).then_inc(c_v.sem, 1)

            def queries(b, prev, j):
                if j >= 1:
                    after(pe, c_vc, b, j)
                ps = psC[(2 + j) % 4][0:TP, :]
                cols, w = slice(j * TP, (j + 1) * TP), slice(0, HID)
                split(ps, xh[:, cols], xl[:, cols], Wqh[:, w], Wql[:, w]).then_inc(c_q.sem, 1)

            def keys(b, prev, p):
                if p == 0:
                    after(pe, c_vc, b, 3)
                else:
                    after(pe, c_qs, b, p)
                bank = psC[(1 + p) % 4]
                w = slice(HID + p * 128, HID + (p + 1) * 128)
                split(bank[:, 0:G + 1], Wqh[:, w], Wql[:, w], xh[:], xl[:])
                mm(bank[:, G:NK], ident[:], mkv[:, 0, p, :], start=True, stop=True).then_inc(c_k.sem, 1)

            def k_transposed(b, prev, j):
                after(pe, c_ke, b, 4)
                cols = slice(j * TP, (j + 1) * TP) if j < GJ else slice(G, NK)
                rows = TP if j < GJ else NM
                for p in range(PAIRS):
                    last = nc.tensor.transpose(psC[(1 + j) % 4][0:rows, p * 128:(p + 1) * 128], ek[:, p, cols], ident[:])
                last.then_inc(c_kt.sem, 1)

            def q_transposed(b, prev, j):
                after(pe, c_qn, b, 1)
                if j == 1:
                    after(pe, c_ktd, b, 1)
                else:
                    after(pe, c_kta, b, 1 if j == 0 else 2)
                for p in range(PAIRS):
                    last = nc.tensor.transpose(psC[1 + j][:, p * TP:(p + 1) * TP], q[:, j, p * 128:(p + 1) * 128],
                                               ident[0:TP, 0:TP])
                last.then_inc(c_qt.sem, 1)

            def context(b, prev):
                after(pe, c_vc, b, 3)
                after(pe, c_kta, b, 2)
                after(pe, c_ktd, b, 2)
                for p in range(PAIRS):
                    d = slice(p * 128, (p + 1) * 128)
                    for j in range(GJ):
                        mm(psC[0][:, d], v[:, j, d], kT[:, j, d], start=j == 0, stop=False)
                    last = mm(psC[0][:, d], mvT[:, d], kTm[:, d], start=False, stop=True)
                last.then_inc(c_ctx.sem, 1)

            def fold(b, prev):
                after(pe, c_cba, b, 1)
                after(pe, c_cbd, b, 1)
                after(pe, c_qtc, b, 1)
                for p in range(PAIRS):
                    last = mm(psC[1][:, p * C:(p + 1) * C], cbd[:, p, :], wo[:, p, :], start=True, stop=True)
                last.then_inc(c_m.sem, 1)

            def attend(b, prev):
                after(pe, c_ms, b, 1)
                after(pe, c_qtc, b, 3)
                for j in range(GJ):
                    for p in range(PAIRS):
                        last = mm(psC[2][0:TP, j * C:(j + 1) * C], qT[:, j, p, :], m[:, p, :], start=p == 0, stop=p == PAIRS - 1)
                last.then_inc(c_fin.sem, 1)

            def xf_transposed(b, prev):
                after(pe, c_xf, b, 1)
                for j in range(GJ):
                    last = nc.tensor.transpose(psC[3][:, j * TP:(j + 1) * TP], xf[:, j, :], ident[0:TP, 0:TP])
                last.then_inc(c_xft.sem, 1)

            def logits(b, prev):
                after(pe, c_xfc, b, 1)
                for j in range(GJ):
                    last = mm(psC[0][0:TP, j * E:(j + 1) * E], xfT[:, j * TP:(j + 1) * TP], swT[:], start=True, stop=True)
                last.then_inc(c_lg.sem, 1)

            def positions(b, prev):
                after(pe, c_oh, b, 1)
                after(pe, c_cnt, b, 4)
                ps = psC[1][0:TP, 0:GJ * E]
                mm(ps, tri_b[:], oh[:].rearrange("p j e -> p (j e)"), start=True, stop=False)
                mm(ps, ones_b[:], cnt[:, 0:GJ, :].rearrange("p j e -> p (j e)"), start=False, stop=True).then_inc(c_pos.sem, 1)

            def row(b, prev):
                for i in range(2):
                    x_transposed(b, prev, i)
                for i in range(2):
                    for k in range(HK):
                        layer1(b, prev, i, k)
                for j in range(TJ):
                    layer2(b, prev, j)
                sums(b, prev)
                warp(b, prev)
                xn_transposed(b, prev)
                for j in range(GJ):
                    values(b, prev, j)
                for j in range(GJ):
                    queries(b, prev, j)
                for p in range(PAIRS):
                    keys(b, prev, p)
                for j in range(GJ + 1):
                    k_transposed(b, prev, j)
                for j in range(GJ):
                    q_transposed(b, prev, j)
                context(b, prev)
                fold(b, prev)
                attend(b, prev)
                xf_transposed(b, prev)
                logits(b, prev)
                positions(b, prev)

            pe.wait_ge(s_prepc, 6)
            pe.wait_ge(s_prep, N_PREP)
            row(0, None)
            for b in range(1, B):
                row(b, b - 1)

            for e in range(E):
                if e % 4 == 0:
                    pe.wait_ge(s_sx[e // 4], 32)
                if e >= 2:
                    pe.wait_ge(s_exc, e - 1)
                nc.tensor.transpose(psA[e % 2][:, 0:SA], sx_a[:, e, :], ident[0:SA, 0:SA])
                nc.tensor.transpose(psA[e % 2][:, SA:CAP], sx_b[:, e, :], ident[0:SB, 0:SB]).then_inc(s_ext, 1)
                pe.wait_ge(s_exc, e + 1)
                if e >= 2:
                    pe.wait_ge(s_eyb, e - 1)
                mm(psB[e % 2][0:SA, 0:C], sxT[:, e % 2, 0:SA], ewT[:, e, :], start=True, stop=True)
                mm(psB[e % 2][0:SB, C:2 * C], sxT[:, e % 2, SA:CAP], ewT[:, e, :], start=True, stop=True).then_inc(s_ey, 1)

        @block.vector
        def _(dve):
            vec = nc.vector

            dve.wait_ge(s_w, 48)
            vec.tensor_copy(W1h[:], W1f[:]).then_inc(s_prep, 1)
            vec.tensor_copy(W2h[:], W2f).then_inc(s_prep, 1)
            dve.wait_ge(s_prep, 2)
            vec.tensor_tensor(W1l[:], W1f[:], W1h[:], ALU.subtract).then_inc(s_prep, 1)
            vec.tensor_tensor(W2l[:], W2f, W2h[:], ALU.subtract).then_inc(s_prep, 1)
            dve.wait_ge(s_w2, 16 * N_W2)
            vec.tensor_scalar(Wqf, Wqf, nwc[:, 0:1], ROOT_C, ALU.mult, ALU.mult).then_inc(s_prep, 1)
            vec.tensor_scalar(onr[:], onr[:], ROOT_C, None, ALU.mult).then_inc(s_prep, 1)
            dve.wait_ge(s_prep, 6)
            vec.tensor_copy(Wqh[:], Wqf).then_inc(s_prep, 1)
            dve.wait_ge(s_prep, 7)
            vec.tensor_tensor(Wql[:], Wqf, Wqh[:], ALU.subtract).then_inc(s_prep, 1)
            dve.wait_ge(s_const, N_CONST)
            dve.wait_ge(s_prep, N_PREP)

            def x_lo(b, prev, i):
                after(dve, c_xth, b, i + 1)
                if prev is not None:
                    after(dve, c_l1, prev, 8)
                vec.tensor_tensor(xTl[:, i, 0:HALF], psA[i][:, 0:HALF], xTh[:, i, 0:HALF], ALU.subtract).then_inc(c_xtl.sem, 1)

            def split_h1(b, prev, i):
                after(dve, c_g1, b, HK * (i + 1))
                if prev is not None:
                    after(dve, c_l2, prev, GJ * (i + 1))
                vec.tensor_copy(h1h[:, :, i, :], h1[:, :, i, :]).then_inc(c_h1h.sem, 1)
                after(dve, c_h1h, b, i + 1)
                vec.tensor_tensor(h1l[:, :, i, :], h1[:, :, i, :], h1h[:, :, i, :], ALU.subtract).then_inc(c_h1l.sem, 1)

            def bias2(b, prev, j):
                after(dve, c_l2, b, j + 1)
                if j >= 2:
                    after(dve, c_g2, b, j - 1)
                elif prev is not None:
                    after(dve, c_g2, prev, TJ - 1 + j)
                vec.tensor_tensor(h2p[:, j % 2, :], psB[j % 2][0:TP, :], b2r[:], ALU.add).then_inc(c_b2.sem, 1)

            def dot3(b, prev, j):
                after(dve, c_g2, b, j + 1)
                if prev is not None and j == 0:
                    after(dve, c_sig, prev, 1)
                vec.tensor_tensor_reduce(h2g[:, j % 2, :], h2g[:, j % 2, :], W3r[:], 1.0, 0.0, ALU.mult, ALU.add,
                                         z[:, j:j + 1]).then_inc(c_z.sem, 1)

            def scan(b, prev):
                after(dve, c_sig, b, 4)
                if prev is not None:
                    after(dve, c_cs, prev, 1)
                vec.tensor_tensor_scan(pre[:, 1:TJ + 1], ones[0:TP, 0:TJ], sx[:, 0:TJ], 0.0, ALU.mult, ALU.add).then_inc(c_scan.sem, 1)

            def lengths(b, prev):
                after(dve, c_cs, b, 1)
                vec.reciprocal(rt[:], psC[0][0:TP, TJ:TJ + 1]).then_inc(c_rt.sem, 1)
                after(dve, c_rt, b, 1)
                if prev is not None:
                    after(dve, c_rel, prev, 1)
                vec.tensor_scalar(cs[:], psC[0][0:TP, 0:TJ], rt[:, 0:1], float(G), ALU.mult, ALU.mult).then_inc(c_csn.sem, 1)

            def clip(b, prev):
                after(dve, c_rel, b, 1)
                vec.tensor_scalar(A[:, :, 0:G - 1], A[:, :, 0:G - 1], 1.0, None, ALU.min).then_inc(c_clip.sem, 1)

            def moments1(b, prev):
                after(dve, c_h, b, 1)
                for j in range(GJ):
                    vec.bn_stats(st[:, j, :], h[:, j, :]).then_inc(c_bn.sem, 1)
                after(dve, c_bn, b, 3)
                if prev is not None:
                    after(dve, c_rs1, prev, 8)
                dve.wait_ge(s_const, N_CONST)
                for j in range(GJ):
                    last = vec.bn_aggr(mv1[:, j, :], st[:, j, :])
                last.then_inc(c_mv.sem, 1)

            def normal1(b, prev):
                after(dve, c_rs1, b, 8)
                if prev is not None:
                    after(dve, c_xnt, prev, 1)
                after(dve, c_mv, b, 1)
                for j in range(GJ):
                    last = vec.tensor_scalar(xn[:, j, :], h[:, j, :], mv1[:, j, 0:1], rs1[:, 7, j:j + 1], ALU.subtract, ALU.mult)
                last.then_inc(c_xn.sem, 1)

            def xn_lo(b, prev):
                after(dve, c_xh, b, 1)
                vec.tensor_tensor(xl[:, 0:G], psC[2][:, 0:G], xh[:, 0:G], ALU.subtract).then_inc(c_xl.sem, 1)

            def query_max(b, prev, j):
                after(dve, c_q, b, j + 1)
                ps = psC[(2 + j) % 4][0:TP, :].rearrange("p (h d) -> p h d", h=HEADS)
                vec.tensor_reduce(qm[:, j, :], ps, AX.X, ALU.max).then_inc(c_qm.sem, 1)
                after(dve, c_qm, b, j + 1)
                if prev is not None:
                    after(dve, c_qt, prev, 3)
                vec.tensor_tensor(q[:, j, :].rearrange("p (h d) -> p h d", h=HEADS), ps,
                                  qm[:, j, :].unsqueeze(2).to_broadcast([TP, HEADS, D]), ALU.subtract).then_inc(c_qs.sem, 1)

            def key_max(b, prev, p):
                after(dve, c_k, b, p + 1)
                if prev is not None:
                    after(dve, c_ke, prev, 4)
                vec.tensor_reduce(nkm[:, p:p + 1], psC[(1 + p) % 4][:, 0:NK], AX.X, ALU.max, negate=True).then_inc(c_km.sem, 1)

            def query_norm(b, prev):
                after(dve, c_qe, b, 1)
                q3 = q.rearrange("p j (h d) -> p (j h) d", d=D)
                vec.tensor_reduce(qsum[:], q3, AX.X, ALU.add).then_inc(c_qsum.sem, 1)
                after(dve, c_qsum, b, 1)
                vec.reciprocal(rq[:], qsum[:]).then_inc(c_rq.sem, 1)
                after(dve, c_rq, b, 1)
                vec.scalar_tensor_tensor(q3, q3, float(D) ** -0.5, rq[:].unsqueeze(2).to_broadcast([TP, GJ * HEADS, D]),
                                         ALU.mult, ALU.mult).then_inc(c_qn.sem, 1)

            def take_kt(b, prev, j):
                after(dve, c_kt, b, j + 1)
                if prev is not None:
                    after(dve, c_ctx, prev, 1)
                if j < GJ:
                    vec.tensor_copy(kT[:, j, :], psC[(1 + j) % 4][0:TP, :]).then_inc(c_ktd.sem, 1)
                else:
                    vec.tensor_copy(kTm[:], psC[(1 + j) % 4][0:NM, :]).then_inc(c_ktd.sem, 1)

            def take_ctx(b, prev):
                after(dve, c_ctx, b, 1)
                if prev is not None:
                    after(dve, c_m, prev, 1)
                vec.tensor_copy(cbd[0:D, :, 0:D], psC[0][0:D, :].rearrange("p (a d) -> p a d", a=PAIRS)[:, :, 0:D]).then_inc(c_cbd.sem, 1)

            def key_sum(b, prev):
                after(dve, c_ke, b, 4)
                if prev is not None:
                    after(dve, c_ms, prev, 1)
                vec.reciprocal(rk[:], ksum[:]).then_inc(c_rk.sem, 1)

            def take_m(b, prev):
                after(dve, c_m, b, 1)
                after(dve, c_rk, b, 1)
                if prev is not None:
                    after(dve, c_fin, prev, 1)
                vec.tensor_tensor(m[:], psC[1][:].rearrange("p (a c) -> p a c", a=PAIRS),
                                  rk[:].unsqueeze(2).to_broadcast([128, PAIRS, C]), ALU.mult).then_inc(c_ms.sem, 1)

            def out_norm(b, prev):
                after(dve, c_fin, b, 1)
                if prev is not None:
                    after(dve, c_on, prev, 3)
                vec.tensor_tensor(o[:], psC[2][0:TP, 0:GJ * C].rearrange("p (j c) -> p j c", j=GJ),
                                  bor[:].unsqueeze(1).to_broadcast([TP, GJ, C]), ALU.add).then_inc(c_o.sem, 1)
                after(dve, c_o, b, 1)
                if prev is not None:
                    after(dve, c_rs2, prev, 3)
                    after(dve, c_h2, prev, 1)
                for j in range(GJ):
                    vec.tensor_tensor_reduce(osq[:, j, :], o[:, j, :], o[:, j, :], 1.0, 0.0, ALU.mult, ALU.add,
                                             ss[:, j:j + 1]).then_inc(c_ss.sem, 1)
                after(dve, c_ss, b, 3)
                after(dve, c_rs2, b, 3)
                for j in range(GJ):
                    vec.scalar_tensor_tensor(osq[:, j, :], o[:, j, :], rs2[:, 2, j:j + 1], onr[:], ALU.mult, ALU.mult).then_inc(c_on.sem, 1)
                after(dve, c_on, b, 3)
                if prev is not None:
                    after(dve, c_base, prev, 3)
                vec.tensor_tensor(h2[:], h[:], osq[:], ALU.add).then_inc(c_h2.sem, 1)

            def moments2(b, prev):
                after(dve, c_h2, b, 1)
                for j in range(GJ):
                    vec.bn_stats(st2[:, j, :], h2[:, j, :]).then_inc(c_bn2.sem, 1)
                after(dve, c_bn2, b, 3)
                if prev is not None:
                    after(dve, c_rs3, prev, 2)
                dve.wait_ge(s_const, N_CONST)
                for j in range(GJ):
                    last = vec.bn_aggr(mv2[:, j, :], st2[:, j, :])
                last.then_inc(c_mv2.sem, 1)

            def normal2(b, prev):
                after(dve, c_mv2, b, 1)
                after(dve, c_rs3, b, 2)
                if prev is not None:
                    after(dve, c_xft, prev, 1)
                    after(dve, c_sct, prev, 48)
                    after(dve, c_base, prev, 3)
                for j in range(GJ):
                    last = vec.tensor_scalar(xf[:, j, :], h2[:, j, :], mv2[:, j, 0:1], rs3[:, 1, j:j + 1], ALU.subtract, ALU.mult)
                last.then_inc(c_xf.sem, 1)

            def route(b, prev):
                after(dve, c_lg, b, 1)
                if prev is not None:
                    after(dve, c_ls, prev, 1)
                vec.tensor_tensor(lg[:], psC[0][0:TP, 0:GJ * E].rearrange("p (j e) -> p j e", j=GJ),
                                  swbr[:].unsqueeze(1).to_broadcast([TP, GJ, E]), ALU.add).then_inc(c_lb.sem, 1)
                after(dve, c_lb, b, 1)
                vec.tensor_reduce(mx[:], lg[:], AX.X, ALU.max).then_inc(c_mx.sem, 1)
                after(dve, c_mx, b, 1)
                mxb = mx[:].unsqueeze(2).to_broadcast([TP, GJ, E])
                rkb = rank[:].unsqueeze(1).to_broadcast([TP, GJ, E])
                vec.tensor_tensor(eq[:], lg[:], mxb, ALU.is_equal).then_inc(c_eq.sem, 1)
                if prev is not None:
                    after(dve, c_sume, prev, 1)
                vec.tensor_tensor(le[:], lg[:], mxb, ALU.subtract).then_inc(c_ls.sem, 1)
                after(dve, c_eq, b, 1)
                vec.tensor_tensor(eq[:], eq[:], rkb, ALU.mult).then_inc(c_eq.sem, 1)
                after(dve, c_eq, b, 2)
                if prev is not None:
                    after(dve, c_idx, prev, 2)
                vec.tensor_reduce(rm[:], eq[:], AX.X, ALU.max).then_inc(c_rm.sem, 1)
                after(dve, c_rm, b, 1)
                if prev is not None:
                    after(dve, c_cnt, prev, 4)
                    after(dve, c_pos, prev, 1)
                vec.tensor_tensor(oh[:], rkb, rm[:].unsqueeze(2).to_broadcast([TP, GJ, E]), ALU.is_equal).then_inc(c_oh.sem, 1)

            def place_in_expert(b, prev):
                after(dve, c_pos, b, 1)
                vec.tensor_tensor(pp[:], psC[1][0:TP, 0:GJ * E].rearrange("p (j e) -> p j e", j=GJ), oh[:], ALU.mult).then_inc(c_pp.sem, 1)
                after(dve, c_pp, b, 1)
                if prev is not None:
                    after(dve, c_idx, prev, 3)
                vec.tensor_reduce(pos[:], pp[:], AX.X, ALU.add).then_inc(c_pp.sem, 1)
                after(dve, c_le, b, 1)
                vec.tensor_reduce(sume[:], le[:], AX.X, ALU.add).then_inc(c_sume.sem, 1)
                after(dve, c_sume, b, 1)
                vec.reciprocal(rp[:], sume[:]).then_inc(c_rp.sem, 1)

            def keep_base(b, prev):
                after(dve, c_rp, b, 1)
                after(dve, c_idx, b, 1)
                ckb = ck[:, bass.ds(b * GJ, GJ)]
                vec.tensor_tensor(ckb, keep[:], rp[:], ALU.mult).then_inc(c_ck.sem, 1)
                after(dve, c_ck, b, 1)
                vec.tensor_tensor(nk[:], rp[:], ckb, ALU.subtract).then_inc(c_ck.sem, 1)
                after(dve, c_ck, b, 2)
                for j in range(GJ):
                    vec.scalar_tensor_tensor(base[:, bass.ds(b * GJ + j, 1), :].rearrange("p o c -> p (o c)"), xf[:, j, :], nk[:, j:j + 1], h2[:, j, :],
                                             ALU.mult, ALU.add).then_inc(c_base.sem, 1)

            def row(b, prev):
                for i in range(2):
                    x_lo(b, prev, i)
                for i in range(2):
                    split_h1(b, prev, i)
                for j in range(TJ + 1):
                    if j < TJ:
                        bias2(b, prev, j)
                    if j >= 1:
                        dot3(b, prev, j - 1)
                scan(b, prev)
                lengths(b, prev)
                clip(b, prev)
                moments1(b, prev)
                normal1(b, prev)
                xn_lo(b, prev)
                for j in range(GJ):
                    query_max(b, prev, j)
                for p in range(PAIRS):
                    key_max(b, prev, p)
                query_norm(b, prev)
                key_sum(b, prev)
                take_kt(b, prev, 1)
                take_kt(b, prev, 3)
                take_ctx(b, prev)
                take_m(b, prev)
                out_norm(b, prev)
                moments2(b, prev)
                normal2(b, prev)
                route(b, prev)
                place_in_expert(b, prev)
                keep_base(b, prev)

            row(0, None)
            for b in range(1, B):
                row(b, b - 1)

            dve.wait_ge(s_eb, 16)
            for e in range(E):
                dve.wait_ge(s_ey, e + 1)
                vec.tensor_tensor(ya[:, e, :], psB[e % 2][0:SA, 0:C], ebr[0:SA, e, :], ALU.add)
                vec.tensor_tensor(yb[:, e, :], psB[e % 2][0:SB, C:2 * C], ebr[0:SB, e, :], ALU.add).then_inc(s_eyb, 1)
            for i in range(B * GJ):
                dve.wait_ge(s_yg[i % 4], 16 * (i // 4 + 1))
                if i >= 2 * GJ and i % GJ == 0:
                    dve.wait_ge(s_out[i // GJ % 2], 16 * (i // (2 * GJ)))
                vec.scalar_tensor_tensor(res[:, i % (2 * GJ), :], yg[i % 4], ck[:, i:i + 1], base[:, i, :],
                                         ALU.mult, ALU.add).then_inc(s_res, 1)


N_CONST = 18
N_W2 = 13
N_PREP = 8

_INS = ['x', 'L0_tok_W1', 'L0_tok_b1', 'L0_tok_W2', 'L0_tok_b2', 'L0_tok_W3', 'L0_tok_b3', 'L0_attn_norm_w',
        'L0_attn_w_qkv', 'L0_attn_mem_kv', 'L0_attn_w_out', 'L0_attn_b_out', 'L0_attn_out_norm_w',
        'L0_ffn_switch_w', 'L0_ffn_switch_b', 'L0_ffn_expert_w', 'L0_ffn_expert_b']


def kernel(**inputs):
    import concourse.bacc as _bacc
    from concourse.bass_utils import run_bass_kernel_spmd as _run

    nc = _bacc.Bacc("TRN2", target_bir_lowering=False, num_devices=1)
    arrays, args = {}, []
    for name in _INS:
        a = np.ascontiguousarray(inputs[name])
        arrays[f"in_{name}"] = a
        args.append(nc.dram_tensor(f"in_{name}", a.shape, mybir.dt.from_np(a.dtype), kind="ExternalInput").ap())
    rows, tokens, channels = inputs["x"].shape
    args.append(nc.dram_tensor("out_0", (rows, tokens // 2, channels), F32, kind="ExternalOutput").ap())
    audio_tower(nc, *args)
    r = _run(nc, [arrays], core_ids=[0])
    return r.results[0]["out_0"]
```

```python
from contextlib import ExitStack

import numpy as np

import concourse.bass as bass
from concourse import mybir

F32 = mybir.dt.float32
F32R = mybir.dt.float32r
BF16 = mybir.dt.bfloat16
U32 = mybir.dt.uint32
I32 = mybir.dt.int32
ALU = mybir.AluOpType
ACT = mybir.ActivationFunctionType
AX = mybir.AxisListType


class Counted:

    def __init__(self, sem, per):
        self.sem, self.per = sem, per

    def count(self, b, k):
        return b * self.per + k


def after(eng, counted, b, k):
    eng.wait_ge(counted.sem, counted.count(b, k))


def audio_tower(nc, x, W1, b1, W2, b2, W3, b3, norm_w, w_qkv, mem_kv, w_out, b_out, out_norm_w,
                switch_w, switch_b, expert_w, expert_b, out):
    B, T, C = x.shape
    H = W1.shape[1]
    G = T // 2
    TP = 125
    TJ, GJ = T // TP, G // TP
    HK = H // 128
    HALF = T // 2
    HP = HALF + 1
    HEADS, D = mem_kv.shape[1], mem_kv.shape[2]
    NM = mem_kv.shape[3]
    HID = HEADS * D
    PAIRS = HID // 128
    NK = G + NM
    E = switch_w.shape[0]
    N = B * G
    CAP = int(1.2 * N / E)
    SLOTS = E * CAP
    SA = (CAP + 1) // 2
    SB = CAP - SA
    EPS = 1e-5
    ROOT_C = float(C) ** 0.5
    LAST = B - 1

    with ExitStack() as ctx:
        def sb(name, shape, dt=F32):
            return ctx.enter_context(nc.sbuf_tensor(name, shape, dt))

        def counted(name, per):
            return Counted(ctx.enter_context(nc.semaphore(name)), per)

        def sem(name):
            return ctx.enter_context(nc.semaphore(name))

        slot_x = nc.dram_tensor("slot_x", [SLOTS + N, C], F32, kind="Internal").ap()
        slot_y = nc.dram_tensor("slot_y", [SLOTS, C], F32, kind="Internal").ap()

        psA = [ctx.enter_context(nc.psum_tensor(f"psA{i}", [128, 512], F32)) for i in range(2)]
        psB = [ctx.enter_context(nc.psum_tensor(f"psB{i}", [128, 512], F32)) for i in range(2)]
        psC = [ctx.enter_context(nc.psum_tensor(f"psC{i}", [128, 512], F32)) for i in range(4)]

        ident = sb("ident", [128, 128])
        ones = sb("ones", [128, 128])
        tri = sb("tri", [TP, TP])
        ones_b = sb("ones_b", [TP, TP], BF16)
        tri_b = sb("tri_b", [TP, TP], BF16)
        neg_g = sb("neg_g", [TP, G])
        p_half = sb("p_half", [TP, GJ])
        m_half = sb("m_half", [TP, GJ])
        m_one = sb("m_one", [TP, TJ])
        euler = sb("euler", [TP, GJ * E])
        rank = sb("rank", [TP, E])
        tok = sb("tok", [TP, GJ])

        W1f = sb("W1f", [C, H]); W1h = sb("W1h", [C, H], F32R); W1l = sb("W1l", [C, H], F32R)
        W2h = sb("W2h", [128, HK, H], F32R); W2l = sb("W2l", [128, HK, H], F32R)
        b1c = sb("b1c", [128, HK])
        b2r = sb("b2r", [TP, H])
        W3r = sb("W3r", [TP, H])
        b3r = sb("b3r", [TP, 1])
        nwc = sb("nwc", [C, 1])
        Wqh = sb("Wqh", [C, 3 * HID], F32R); Wql = sb("Wql", [C, 3 * HID], F32R)
        mkv = sb("mkv", [128, 2, PAIRS, NM])
        mvT = sb("mvT", [NM, HID])
        wo = sb("wo", [128, PAIRS, C])
        bor = sb("bor", [TP, C])
        onr = sb("onr", [TP, C])
        swf = sb("swf", [E, C]); swT = sb("swT", [C, E])
        swbr = sb("swbr", [TP, E])
        ewf = sb("ewf", [128, E, C]); ewT = sb("ewT", [C, E, 128])
        ebr = sb("ebr", [128, E, C])
        zero = ebr[0:120, 0:15, :]

        xt = sb("xt", [TP, TJ, C])
        xs = sb("xs", [TP, TJ, C])
        dx = sb("dx", [TP, TJ, C])
        xTh = sb("xTh", [C, 2, HP], F32R); xTl = sb("xTl", [C, 2, HP], F32R)
        h1 = sb("h1", [128, HK, 2, HP])
        h1h = sb("h1h", [128, HK, 2, HP], F32R); h1l = sb("h1l", [128, HK, 2, HP], F32R)
        h2b = sb("h2b", [TP, 4, H])
        z = sb("z", [TP, TJ])

        sg = sb("sg", [TP, TJ, 3])
        sx = sb("sx", [TP, TJ + 1])
        pre = sb("pre", [TP, TJ + 1])
        rt = sb("rt", [TP, 1])
        cs = sb("cs", [TP, TJ])
        A = sb("A", [TP, TJ, G])

        h = sb("h", [TP, GJ, C])
        hres = sb("hres", [TP, GJ, C])
        st = sb("st", [TP, GJ, 6])
        mv1 = sb("mv1", [TP, GJ, 2])
        rs1 = sb("rs1", [TP, 8, GJ])
        xn = sb("xn", [TP, GJ, C])
        xh = sb("xh", [C, G + 1], F32R); xl = sb("xl", [C, G + 1], F32R)
        v = sb("v", [TP, GJ, HID])
        qm = sb("qm", [TP, GJ, HEADS])
        qa = sb("qa", [128, GJ, HID])
        q = qa[0:TP]
        Wqf = qa[:].rearrange("p j d -> p (j d)")
        qsum = sb("qsum", [TP, GJ * HEADS])
        rq = sb("rq", [TP, GJ * HEADS])
        nkm = sb("nkm", [128, PAIRS])
        ek = sb("ek", [128, PAIRS, NK])
        ksum = sb("ksum", [128, PAIRS])
        rk = sb("rk", [128, PAIRS])
        kT = sb("kT", [TP, GJ, HID])
        kTm = sb("kTm", [NM, HID])
        qT = sb("qT", [128, GJ, PAIRS, TP])
        cbd = sb("cbd", [128, PAIRS, 128])
        m = sb("m", [128, PAIRS, C])
        o = sb("o", [TP, GJ, C])
        osq = sb("osq", [TP, GJ, C])
        ss = sb("ss", [TP, GJ])
        rs2 = sb("rs2", [TP, 3, GJ])
        h2 = sb("h2", [TP, GJ, C])

        st2 = sb("st2", [TP, GJ, 6])
        mv2 = sb("mv2", [TP, GJ, 2])
        rs3 = sb("rs3", [TP, 2, GJ])
        xf = sb("xf", [TP, GJ, C])
        xfT = sb("xfT", [C, G])
        lg = sb("lg", [TP, GJ, E])
        mx = sb("mx", [TP, GJ])
        eq = sb("eq", [TP, GJ, E])
        rm = sb("rm", [TP, GJ])
        oh = sb("oh", [TP, GJ, E], BF16)
        le = sb("le", [TP, GJ, E])
        sume = sb("sume", [TP, GJ])
        rp = sb("rp", [TP, GJ])
        cnt = sb("cnt", [TP, GJ + 1, E], BF16)
        pp = sb("pp", [TP, GJ, E])
        pos = sb("pos", [TP, GJ])
        keep = sb("keep", [TP, GJ])
        place = sb("place", [TP, 5, GJ])
        idx_s = sb("idx_s", [TP, GJ], U32)
        nk = sb("nk", [TP, GJ])
        basef = sb("basef", [128, B * GJ, C])
        base = basef[0:TP]
        W2f = basef[:].rearrange("p j c -> p (j c)")[:, 0:HK * H].rearrange("p (k n) -> p k n", k=HK)
        ck = sb("ck", [TP, B * GJ])
        idx_g = sb("idx_g", [TP, B * GJ], U32)

        sx_a = ewf[0:SA]
        sx_b = h2b[0:SB].rearrange("p k n -> p (k n)").rearrange("p (e c) -> p e c", e=E)
        ya = h1[0:SA].rearrange("p k i t -> p (k i t)")[:, 0:E * C].rearrange("p (e c) -> p e c", e=E)
        yb = A[0:SB].rearrange("p j g -> p (j g)")[:, 0:E * C].rearrange("p (e c) -> p e c", e=E)
        sxT = sb("sxT", [C, 2, CAP])
        yg = [q[:, 0, i * C:(i + 1) * C] for i in range(4)]
        res = xt

        s_w = sem("s_w")
        s_w2 = sem("s_w2")
        s_const = sem("s_const")
        s_csel = sem("s_csel")
        s_prep = sem("s_prep")
        s_prept = sem("s_prept")
        s_prepc = sem("s_prepc")
        s_zero = sem("s_zero"); s_zfill = sem("s_zfill"); s_eb = sem("s_eb")

        c_x = counted("c_x", 16); c_xs = counted("c_xs", 32)
        c_xt = counted("c_xt", 2); c_xth = counted("c_xth", 2); c_xtl = counted("c_xtl", 2)
        c_dx = counted("c_dx", 1)
        c_l1 = counted("c_l1", 8); c_g1 = counted("c_g1", 8); c_h1h = counted("c_h1h", 2); c_h1l = counted("c_h1l", 2)
        c_l2 = counted("c_l2", 6); c_b2 = counted("c_b2", 6); c_g2 = counted("c_g2", 6); c_z = counted("c_z", 6)
        c_sig = counted("c_sig", 4); c_scan = counted("c_scan", 1); c_cs = counted("c_cs", 1)
        c_rt = counted("c_rt", 1); c_csn = counted("c_csn", 1)
        c_rel = counted("c_rel", 1); c_clip = counted("c_clip", 1); c_warp = counted("c_warp", 1)
        c_h = counted("c_h", 1); c_hres = counted("c_hres", 1); c_bn = counted("c_bn", 3); c_mv = counted("c_mv", 1); c_rs1 = counted("c_rs1", 8)
        c_xn = counted("c_xn", 1); c_xnt = counted("c_xnt", 1); c_xh = counted("c_xh", 1); c_xl = counted("c_xl", 1)
        c_v = counted("c_v", 3); c_vc = counted("c_vc", 3)
        c_q = counted("c_q", 3); c_qm = counted("c_qm", 3); c_qs = counted("c_qs", 3)
        c_k = counted("c_k", 4); c_km = counted("c_km", 4); c_ke = counted("c_ke", 4)
        c_qe = counted("c_qe", 1); c_qsum = counted("c_qsum", 1); c_rq = counted("c_rq", 1); c_qn = counted("c_qn", 1)
        c_kt = counted("c_kt", 4); c_kta = counted("c_kta", 4)
        c_qt = counted("c_qt", 3); c_qtc = counted("c_qtc", 3)
        c_ctx = counted("c_ctx", 1); c_cba = counted("c_cba", 1); c_cbd = counted("c_cbd", 1)
        c_m = counted("c_m", 1); c_rk = counted("c_rk", 1); c_ms = counted("c_ms", 1)
        c_fin = counted("c_fin", 1); c_o = counted("c_o", 1); c_ss = counted("c_ss", 3); c_rs2 = counted("c_rs2", 3)
        c_on = counted("c_on", 3); c_h2 = counted("c_h2", 1)
        c_bn2 = counted("c_bn2", 3); c_mv2 = counted("c_mv2", 1); c_rs3 = counted("c_rs3", 2); c_xf = counted("c_xf", 1)
        c_xft = counted("c_xft", 1); c_xfc = counted("c_xfc", 1); c_lg = counted("c_lg", 1); c_lb = counted("c_lb", 1)
        c_mx = counted("c_mx", 1); c_eq = counted("c_eq", 2); c_rm = counted("c_rm", 1); c_oh = counted("c_oh", 1)
        c_ls = counted("c_ls", 1); c_le = counted("c_le", 1); c_sume = counted("c_sume", 1); c_rp = counted("c_rp", 1)
        c_cnt = counted("c_cnt", 4); c_pos = counted("c_pos", 1); c_pp = counted("c_pp", 2)
        c_idx = counted("c_idx", 10); c_sct = counted("c_sct", 48)
        c_ck = counted("c_ck", 2); c_base = counted("c_base", 3)

        s_sx = [sem(f"s_sx{i}") for i in range(4)]
        s_ext = sem("s_ext"); s_exc = sem("s_exc"); s_ey = sem("s_ey"); s_eyb = sem("s_eyb")
        s_yst = sem("s_yst"); s_yg = [sem(f"s_yg{i}") for i in range(4)]
        s_res = sem("s_res"); s_out = [sem(f"s_out{i}") for i in range(2)]

        block = ctx.enter_context(nc.Block())

        def h2_slot(j):
            return j % 4

        def h2_before(j):
            return j + 4 if j < 2 else j

        def half_cols(j):
            c = (j % GJ) * TP
            return j // GJ, slice(c, c + TP)

        def before(b):
            return None if isinstance(b, int) and b == 0 else b - 1

        def has_next(m):
            return not isinstance(m, int) or m < LAST

        def pipeline(eng, step):
            def rows(i):
                return [b if 0 <= b < B else None for b in (i + 1, i, i - 1, i - 2)]

            for i in range(-1, 2):
                step(*rows(i))
            for i in range(2, B - 2):
                step(i + 1, i, i - 1, i - 2)
            for i in range(B - 2, B + 2):
                step(*rows(i))

        @block.sync
        def _(sp):
            sp.dma_start(W1f[:], W1).then_inc(s_w, 16)
            sp.dma_start(b1c[:], b1.rearrange("(k p) -> p k", p=128), allow_slow_non_contiguous=True).then_inc(s_w, 16)
            sp.dma_start(W2f, W2.rearrange("(k p) n -> p k n", p=128)).then_inc(s_w, 16)

            def load_row(b, prev):
                if prev is not None:
                    after(sp, c_xt, prev, 2)
                    after(sp, c_dx, prev, 1)
                sp.dma_start(xt[:], x[bass.ds(b, 1)].rearrange("o (j p) c -> p (o j) c", p=TP)).then_inc(c_x.sem, 16)
                sp.dma_start(xs[:, 0:TJ - 1, :],
                             x[bass.ds(b, 1), 1:1 + (TJ - 1) * TP].rearrange("o (j p) c -> p (o j) c", p=TP)).then_inc(c_xs.sem, 16)
                sp.dma_start(xs[0:TP - 1, TJ - 1, :],
                             x[bass.ds(b, 1), 1 + (TJ - 1) * TP:T].rearrange("o p c -> p (o c)")).then_inc(c_xs.sem, 16)

            sp.wait_ge(s_zero, 2)
            load_row(0, None)
            for dst, src in ((b2r[:], b2.partition_broadcast(TP)), (W3r[:], W3.rearrange("h o -> (o h)").partition_broadcast(TP)),
                             (b3r[:], b3.partition_broadcast(TP)),
                             (nwc[:], norm_w.rearrange("a b c -> c (a b)")), (Wqf, w_qkv),
                             (mkv[:, 0], mem_kv[0].rearrange("(p a) d n -> (a d) p n", a=2)),
                             (mkv[:, 1], mem_kv[1].rearrange("(p a) d n -> (a d) p n", a=2)),
                             (wo[:], w_out.rearrange("(p k) c -> k p c", k=128)),
                             (bor[:], b_out.partition_broadcast(TP)),
                             (onr[:], out_norm_w.rearrange("a b c -> (a b c)").partition_broadcast(TP)),
                             (swf[:], switch_w), (swbr[:], switch_b.partition_broadcast(TP)),
                             (ewf[:], expert_w.rearrange("e f d -> f e d"))):
                sp.dma_start(dst, src, allow_slow_non_contiguous=True).then_inc(s_w2, 16)
            for i in range(2):
                rows = SLOTS // 2
                sp.dma_start(slot_x[i * rows:(i + 1) * rows].rearrange("(p r) c -> p r c", r=15), zero).then_inc(s_zfill, 16)
            load_row(1, 0)
            sp.wait_ge(s_zfill, 32)
            sp.dma_start(ebr[:].rearrange("p e c -> p (e c)"),
                         expert_b.rearrange("e c -> (e c)").partition_broadcast(128)).then_inc(s_eb, 16)
            for b in range(2, B):
                load_row(b, b - 1)

            after(sp, c_sct, LAST, 48)
            for i in range(4):
                part = slot_x[i * 4 * CAP:(i + 1) * 4 * CAP].rearrange("(e s) c -> s e c", s=CAP)
                sp.dma_start(sx_a[:, 4 * i:4 * i + 4, :], part[0:SA]).then_inc(s_sx[i], 16)
                sp.dma_start(sx_b[:, 4 * i:4 * i + 4, :], part[SA:CAP]).then_inc(s_sx[i], 16)
            for i in range(4):
                sp.wait_ge(s_eyb, 4 * (i + 1))
                part = slot_y[i * 4 * CAP:(i + 1) * 4 * CAP].rearrange("(e s) c -> s e c", s=CAP)
                sp.dma_start(part[0:SA], ya[:, 4 * i:4 * i + 4, :]).then_inc(s_yst, 16)
                sp.dma_start(part[SA:CAP], yb[:, 4 * i:4 * i + 4, :]).then_inc(s_yst, 16)
            for b in range(B):
                sp.wait_ge(s_res, GJ * (b + 1))
                sp.dma_start(out[b].rearrange("(j p) c -> p j c", p=TP),
                             res[:, (b % 2) * GJ:(b % 2 + 1) * GJ, :]).then_inc(s_out[b % 2], 16)
            for i in range(2):
                sp.wait_ge(s_out[i], 16 * B // 2)

        @block.gpsimd
        def _(pool):
            pool.memset(ebr[:], 0.0).then_inc(s_zero, 1)
            pool.memset(xs[:], 0.0).then_inc(s_zero, 1)
            pool.memset(ident[:], 0.0).then_inc(s_csel, 1)
            pool.memset(ones[:], 1.0).then_inc(s_csel, 1)
            pool.memset(ones_b[:], 1.0).then_inc(s_csel, 1)
            pool.wait_ge(s_csel, 3)
            pool.affine_select(out=ident[:], in_=ident[:], compare_op=ALU.not_equal, fill=1.0, base=0,
                               pattern=[[-1, 128]], channel_multiplier=1).then_inc(s_const, 1)
            pool.affine_select(out=tri[:], in_=ones[0:TP, 0:TP], compare_op=ALU.is_ge, fill=0.0, base=0,
                               pattern=[[1, TP]], channel_multiplier=-1).then_inc(s_const, 1)
            pool.affine_select(out=tri_b[:], in_=ones_b[:], compare_op=ALU.is_ge, fill=0.0, base=0,
                               pattern=[[1, TP]], channel_multiplier=-1).then_inc(s_const, 1)
            pool.iota(neg_g[:], pattern=[[-1, G]], base=0, channel_multiplier=0,
                      allow_small_or_imprecise_dtypes=True).then_inc(s_const, 1)
            pool.iota(rank[:], pattern=[[-1, E]], base=E, channel_multiplier=0,
                      allow_small_or_imprecise_dtypes=True).then_inc(s_const, 1)
            pool.iota(tok[:], pattern=[[TP, GJ]], base=SLOTS, channel_multiplier=1,
                      allow_small_or_imprecise_dtypes=True).then_inc(s_const, 1)
            pool.memset(p_half[:], 0.5).then_inc(s_const, 1)
            pool.memset(m_half[:], -0.5).then_inc(s_const, 1)
            pool.memset(m_one[:], -1.0).then_inc(s_const, 1)
            pool.memset(euler[:], float(np.e)).then_inc(s_const, 1)
            pool.memset(sx[:], 0.0).then_inc(s_const, 1)
            pool.memset(pre[:], 0.0).then_inc(s_const, 1)
            pool.memset(cbd[:], 0.0).then_inc(s_const, 1)
            pool.memset(cnt[:], 0.0).then_inc(s_const, 1)
            pool.memset(xTh[:, :, HALF:HP].bitcast(F32), 0.0).then_inc(s_const, 1)
            pool.memset(xTl[:, :, HALF:HP].bitcast(F32), 0.0).then_inc(s_const, 1)
            pool.memset(xh[:, G:G + 1].bitcast(F32), 0.0).then_inc(s_const, 1)
            pool.memset(xl[:, G:G + 1].bitcast(F32), 0.0).then_inc(s_const, 1)
            pool.wait_ge(s_const, N_CONST)
            pool.wait_ge(s_w2, 16 * N_W2)

            def differences(b, prev):
                after(pool, c_x, b, 16)
                after(pool, c_xs, b, 32)
                if prev is not None:
                    after(pool, c_warp, prev, 1)
                pool.tensor_tensor(dx[:], xt[:], xs[:], ALU.subtract).then_inc(c_dx.sem, 1)

            def sigmoid(b, prev):
                after(pool, c_z, b, TJ)
                pool.tensor_scalar(sg[:, :, 0], z[:], b3r[:, 0:1], -1.0, ALU.add, ALU.mult).then_inc(c_sig.sem, 1)
                after(pool, c_sig, b, 1)
                pool.tensor_tensor(sg[:, :, 1], euler[:, 0:TJ], sg[:, :, 0], ALU.pow).then_inc(c_sig.sem, 1)
                after(pool, c_sig, b, 2)
                pool.tensor_scalar(sg[:, :, 2], sg[:, :, 1], 1.0, None, ALU.add).then_inc(c_sig.sem, 1)
                after(pool, c_sig, b, 3)
                if prev is not None:
                    after(pool, c_cs, prev, 1)
                pool.tensor_tensor(sx[:, 0:TJ], sg[:, :, 2], m_one[:], ALU.pow).then_inc(c_sig.sem, 1)

            def norm1(b, prev):
                after(pool, c_mv, b, 1)
                if prev is not None:
                    after(pool, c_xn, prev, 1)
                var = mv1[:, :, 1]
                pool.tensor_scalar(rs1[:, 0], var, EPS, None, ALU.add).then_inc(c_rs1.sem, 1)
                pool.tensor_scalar(rs1[:, 1], var, float(C), None, ALU.mult).then_inc(c_rs1.sem, 1)
                after(pool, c_rs1, b, 2)
                pool.tensor_tensor(rs1[:, 2], rs1[:, 0], m_half[:], ALU.pow).then_inc(c_rs1.sem, 1)
                pool.tensor_tensor(rs1[:, 3], rs1[:, 1], p_half[:], ALU.pow).then_inc(c_rs1.sem, 1)
                after(pool, c_rs1, b, 4)
                pool.tensor_tensor(rs1[:, 4], rs1[:, 2], rs1[:, 3], ALU.mult).then_inc(c_rs1.sem, 1)
                after(pool, c_rs1, b, 5)
                pool.tensor_scalar(rs1[:, 5], rs1[:, 4], 1e-12, None, ALU.max).then_inc(c_rs1.sem, 1)
                after(pool, c_rs1, b, 6)
                pool.tensor_tensor(rs1[:, 6], rs1[:, 5], m_one[:, 0:GJ], ALU.pow).then_inc(c_rs1.sem, 1)
                after(pool, c_rs1, b, 7)
                pool.tensor_tensor(rs1[:, 7], rs1[:, 6], rs1[:, 2], ALU.mult).then_inc(c_rs1.sem, 1)

            def norm2(b, prev):
                after(pool, c_ss, b, 3)
                if prev is not None:
                    after(pool, c_on, prev, 3)
                pool.tensor_tensor(rs2[:, 0], ss[:], p_half[:], ALU.pow).then_inc(c_rs2.sem, 1)
                after(pool, c_rs2, b, 1)
                pool.tensor_scalar(rs2[:, 1], rs2[:, 0], 1e-12, None, ALU.max).then_inc(c_rs2.sem, 1)
                after(pool, c_rs2, b, 2)
                pool.tensor_tensor(rs2[:, 2], rs2[:, 1], m_one[:, 0:GJ], ALU.pow).then_inc(c_rs2.sem, 1)

            def norm3(b, prev):
                after(pool, c_mv2, b, 1)
                if prev is not None:
                    after(pool, c_xf, prev, 1)
                pool.tensor_scalar(rs3[:, 0], mv2[:, :, 1], EPS, None, ALU.add).then_inc(c_rs3.sem, 1)
                after(pool, c_rs3, b, 1)
                pool.tensor_tensor(rs3[:, 1], rs3[:, 0], m_half[:], ALU.pow).then_inc(c_rs3.sem, 1)

            def route_exp(b, prev):
                after(pool, c_ls, b, 1)
                pool.tensor_tensor(le[:].rearrange("p j e -> p (j e)"), euler[:], le[:].rearrange("p j e -> p (j e)"),
                                   ALU.pow).then_inc(c_le.sem, 1)

            def counts(b, prev):
                if prev is not None:
                    after(pool, c_cnt, prev, 4)
                    after(pool, c_pos, prev, 1)
                pool.tensor_copy(cnt[:, 0, :], cnt[:, GJ, :]).then_inc(c_cnt.sem, 1)
                after(pool, c_oh, b, 1)
                for j in range(GJ):
                    after(pool, c_cnt, b, j + 1)
                    pool.tensor_tensor(cnt[:, j + 1, :], cnt[:, j, :], oh[:, j, :], ALU.add).then_inc(c_cnt.sem, 1)

            def scatter(b, prev):
                after(pool, c_pp, b, 2)
                after(pool, c_rm, b, 1)
                if prev is not None:
                    after(pool, c_sct, prev, 48)
                    after(pool, c_ck, prev, 2)
                    after(pool, c_idx, prev, 10)
                pool.tensor_scalar(keep[:], pos[:], float(CAP), None, ALU.is_le).then_inc(c_idx.sem, 1)
                pool.tensor_scalar(place[:, 0], rm[:], -float(CAP), float(SLOTS - 1), ALU.mult, ALU.add).then_inc(c_idx.sem, 1)
                after(pool, c_idx, b, 2)
                pool.tensor_tensor(place[:, 1], place[:, 0], pos[:], ALU.add).then_inc(c_idx.sem, 1)
                after(pool, c_idx, b, 3)
                pool.tensor_tensor(place[:, 2], place[:, 1], tok[:], ALU.subtract).then_inc(c_idx.sem, 1)
                after(pool, c_idx, b, 4)
                pool.tensor_tensor(place[:, 3], place[:, 2], keep[:], ALU.mult).then_inc(c_idx.sem, 1)
                after(pool, c_idx, b, 5)
                pool.tensor_tensor(place[:, 4], place[:, 3], tok[:], ALU.add).then_inc(c_idx.sem, 1)
                after(pool, c_idx, b, 6)
                pool.tensor_copy(idx_s[:], place[:, 4]).then_inc(c_idx.sem, 1)
                pool.tensor_scalar(place[:, 2], place[:, 4], float(SLOTS - 1), None, ALU.min).then_inc(c_idx.sem, 1)
                pool.tensor_scalar(tok[:], tok[:], float(G), None, ALU.add).then_inc(c_idx.sem, 1)
                after(pool, c_idx, b, 9)
                pool.tensor_copy(idx_g[:, bass.ds(b * GJ, GJ)], place[:, 2]).then_inc(c_idx.sem, 1)
                for j in range(GJ):
                    pool.indirect_dma_start(out=slot_x, out_offset=bass.IndirectOffsetOnAxis(ap=idx_s[:, j:j + 1], axis=0),
                                            in_=xf[:, j, :], in_offset=None,
                                            bounds_check=SLOTS + N - 1, oob_is_err=True).then_inc(c_sct.sem, 16)

            pool.wait_ge(s_zfill, 32)

            def step(m, f, k, r):
                if f is not None:
                    sigmoid(f, before(f))
                if r is not None:
                    scatter(r, before(r))
                    route_exp(r, before(r))
                if f is not None:
                    norm1(f, before(f))
                if k is not None:
                    norm2(k, before(k))
                if m is not None:
                    differences(m, before(m))
                if k is not None:
                    norm3(k, before(k))
                    counts(k, before(k))

            pipeline(pool, step)

            after(pool, c_idx, LAST, 10)
            pool.wait_ge(s_yst, 128)
            for i in range(B * GJ):
                if i >= 4:
                    pool.wait_ge(s_res, i - 3)
                pool.indirect_dma_start(out=yg[i % 4], out_offset=None, in_=slot_y,
                                        in_offset=bass.IndirectOffsetOnAxis(ap=idx_g[:, i:i + 1], axis=0),
                                        bounds_check=SLOTS - 1, oob_is_err=True).then_inc(s_yg[i % 4], 16)

        @block.scalar
        def _(act):
            def copy(out_, in_):
                return nc.scalar.activation(out_, in_, ACT.Copy)

            act.wait_ge(s_prept, 1)
            copy(mvT[:], psC[0][0:NM, 0:HID]).then_inc(s_prepc, 1)
            act.wait_ge(s_prept, 2)
            copy(swT[:], psC[1][:, 0:E]).then_inc(s_prepc, 1)
            for i in range(4):
                act.wait_ge(s_prept, 3 + i)
                copy(ewT[:, 4 * i:4 * i + 4, :], psC[2 + i % 2][:].rearrange("p (e f) -> p e f", e=4)).then_inc(s_prepc, 1)

            def x_hi(b, prev, i):
                after(act, c_xt, b, i + 1)
                if prev is not None:
                    after(act, c_l1, prev, 8)
                copy(xTh[:, i, 0:HALF], psA[i][:, 0:HALF]).then_inc(c_xth.sem, 1)

            def gelu1(b, prev, i, k):
                n = i * HK + k
                after(act, c_l1, b, n + 1)
                if prev is not None and k == 0:
                    after(act, c_h1l, prev, i + 1)
                nc.scalar.activation(h1[:, k, i, :], psA[n % 2][:, 0:HP], ACT.Gelu, bias=b1c[:, k:k + 1]).then_inc(c_g1.sem, 1)

            def gelu2(b, j):
                after(act, c_b2, b, j + 1)
                slot = h2b[:, h2_slot(j), :]
                nc.scalar.activation(slot, slot, ACT.Gelu).then_inc(c_g2.sem, 1)

            def relu(b, prev):
                after(act, c_csn, b, 1)
                if prev is not None:
                    after(act, c_warp, prev, 1)
                for j in range(TJ):
                    last = nc.scalar.activation(A[:, j, :], neg_g[:], ACT.Relu, bias=cs[:, j:j + 1])
                last.then_inc(c_rel.sem, 1)

            def take_h(b, prev):
                after(act, c_warp, b, 1)
                if prev is not None:
                    after(act, c_xn, prev, 1)
                    after(act, c_hres, prev, 1)
                copy(h[:].rearrange("p j c -> p (j c)"), psC[2][0:TP, 0:GJ * C]).then_inc(c_h.sem, 1)

            def xn_hi(b, prev):
                after(act, c_xnt, b, 1)
                if prev is not None:
                    after(act, c_k, prev, 4)
                copy(xh[:, 0:G], psC[1][:, 0:G]).then_inc(c_xh.sem, 1)

            def take_v(b, prev, j):
                after(act, c_v, b, j + 1)
                if prev is not None:
                    after(act, c_ctx, prev, 1)
                copy(v[:, j, :], psC[(2 + j) % 4][0:TP, :]).then_inc(c_vc.sem, 1)

            def exps(b, prev):
                after(act, c_qs, b, GJ)
                nc.scalar.activation(q.rearrange("p j d -> p (j d)"), q.rearrange("p j d -> p (j d)"),
                                     ACT.Exp).then_inc(c_qe.sem, 1)
                if prev is not None:
                    after(act, c_kt, prev, 4)
                    after(act, c_rk, prev, 1)
                for p in range(PAIRS):
                    after(act, c_km, b, p + 1)
                    nc.scalar.activation(ek[:, p, :], psC[(1 + p) % 4][:, 0:NK], ACT.Exp, bias=nkm[:, p:p + 1],
                                         accum_out=ksum[:, p:p + 1]).then_inc(c_ke.sem, 1)

            def take_kt(b, prev, j):
                after(act, c_kt, b, j + 1)
                if prev is not None:
                    after(act, c_ctx, prev, 1)
                if j < GJ:
                    copy(kT[:, j, :], psC[j][0:TP, :]).then_inc(c_kta.sem, 1)
                else:
                    copy(kTm[:], psC[j][0:NM, :]).then_inc(c_kta.sem, 1)

            def take_qt(b, prev, j):
                after(act, c_qt, b, j + 1)
                if prev is not None:
                    after(act, c_fin, prev, 1)
                copy(qT[:, j, :, :].rearrange("p a t -> p (a t)"), psC[j][:, 0:PAIRS * TP]).then_inc(c_qtc.sem, 1)

            def take_ctx(b, prev):
                after(act, c_ctx, b, 1)
                if prev is not None:
                    after(act, c_m, prev, 1)
                copy(cbd[D:128, :, D:128], psC[0][D:128, :].rearrange("p (a d) -> p a d", a=PAIRS)[:, :, D:128]).then_inc(c_cba.sem, 1)

            def take_xft(b, prev):
                after(act, c_xft, b, 1)
                if prev is not None:
                    after(act, c_lg, prev, 1)
                copy(xfT[:], psA[1][:, 0:G]).then_inc(c_xfc.sem, 1)

            act.wait_ge(s_w, 48)
            act.wait_ge(s_const, N_CONST)

            def step(m, f, k, r):
                if m is not None:
                    gelu1(m, before(m), 0, 0)
                    gelu1(m, before(m), 0, 1)
                if f is not None:
                    gelu2(f, 5)
                if k is not None:
                    take_kt(k, before(k), 0)
                    take_kt(k, before(k), 1)
                if m is not None:
                    gelu1(m, before(m), 0, 2)
                if k is not None:
                    take_kt(k, before(k), 2)
                if m is not None:
                    gelu1(m, before(m), 0, 3)
                if k is not None:
                    take_kt(k, before(k), 3)
                if m is not None:
                    gelu1(m, before(m), 1, 0)
                    gelu1(m, before(m), 1, 1)
                if k is not None:
                    for j in range(GJ):
                        take_qt(k, before(k), j)
                if f is not None:
                    relu(f, before(f))
                if k is not None:
                    take_ctx(k, before(k))
                if m is not None:
                    gelu1(m, before(m), 1, 2)
                    gelu1(m, before(m), 1, 3)
                    gelu2(m, 0)
                if f is not None:
                    take_h(f, before(f))
                if m is not None:
                    gelu2(m, 1)
                    gelu2(m, 2)
                if f is not None:
                    xn_hi(f, before(f))
                    for j in range(GJ):
                        take_v(f, before(f), j)
                if m is not None:
                    gelu2(m, 3)
                if k is not None:
                    take_xft(k, before(k))
                if f is not None:
                    exps(f, before(f))
                if m is not None:
                    x_hi_next(m)
                    gelu2(m, 4)

            def x_hi_next(m):
                if has_next(m):
                    for i in range(2):
                        x_hi(m + 1, m, i)

            for i in range(2):
                x_hi(0, None, i)
            pipeline(act, step)

            for e in range(E):
                act.wait_ge(s_ext, e + 1)
                if e >= 2:
                    act.wait_ge(s_ey, e - 1)
                copy(sxT[:, e % 2, :], psA[e % 2][:, 0:CAP]).then_inc(s_exc, 1)

        @block.tensor
        def _(pe):
            mm = nc.tensor.matmul

            def split(ps, wh, wl, mh, ml):
                mm(ps, wh, ml, start=True, stop=False)
                mm(ps, wl, mh, start=False, stop=False)
                return mm(ps, wh, mh, start=False, stop=True)

            pe.wait_ge(s_const, N_CONST)
            pe.wait_ge(s_w2, 16 * N_W2)
            for p in range(PAIRS):
                last = nc.tensor.transpose(psC[0][0:NM, p * 128:(p + 1) * 128], mkv[:, 1, p, :], ident[:])
            last.then_inc(s_prept, 1)
            nc.tensor.transpose(psC[1][:, 0:E], swf[:], ident[0:E, 0:E]).then_inc(s_prept, 1)
            for i in range(4):
                if i >= 2:
                    pe.wait_ge(s_prepc, 1 + i)
                for k in range(4):
                    last = nc.tensor.transpose(psC[2 + i % 2][:, k * 128:(k + 1) * 128], ewf[:, 4 * i + k, :], ident[:])
                last.then_inc(s_prept, 1)

            def x_transposed(b, prev, i, k):
                after(pe, c_x, b, 16)
                if prev is not None:
                    after(pe, c_g1, prev, 7 + i)
                if k is not None:
                    after(pe, c_lb if i == 0 else c_xfc, k, 1)
                for j in range(GJ):
                    last = nc.tensor.transpose(psA[i][:, j * TP:(j + 1) * TP], xt[:, GJ * i + j, :], ident[0:TP, 0:TP])
                last.then_inc(c_xt.sem, 1)

            def layer1(b, prev, i, k):
                n = i * HK + k
                after(pe, c_xtl, b, i + 1)
                if n < 2:
                    after(pe, c_xtl, b, n + 1)
                else:
                    after(pe, c_g1, b, n - 1)
                w = slice(k * 128, (k + 1) * 128)
                split(psA[n % 2][:, 0:HP], W1h[:, w], W1l[:, w], xTh[:, i, :], xTl[:, i, :]).then_inc(c_l1.sem, 1)

            def layer2(b, prev, j):
                i, cols = half_cols(j)
                after(pe, c_h1l, b, i + 1)
                if j >= 2:
                    after(pe, c_b2, b, j - 1)
                elif prev is not None:
                    after(pe, c_b2, prev, TJ - 1 + j)
                ps = psB[j % 2][0:TP, :]
                for k in range(HK):
                    hi, lo = h1h[:, k, i, cols], h1l[:, k, i, cols]
                    mm(ps, lo, W2h[:, k, :], start=k == 0, stop=False)
                    mm(ps, hi, W2l[:, k, :], start=False, stop=False)
                    last = mm(ps, hi, W2h[:, k, :], start=False, stop=k == HK - 1)
                last.then_inc(c_l2.sem, 1)

            def sums(b, prev):
                after(pe, c_sig, b, 4)
                after(pe, c_scan, b, 1)
                if prev is not None:
                    after(pe, c_kta, prev, 4)
                mm(psC[3][0:TP, 0:TJ + 1], tri[:], sx[:], start=True, stop=False)
                mm(psC[3][0:TP, 0:TJ + 1], ones[0:TP, 0:TP], pre[:], start=False, stop=True).then_inc(c_cs.sem, 1)

            def warp(b, prev):
                after(pe, c_clip, b, 1)
                after(pe, c_dx, b, 1)
                if prev is not None:
                    after(pe, c_qtc, prev, 3)
                for g in range(GJ):
                    for j in range(TJ):
                        last = mm(psC[2][0:TP, g * C:(g + 1) * C], A[:, j, g * TP:(g + 1) * TP], dx[:, j, :],
                                  start=j == 0, stop=j == TJ - 1)
                last.then_inc(c_warp.sem, 1)

            def xn_transposed(b, prev):
                after(pe, c_xn, b, 1)
                if prev is not None:
                    after(pe, c_ms, prev, 1)
                for j in range(GJ):
                    last = nc.tensor.transpose(psC[1][:, j * TP:(j + 1) * TP], xn[:, j, :], ident[0:TP, 0:TP])
                last.then_inc(c_xnt.sem, 1)

            def values(b, prev, j):
                after(pe, c_xl, b, 1)
                if j == 0:
                    after(pe, c_h, b, 1)
                elif j == 1:
                    after(pe, c_csn, b, 1)
                elif prev is not None:
                    after(pe, c_o, prev, 1)
                ps = psC[(2 + j) % 4][0:TP, :]
                cols, w = slice(j * TP, (j + 1) * TP), slice(2 * HID, 3 * HID)
                split(ps, xh[:, cols], xl[:, cols], Wqh[:, w], Wql[:, w]).then_inc(c_v.sem, 1)

            def queries(b, prev, j):
                after(pe, c_vc, b, j + 1)
                ps = psC[(2 + j) % 4][0:TP, :]
                cols, w = slice(j * TP, (j + 1) * TP), slice(0, HID)
                split(ps, xh[:, cols], xl[:, cols], Wqh[:, w], Wql[:, w]).then_inc(c_q.sem, 1)

            def keys(b, prev, p):
                if p >= 1:
                    after(pe, c_qs, b, p)
                else:
                    after(pe, c_xl, b, 1)
                bank = psC[(1 + p) % 4]
                w = slice(HID + p * 128, HID + (p + 1) * 128)
                split(bank[:, 0:G + 1], Wqh[:, w], Wql[:, w], xh[:], xl[:])
                mm(bank[:, G:NK], ident[:], mkv[:, 0, p, :], start=True, stop=True).then_inc(c_k.sem, 1)

            def k_transposed(b, prev, j):
                after(pe, c_ke, b, 4)
                if j == 1 and prev is not None:
                    after(pe, c_pp, prev, 1)
                cols = slice(j * TP, (j + 1) * TP) if j < GJ else slice(G, NK)
                rows = TP if j < GJ else NM
                for p in range(PAIRS):
                    last = nc.tensor.transpose(psC[j][0:rows, p * 128:(p + 1) * 128], ek[:, p, cols], ident[:])
                last.then_inc(c_kt.sem, 1)

            def q_transposed(b, prev, j):
                after(pe, c_qn, b, 1)
                after(pe, c_kta, b, j + 1)
                for p in range(PAIRS):
                    last = nc.tensor.transpose(psC[j][:, p * TP:(p + 1) * TP], q[:, j, p * 128:(p + 1) * 128],
                                               ident[0:TP, 0:TP])
                last.then_inc(c_qt.sem, 1)

            def context(b, prev):
                after(pe, c_vc, b, 3)
                after(pe, c_kta, b, 4)
                after(pe, c_qtc, b, 1)
                for p in range(PAIRS):
                    d = slice(p * 128, (p + 1) * 128)
                    for j in range(GJ):
                        mm(psC[0][:, d], v[:, j, d], kT[:, j, d], start=j == 0, stop=False)
                    last = mm(psC[0][:, d], mvT[:, d], kTm[:, d], start=False, stop=True)
                last.then_inc(c_ctx.sem, 1)

            def fold(b, prev):
                after(pe, c_cba, b, 1)
                after(pe, c_cbd, b, 1)
                after(pe, c_qtc, b, 2)
                for p in range(PAIRS):
                    last = mm(psC[1][:, p * C:(p + 1) * C], cbd[:, p, :], wo[:, p, :], start=True, stop=True)
                last.then_inc(c_m.sem, 1)

            def attend(b, prev):
                after(pe, c_ms, b, 1)
                after(pe, c_qtc, b, 3)
                for j in range(GJ):
                    for p in range(PAIRS):
                        last = mm(psC[0][0:TP, j * C:(j + 1) * C], qT[:, j, p, :], m[:, p, :], start=p == 0, stop=p == PAIRS - 1)
                last.then_inc(c_fin.sem, 1)

            def xf_transposed(b, m):
                after(pe, c_xf, b, 1)
                if m is not None:
                    after(pe, c_g1, m, 8)
                for j in range(GJ):
                    last = nc.tensor.transpose(psA[1][:, j * TP:(j + 1) * TP], xf[:, j, :], ident[0:TP, 0:TP])
                last.then_inc(c_xft.sem, 1)

            def logits(b, m):
                after(pe, c_xfc, b, 1)
                if m is not None:
                    after(pe, c_g1, m, 7)
                for j in range(GJ):
                    last = mm(psA[0][0:TP, j * E:(j + 1) * E], xfT[:, j * TP:(j + 1) * TP], swT[:], start=True, stop=True)
                last.then_inc(c_lg.sem, 1)

            def positions(b, f):
                after(pe, c_oh, b, 1)
                after(pe, c_cnt, b, 4)
                if f is not None:
                    after(pe, c_ke, f, 1)
                ps = psC[1][0:TP, 0:GJ * E]
                mm(ps, tri_b[:], oh[:].rearrange("p j e -> p (j e)"), start=True, stop=False)
                mm(ps, ones_b[:], cnt[:, 0:GJ, :].rearrange("p j e -> p (j e)"), start=False, stop=True).then_inc(c_pos.sem, 1)

            pe.wait_ge(s_prepc, 6)
            pe.wait_ge(s_prep, N_PREP)

            def step(m, f, k, r):
                if m is not None:
                    layer1(m, before(m), 0, 0)
                    layer1(m, before(m), 0, 1)
                if k is not None:
                    k_transposed(k, before(k), 0)
                    k_transposed(k, before(k), 1)
                if m is not None:
                    layer1(m, before(m), 0, 2)
                if k is not None:
                    k_transposed(k, before(k), 2)
                if m is not None:
                    layer1(m, before(m), 0, 3)
                if k is not None:
                    k_transposed(k, before(k), 3)
                if m is not None:
                    layer1(m, before(m), 1, 0)
                    layer1(m, before(m), 1, 1)
                if k is not None:
                    for j in range(GJ):
                        q_transposed(k, before(k), j)
                if f is not None:
                    sums(f, before(f))
                if k is not None:
                    context(k, before(k))
                if m is not None:
                    layer1(m, before(m), 1, 2)
                    layer1(m, before(m), 1, 3)
                    layer2(m, before(m), 0)
                if k is not None:
                    fold(k, before(k))
                if f is not None:
                    warp(f, before(f))
                if k is not None:
                    attend(k, before(k))
                if m is not None:
                    layer2(m, before(m), 1)
                    layer2(m, before(m), 2)
                if f is not None:
                    xn_transposed(f, before(f))
                if m is not None:
                    layer2(m, before(m), 3)
                if f is not None:
                    for j in range(GJ):
                        values(f, before(f), j)
                    for j in range(GJ):
                        queries(f, before(f), j)
                if m is not None:
                    layer2(m, before(m), 4)
                if k is not None:
                    xf_transposed(k, m)
                if f is not None:
                    keys(f, before(f), 0)
                if k is not None:
                    logits(k, m)
                if f is not None:
                    for p in range(1, PAIRS):
                        keys(f, before(f), p)
                if m is not None:
                    x_next(m, k)
                    layer2(m, before(m), 5)
                if k is not None:
                    positions(k, f)

            def x_next(m, k):
                if has_next(m):
                    for i in range(2):
                        x_transposed(m + 1, m, i, k)

            for i in range(2):
                x_transposed(0, None, i, None)
            pipeline(pe, step)

            for e in range(E):
                if e % 4 == 0:
                    pe.wait_ge(s_sx[e // 4], 32)
                if e >= 2:
                    pe.wait_ge(s_exc, e - 1)
                nc.tensor.transpose(psA[e % 2][:, 0:SA], sx_a[:, e, :], ident[0:SA, 0:SA])
                nc.tensor.transpose(psA[e % 2][:, SA:CAP], sx_b[:, e, :], ident[0:SB, 0:SB]).then_inc(s_ext, 1)
                pe.wait_ge(s_exc, e + 1)
                if e >= 2:
                    pe.wait_ge(s_eyb, e - 1)
                mm(psB[e % 2][0:SA, 0:C], sxT[:, e % 2, 0:SA], ewT[:, e, :], start=True, stop=True)
                mm(psB[e % 2][0:SB, C:2 * C], sxT[:, e % 2, SA:CAP], ewT[:, e, :], start=True, stop=True).then_inc(s_ey, 1)

        @block.vector
        def _(dve):
            vec = nc.vector

            dve.wait_ge(s_w, 48)
            vec.tensor_copy(W1h[:], W1f[:]).then_inc(s_prep, 1)
            vec.tensor_copy(W2h[:], W2f).then_inc(s_prep, 1)
            dve.wait_ge(s_prep, 2)
            vec.tensor_tensor(W1l[:], W1f[:], W1h[:], ALU.subtract).then_inc(s_prep, 1)
            vec.tensor_tensor(W2l[:], W2f, W2h[:], ALU.subtract).then_inc(s_prep, 1)
            dve.wait_ge(s_w2, 16 * N_W2)
            vec.tensor_scalar(Wqf, Wqf, nwc[:, 0:1], ROOT_C, ALU.mult, ALU.mult).then_inc(s_prep, 1)
            vec.tensor_scalar(onr[:], onr[:], ROOT_C, None, ALU.mult).then_inc(s_prep, 1)
            dve.wait_ge(s_prep, 6)
            vec.tensor_copy(Wqh[:], Wqf).then_inc(s_prep, 1)
            dve.wait_ge(s_prep, 7)
            vec.tensor_tensor(Wql[:], Wqf, Wqh[:], ALU.subtract).then_inc(s_prep, 1)
            dve.wait_ge(s_const, N_CONST)
            dve.wait_ge(s_prep, N_PREP)

            def x_lo(b, prev, i):
                after(dve, c_xth, b, i + 1)
                if prev is not None:
                    after(dve, c_l1, prev, 8)
                vec.tensor_tensor(xTl[:, i, 0:HALF], psA[i][:, 0:HALF], xTh[:, i, 0:HALF], ALU.subtract).then_inc(c_xtl.sem, 1)

            def split_h1(b, prev, i):
                after(dve, c_g1, b, HK * (i + 1))
                if prev is not None:
                    after(dve, c_l2, prev, GJ * (i + 1))
                vec.tensor_copy(h1h[:, :, i, :], h1[:, :, i, :]).then_inc(c_h1h.sem, 1)
                after(dve, c_h1h, b, i + 1)
                vec.tensor_tensor(h1l[:, :, i, :], h1[:, :, i, :], h1h[:, :, i, :], ALU.subtract).then_inc(c_h1l.sem, 1)

            def bias2(b, prev, j):
                after(dve, c_l2, b, j + 1)
                if j >= 4:
                    after(dve, c_z, b, j - 3)
                elif prev is not None:
                    after(dve, c_z, prev, h2_before(j) + 1)
                vec.tensor_tensor(h2b[:, h2_slot(j), :], psB[j % 2][0:TP, :], b2r[:], ALU.add).then_inc(c_b2.sem, 1)

            def dot3(b, prev, j):
                after(dve, c_g2, b, j + 1)
                if prev is not None and j == 0:
                    after(dve, c_sig, prev, 1)
                vec.tensor_tensor_reduce(h2b[:, h2_slot(j), :], h2b[:, h2_slot(j), :], W3r[:], 1.0, 0.0, ALU.mult, ALU.add,
                                         z[:, j:j + 1]).then_inc(c_z.sem, 1)

            def scan(b, prev):
                after(dve, c_sig, b, 4)
                if prev is not None:
                    after(dve, c_cs, prev, 1)
                vec.tensor_tensor_scan(pre[:, 1:TJ + 1], ones[0:TP, 0:TJ], sx[:, 0:TJ], 0.0, ALU.mult, ALU.add).then_inc(c_scan.sem, 1)

            def lengths(b, prev):
                after(dve, c_cs, b, 1)
                vec.reciprocal(rt[:], psC[3][0:TP, TJ:TJ + 1]).then_inc(c_rt.sem, 1)
                after(dve, c_rt, b, 1)
                if prev is not None:
                    after(dve, c_rel, prev, 1)
                vec.tensor_scalar(cs[:], psC[3][0:TP, 0:TJ], rt[:, 0:1], float(G), ALU.mult, ALU.mult).then_inc(c_csn.sem, 1)

            def clip(b, prev):
                after(dve, c_rel, b, 1)
                vec.tensor_scalar(A[:, :, 0:G - 1], A[:, :, 0:G - 1], 1.0, None, ALU.min).then_inc(c_clip.sem, 1)

            def keep_h(b, prev):
                after(dve, c_h, b, 1)
                if prev is not None:
                    after(dve, c_h2, prev, 1)
                vec.tensor_copy(hres[:], h[:]).then_inc(c_hres.sem, 1)

            def moments1(b, prev):
                after(dve, c_h, b, 1)
                for j in range(GJ):
                    vec.bn_stats(st[:, j, :], h[:, j, :]).then_inc(c_bn.sem, 1)
                after(dve, c_bn, b, 3)
                if prev is not None:
                    after(dve, c_rs1, prev, 8)
                dve.wait_ge(s_const, N_CONST)
                for j in range(GJ):
                    last = vec.bn_aggr(mv1[:, j, :], st[:, j, :])
                last.then_inc(c_mv.sem, 1)

            def normal1(b, prev):
                after(dve, c_rs1, b, 8)
                if prev is not None:
                    after(dve, c_xnt, prev, 1)
                after(dve, c_mv, b, 1)
                for j in range(GJ):
                    last = vec.tensor_scalar(xn[:, j, :], h[:, j, :], mv1[:, j, 0:1], rs1[:, 7, j:j + 1], ALU.subtract, ALU.mult)
                last.then_inc(c_xn.sem, 1)

            def xn_lo(b, prev):
                after(dve, c_xh, b, 1)
                vec.tensor_tensor(xl[:, 0:G], psC[1][:, 0:G], xh[:, 0:G], ALU.subtract).then_inc(c_xl.sem, 1)

            def query_max(b, prev, j):
                after(dve, c_q, b, j + 1)
                ps = psC[(2 + j) % 4][0:TP, :].rearrange("p (h d) -> p h d", h=HEADS)
                vec.tensor_reduce(qm[:, j, :], ps, AX.X, ALU.max).then_inc(c_qm.sem, 1)
                after(dve, c_qm, b, j + 1)
                if prev is not None:
                    after(dve, c_qt, prev, 3)
                vec.tensor_tensor(q[:, j, :].rearrange("p (h d) -> p h d", h=HEADS), ps,
                                  qm[:, j, :].unsqueeze(2).to_broadcast([TP, HEADS, D]), ALU.subtract).then_inc(c_qs.sem, 1)

            def key_max(b, prev, p):
                after(dve, c_k, b, p + 1)
                if prev is not None:
                    after(dve, c_ke, prev, 4)
                vec.tensor_reduce(nkm[:, p:p + 1], psC[(1 + p) % 4][:, 0:NK], AX.X, ALU.max, negate=True).then_inc(c_km.sem, 1)

            q3 = q.rearrange("p j (h d) -> p (j h) d", d=D)

            def query_sum(b, prev):
                after(dve, c_qe, b, 1)
                if prev is not None:
                    after(dve, c_rq, prev, 1)
                vec.tensor_reduce(qsum[:], q3, AX.X, ALU.add).then_inc(c_qsum.sem, 1)
                after(dve, c_qsum, b, 1)
                vec.reciprocal(rq[:], qsum[:]).then_inc(c_rq.sem, 1)

            def query_norm(b, prev):
                after(dve, c_rq, b, 1)
                vec.scalar_tensor_tensor(q3, q3, float(D) ** -0.5, rq[:].unsqueeze(2).to_broadcast([TP, GJ * HEADS, D]),
                                         ALU.mult, ALU.mult).then_inc(c_qn.sem, 1)

            def take_ctx(b, prev):
                after(dve, c_ctx, b, 1)
                if prev is not None:
                    after(dve, c_m, prev, 1)
                vec.tensor_copy(cbd[0:D, :, 0:D], psC[0][0:D, :].rearrange("p (a d) -> p a d", a=PAIRS)[:, :, 0:D]).then_inc(c_cbd.sem, 1)

            def key_sum(b, prev):
                after(dve, c_ke, b, 4)
                if prev is not None:
                    after(dve, c_ms, prev, 1)
                vec.reciprocal(rk[:], ksum[:]).then_inc(c_rk.sem, 1)

            def take_m(b, prev):
                after(dve, c_m, b, 1)
                after(dve, c_rk, b, 1)
                if prev is not None:
                    after(dve, c_fin, prev, 1)
                vec.tensor_tensor(m[:], psC[1][:].rearrange("p (a c) -> p a c", a=PAIRS),
                                  rk[:].unsqueeze(2).to_broadcast([128, PAIRS, C]), ALU.mult).then_inc(c_ms.sem, 1)

            def out_norm(b, prev):
                after(dve, c_fin, b, 1)
                if prev is not None:
                    after(dve, c_on, prev, 3)
                vec.tensor_tensor(o[:], psC[0][0:TP, 0:GJ * C].rearrange("p (j c) -> p j c", j=GJ),
                                  bor[:].unsqueeze(1).to_broadcast([TP, GJ, C]), ALU.add).then_inc(c_o.sem, 1)
                after(dve, c_o, b, 1)
                if prev is not None:
                    after(dve, c_rs2, prev, 3)
                    after(dve, c_h2, prev, 1)
                for j in range(GJ):
                    vec.tensor_tensor_reduce(osq[:, j, :], o[:, j, :], o[:, j, :], 1.0, 0.0, ALU.mult, ALU.add,
                                             ss[:, j:j + 1]).then_inc(c_ss.sem, 1)

            def residual(b, prev):
                after(dve, c_ss, b, 3)
                after(dve, c_rs2, b, 3)
                for j in range(GJ):
                    vec.scalar_tensor_tensor(osq[:, j, :], o[:, j, :], rs2[:, 2, j:j + 1], onr[:], ALU.mult, ALU.mult).then_inc(c_on.sem, 1)
                after(dve, c_on, b, 3)
                after(dve, c_hres, b, 1)
                if prev is not None:
                    after(dve, c_base, prev, 3)
                vec.tensor_tensor(h2[:], hres[:], osq[:], ALU.add).then_inc(c_h2.sem, 1)

            def moments2(b, prev):
                after(dve, c_h2, b, 1)
                for j in range(GJ):
                    vec.bn_stats(st2[:, j, :], h2[:, j, :]).then_inc(c_bn2.sem, 1)
                after(dve, c_bn2, b, 3)
                if prev is not None:
                    after(dve, c_rs3, prev, 2)
                dve.wait_ge(s_const, N_CONST)
                for j in range(GJ):
                    last = vec.bn_aggr(mv2[:, j, :], st2[:, j, :])
                last.then_inc(c_mv2.sem, 1)

            def normal2(b, prev):
                after(dve, c_mv2, b, 1)
                after(dve, c_rs3, b, 2)
                if prev is not None:
                    after(dve, c_xft, prev, 1)
                    after(dve, c_sct, prev, 48)
                    after(dve, c_base, prev, 3)
                for j in range(GJ):
                    last = vec.tensor_scalar(xf[:, j, :], h2[:, j, :], mv2[:, j, 0:1], rs3[:, 1, j:j + 1], ALU.subtract, ALU.mult)
                last.then_inc(c_xf.sem, 1)

            def route(b, prev):
                after(dve, c_lg, b, 1)
                if prev is not None:
                    after(dve, c_ls, prev, 1)
                vec.tensor_tensor(lg[:], psA[0][0:TP, 0:GJ * E].rearrange("p (j e) -> p j e", j=GJ),
                                  swbr[:].unsqueeze(1).to_broadcast([TP, GJ, E]), ALU.add).then_inc(c_lb.sem, 1)
                after(dve, c_lb, b, 1)
                vec.tensor_reduce(mx[:], lg[:], AX.X, ALU.max).then_inc(c_mx.sem, 1)
                after(dve, c_mx, b, 1)
                mxb = mx[:].unsqueeze(2).to_broadcast([TP, GJ, E])
                rkb = rank[:].unsqueeze(1).to_broadcast([TP, GJ, E])
                vec.tensor_tensor(eq[:], lg[:], mxb, ALU.is_equal).then_inc(c_eq.sem, 1)
                if prev is not None:
                    after(dve, c_sume, prev, 1)
                vec.tensor_tensor(le[:], lg[:], mxb, ALU.subtract).then_inc(c_ls.sem, 1)
                after(dve, c_eq, b, 1)
                vec.tensor_tensor(eq[:], eq[:], rkb, ALU.mult).then_inc(c_eq.sem, 1)
                after(dve, c_eq, b, 2)
                if prev is not None:
                    after(dve, c_idx, prev, 2)
                vec.tensor_reduce(rm[:], eq[:], AX.X, ALU.max).then_inc(c_rm.sem, 1)
                after(dve, c_rm, b, 1)
                if prev is not None:
                    after(dve, c_cnt, prev, 4)
                    after(dve, c_pos, prev, 1)
                vec.tensor_tensor(oh[:], rkb, rm[:].unsqueeze(2).to_broadcast([TP, GJ, E]), ALU.is_equal).then_inc(c_oh.sem, 1)

            def place_in_expert(b, prev):
                after(dve, c_pos, b, 1)
                vec.tensor_tensor(pp[:], psC[1][0:TP, 0:GJ * E].rearrange("p (j e) -> p j e", j=GJ), oh[:], ALU.mult).then_inc(c_pp.sem, 1)
                after(dve, c_pp, b, 1)
                if prev is not None:
                    after(dve, c_idx, prev, 3)
                vec.tensor_reduce(pos[:], pp[:], AX.X, ALU.add).then_inc(c_pp.sem, 1)

            def probability(b, prev):
                after(dve, c_le, b, 1)
                vec.tensor_reduce(sume[:], le[:], AX.X, ALU.add).then_inc(c_sume.sem, 1)
                after(dve, c_sume, b, 1)
                vec.reciprocal(rp[:], sume[:]).then_inc(c_rp.sem, 1)

            def keep_base(b, prev):
                after(dve, c_rp, b, 1)
                after(dve, c_idx, b, 1)
                ckb = ck[:, bass.ds(b * GJ, GJ)]
                vec.tensor_tensor(ckb, keep[:], rp[:], ALU.mult).then_inc(c_ck.sem, 1)
                after(dve, c_ck, b, 1)
                vec.tensor_tensor(nk[:], rp[:], ckb, ALU.subtract).then_inc(c_ck.sem, 1)
                after(dve, c_ck, b, 2)
                for j in range(GJ):
                    vec.scalar_tensor_tensor(base[:, bass.ds(b * GJ + j, 1), :].rearrange("p o c -> p (o c)"), xf[:, j, :], nk[:, j:j + 1], h2[:, j, :],
                                             ALU.mult, ALU.add).then_inc(c_base.sem, 1)

            def step(m, f, k, r):
                if k is not None:
                    key_sum(k, before(k))
                if f is not None:
                    dot3(f, before(f), 5)
                if k is not None:
                    query_norm(k, before(k))
                if m is not None:
                    split_h1(m, before(m), 0)
                if f is not None:
                    scan(f, before(f))
                    lengths(f, before(f))
                if k is not None:
                    take_ctx(k, before(k))
                if f is not None:
                    clip(f, before(f))
                if m is not None:
                    split_h1(m, before(m), 1)
                    bias2(m, before(m), 0)
                if k is not None:
                    take_m(k, before(k))
                if r is not None:
                    probability(r, before(r))
                    keep_base(r, before(r))
                if m is not None:
                    dot3(m, before(m), 0)
                if f is not None:
                    moments1(f, before(f))
                if k is not None:
                    out_norm(k, before(k))
                if m is not None:
                    bias2(m, before(m), 1)
                if f is not None:
                    normal1(f, before(f))
                if m is not None:
                    dot3(m, before(m), 1)
                    bias2(m, before(m), 2)
                if f is not None:
                    xn_lo(f, before(f))
                if k is not None:
                    residual(k, before(k))
                    moments2(k, before(k))
                if f is not None:
                    keep_h(f, before(f))
                if m is not None:
                    dot3(m, before(m), 2)
                    bias2(m, before(m), 3)
                if f is not None:
                    query_max(f, before(f), 0)
                if k is not None:
                    normal2(k, before(k))
                if f is not None:
                    query_max(f, before(f), 1)
                    query_max(f, before(f), 2)
                if m is not None:
                    dot3(m, before(m), 3)
                if f is not None:
                    key_max(f, before(f), 0)
                if k is not None:
                    route(k, before(k))
                if f is not None:
                    for p in range(1, PAIRS):
                        key_max(f, before(f), p)
                if m is not None:
                    bias2(m, before(m), 4)
                    x_lo_next(m)
                    bias2(m, before(m), 5)
                if k is not None:
                    place_in_expert(k, before(k))
                if f is not None:
                    query_sum(f, before(f))
                if m is not None:
                    dot3(m, before(m), 4)

            def x_lo_next(m):
                if has_next(m):
                    for i in range(2):
                        x_lo(m + 1, m, i)

            for i in range(2):
                x_lo(0, None, i)
            pipeline(dve, step)

            dve.wait_ge(s_eb, 16)
            for e in range(E):
                dve.wait_ge(s_ey, e + 1)
                vec.tensor_tensor(ya[:, e, :], psB[e % 2][0:SA, 0:C], ebr[0:SA, e, :], ALU.add)
                vec.tensor_tensor(yb[:, e, :], psB[e % 2][0:SB, C:2 * C], ebr[0:SB, e, :], ALU.add).then_inc(s_eyb, 1)
            for i in range(B * GJ):
                dve.wait_ge(s_yg[i % 4], 16 * (i // 4 + 1))
                if i >= 2 * GJ and i % GJ == 0:
                    dve.wait_ge(s_out[i // GJ % 2], 16 * (i // (2 * GJ)))
                vec.scalar_tensor_tensor(res[:, i % (2 * GJ), :], yg[i % 4], ck[:, i:i + 1], base[:, i, :],
                                         ALU.mult, ALU.add).then_inc(s_res, 1)


N_CONST = 18
N_W2 = 13
N_PREP = 8

_INS = ['x', 'L0_tok_W1', 'L0_tok_b1', 'L0_tok_W2', 'L0_tok_b2', 'L0_tok_W3', 'L0_tok_b3', 'L0_attn_norm_w',
        'L0_attn_w_qkv', 'L0_attn_mem_kv', 'L0_attn_w_out', 'L0_attn_b_out', 'L0_attn_out_norm_w',
        'L0_ffn_switch_w', 'L0_ffn_switch_b', 'L0_ffn_expert_w', 'L0_ffn_expert_b']


def kernel(**inputs):
    import concourse.bacc as _bacc
    from concourse.bass_utils import run_bass_kernel_spmd as _run

    nc = _bacc.Bacc("TRN2", target_bir_lowering=False, num_devices=1)
    arrays, args = {}, []
    for name in _INS:
        a = np.ascontiguousarray(inputs[name])
        arrays[f"in_{name}"] = a
        args.append(nc.dram_tensor(f"in_{name}", a.shape, mybir.dt.from_np(a.dtype), kind="ExternalInput").ap())
    rows, tokens, channels = inputs["x"].shape
    args.append(nc.dram_tensor("out_0", (rows, tokens // 2, channels), F32, kind="ExternalOutput").ap())
    audio_tower(nc, *args)
    r = _run(nc, [arrays], core_ids=[0])
    return r.results[0]["out_0"]
```

```python
from contextlib import ExitStack

import numpy as np

import concourse.bass as bass
from concourse import mybir

F32 = mybir.dt.float32
F32R = mybir.dt.float32r
BF16 = mybir.dt.bfloat16
U32 = mybir.dt.uint32
I32 = mybir.dt.int32
ALU = mybir.AluOpType
ACT = mybir.ActivationFunctionType
AX = mybir.AxisListType


class Counted:

    def __init__(self, sem, per):
        self.sem, self.per = sem, per

    def count(self, b, k):
        return b * self.per + k


def after(eng, counted, b, k):
    eng.wait_ge(counted.sem, counted.count(b, k))


def audio_tower(nc, x, W1, b1, W2, b2, W3, b3, norm_w, w_qkv, mem_kv, w_out, b_out, out_norm_w,
                switch_w, switch_b, expert_w, expert_b, out):
    B, T, C = x.shape
    H = W1.shape[1]
    G = T // 2
    TP = 125
    TJ, GJ = T // TP, G // TP
    HK = H // 128
    HALF = T // 2
    HP = HALF + 1
    HEADS, D = mem_kv.shape[1], mem_kv.shape[2]
    NM = mem_kv.shape[3]
    HID = HEADS * D
    PAIRS = HID // 128
    NK = G + NM
    E = switch_w.shape[0]
    CAP = int(1.2 * B * G / E)
    N = (B - 1) * G
    SLOTS = E * CAP
    SA = (CAP + 1) // 2
    SB = CAP - SA
    EPS = 1e-5
    ROOT_C = float(C) ** 0.5
    LAST = B - 1
    GATHERED_FIRST = 3

    with ExitStack() as ctx:
        def sb(name, shape, dt=F32):
            return ctx.enter_context(nc.sbuf_tensor(name, shape, dt))

        def counted(name, per):
            return Counted(ctx.enter_context(nc.semaphore(name)), per)

        def sem(name):
            return ctx.enter_context(nc.semaphore(name))

        slot_x = nc.dram_tensor("slot_x", [SLOTS + N, C], F32, kind="Internal").ap()
        slot_y = nc.dram_tensor("slot_y", [SLOTS, C], F32, kind="Internal").ap()

        psA = [ctx.enter_context(nc.psum_tensor(f"psA{i}", [128, 512], F32)) for i in range(2)]
        psB = [ctx.enter_context(nc.psum_tensor(f"psB{i}", [128, 512], F32)) for i in range(2)]
        psC = [ctx.enter_context(nc.psum_tensor(f"psC{i}", [128, 512], F32)) for i in range(4)]

        ident = sb("ident", [128, 128])
        ones = sb("ones", [128, 128])
        tri = sb("tri", [TP, TP])
        ones_b = sb("ones_b", [TP, TP], BF16)
        tri_b = sb("tri_b", [TP, TP], BF16)
        neg_g = sb("neg_g", [TP, G])
        half = sb("half", [TP, 2, GJ])
        m_half, p_half = half[:, 0], half[:, 1]
        euler = sb("euler", [TP, TJ])
        rank = sb("rank", [TP, E])
        tok = sb("tok", [TP, GJ])
        rank_e = sb("rank_e", [E, 1])

        W1f = sb("W1f", [C, H]); W1h = sb("W1h", [C, H], F32R); W1l = sb("W1l", [C, H], F32R)
        W2h = sb("W2h", [128, HK, H], F32R); W2l = sb("W2l", [128, HK, H], F32R)
        b1c = sb("b1c", [128, HK])
        b2r = sb("b2r", [TP, H])
        W3r = sb("W3r", [TP, H])
        b3r = sb("b3r", [TP, 1])
        nwc = sb("nwc", [C, 1])
        Wqh = sb("Wqh", [C, 3 * HID], F32R); Wql = sb("Wql", [C, 3 * HID], F32R)
        mkv = sb("mkv", [128, 2, PAIRS, NM])
        mvT = sb("mvT", [NM, HID])
        wo = sb("wo", [128, PAIRS, C])
        bor = sb("bor", [TP, C])
        onr = sb("onr", [TP, C])
        swf = sb("swf", [E, C]); swT = sb("swT", [C, E])
        swbr = sb("swbr", [TP, E])
        ewf = sb("ewf", [128, E, C]); ewT = sb("ewT", [C, E, 128])
        ebr = sb("ebr", [128, E, C])
        ebs = sb("ebs", [E, C])
        zero = ebr[0:120, 0:15, :]

        xt = sb("xt", [TP, TJ, C])
        xs = sb("xs", [TP, TJ, C])
        dx = sb("dx", [TP, TJ, C])
        xTh = sb("xTh", [C, 2, HP], F32R); xTl = sb("xTl", [C, 2, HP], F32R)
        h1 = sb("h1", [128, HK, 2, HP])
        h1h = sb("h1h", [128, HK, 2, HP], F32R); h1l = sb("h1l", [128, HK, 2, HP], F32R)
        h2b = sb("h2b", [TP, 4, H])
        z = sb("z", [TP, TJ])

        sg = sb("sg", [TP, 3, TJ])
        sx = sb("sx", [TP, TJ + 1])
        pre = sb("pre", [TP, TJ + 1])
        rt = sb("rt", [TP, 1])
        cs = sb("cs", [TP, TJ])
        A = sb("A", [TP, TJ, G])

        h = sb("h", [TP, GJ, C])
        hres = sb("hres", [TP, GJ, C])
        st = sb("st", [TP, GJ, 6])
        mv1 = sb("mv1", [TP, GJ, 2])
        rs1 = sb("rs1", [TP, 8, GJ])
        xn = sb("xn", [TP, GJ, C])
        xh = sb("xh", [C, G + 1], F32R); xl = sb("xl", [C, G + 1], F32R)
        v = sb("v", [TP, GJ, HID])
        qm = sb("qm", [TP, GJ, HEADS])
        qa = sb("qa", [128, GJ, HID])
        q = qa[0:TP]
        Wqf = qa[:].rearrange("p j d -> p (j d)")
        qsum = sb("qsum", [TP, GJ * HEADS])
        rq = sb("rq", [TP, GJ * HEADS])
        nkm = sb("nkm", [128, PAIRS])
        ek = sb("ek", [128, PAIRS, NK])
        ksum = sb("ksum", [128, PAIRS])
        rk = sb("rk", [128, PAIRS])
        kT = sb("kT", [TP, GJ, HID])
        kTm = sb("kTm", [NM, HID])
        qT = sb("qT", [128, GJ, PAIRS, TP])
        cbd = sb("cbd", [128, PAIRS, 128])
        m = sb("m", [128, PAIRS, C])
        o = sb("o", [TP, GJ, C])
        osq = sb("osq", [TP, GJ, C])
        ss = sb("ss", [TP, GJ])
        rs2 = sb("rs2", [TP, 3, GJ])
        h2 = sb("h2", [TP, GJ, C])

        st2 = sb("st2", [TP, GJ, 6])
        mv2 = sb("mv2", [TP, GJ, 2])
        rs3 = sb("rs3", [TP, 2, GJ])
        xf = sb("xf", [TP, GJ, C])
        xfT = sb("xfT", [C, G])
        lg = sb("lg", [TP, GJ, E])
        mx = sb("mx", [TP, GJ])
        eq = sb("eq", [TP, GJ, E])
        rm = sb("rm", [TP, GJ])
        oh = sb("oh", [TP, GJ, E], BF16)
        le = sb("le", [TP, GJ, E])
        sume = sb("sume", [TP, GJ])
        rp = sb("rp", [TP, GJ])
        cnt = sb("cnt", [TP, GJ + 1, E], BF16)
        pp = sb("pp", [TP, GJ, E])
        pos = sb("pos", [TP, GJ])
        keep = sb("keep", [TP, GJ])
        place = sb("place", [TP, 5, GJ])
        idx_s = sb("idx_s", [TP, GJ], U32)
        nk = sb("nk", [TP, GJ])
        basef = sb("basef", [128, B * GJ, C])
        base = basef[0:TP]
        W2f = basef[:].rearrange("p j c -> p (j c)")[:, 0:HK * H].rearrange("p (k n) -> p k n", k=HK)
        ck = sb("ck", [TP, B * GJ])
        idx_g = sb("idx_g", [TP, B * GJ], U32)

        sx_a = ewf[0:SA]
        sx_b = h2b[0:SB].rearrange("p k n -> p (k n)").rearrange("p (e c) -> p e c", e=E)
        ya = h1[0:SA].rearrange("p k i t -> p (k i t)")[:, 0:E * C].rearrange("p (e c) -> p e c", e=E)
        yb = A[0:SB].rearrange("p j g -> p (j g)")[:, 0:E * C].rearrange("p (e c) -> p e c", e=E)
        sxT = ek[:].rearrange("p a n -> p (a n)")[:, 0:4 * CAP].rearrange("p (i s) -> p i s", i=2)
        flat = [t[:].rearrange("p j c -> p (j c)") for t in (dx, xs, v)]
        yg = [flat[min(b // 2, 2)][:, (b - 2 * min(b // 2, 2)) * GJ * C:][:, 0:GJ * C].rearrange("p (j c) -> p j c", j=GJ)
              for b in range(LAST)] + [xt[:, 0:GJ, :]]
        wide = (qT[:].rearrange("p j a t -> p (j a t)"), ewf[:].rearrange("p e c -> p (e c)"),
                ebr[:].rearrange("p e c -> p (e c)"), ek[:].rearrange("p a n -> p (a n)"))
        only = [t[:, i * G:(i + 1) * G] for t in wide for i in range(t.shape[1] // G)][0:E]
        IN_QT = qT.shape[1] * qT.shape[2] * qT.shape[3] // G
        rmw = osq
        ohT = kT[0:E, 0, 0:G]

        s_w1 = sem("s_w1"); s_b1 = sem("s_b1"); s_w2 = sem("s_w2"); s_w3 = sem("s_w3")
        s_wr = sem("s_wr")
        s_ident = sem("s_ident")
        s_const = sem("s_const")
        s_csel = sem("s_csel")
        s_prep = sem("s_prep")
        s_prept = sem("s_prept")
        s_prepc = sem("s_prepc")
        s_zero = sem("s_zero"); s_zfill = sem("s_zfill"); s_eb = sem("s_eb")

        c_x = counted("c_x", 16); c_xs = counted("c_xs", 32)
        c_xt = counted("c_xt", 2); c_xth = counted("c_xth", 2); c_xtl = counted("c_xtl", 2)
        c_dx = counted("c_dx", 1)
        c_l1 = counted("c_l1", 8); c_g1 = counted("c_g1", 8); c_h1h = counted("c_h1h", 2); c_h1l = counted("c_h1l", 2)
        c_l2 = counted("c_l2", 6); c_b2 = counted("c_b2", 6); c_g2 = counted("c_g2", 6); c_z = counted("c_z", 6)
        c_nz = counted("c_nz", 1); c_sig = counted("c_sig", 1); c_s = counted("c_s", 2); c_scan = counted("c_scan", 1); c_cs = counted("c_cs", 1)
        c_rt = counted("c_rt", 1); c_csn = counted("c_csn", 1)
        c_rel = counted("c_rel", 1); c_clip = counted("c_clip", 1); c_warp = counted("c_warp", 1)
        c_h = counted("c_h", 1); c_hres = counted("c_hres", 1); c_bn = counted("c_bn", 3); c_mv = counted("c_mv", 1)
        c_var = counted("c_var", 2); c_rs1 = counted("c_rs1", 1); c_sc = counted("c_sc", 4)
        c_xn = counted("c_xn", 1); c_xnt = counted("c_xnt", 1); c_xh = counted("c_xh", 1); c_xl = counted("c_xl", 1)
        c_v = counted("c_v", 3); c_vc = counted("c_vc", 3)
        c_q = counted("c_q", 3); c_qm = counted("c_qm", 3); c_qs = counted("c_qs", 3)
        c_k = counted("c_k", 4); c_km = counted("c_km", 4); c_ke = counted("c_ke", 4)
        c_qe = counted("c_qe", 3); c_qsum = counted("c_qsum", 1); c_rq = counted("c_rq", 1); c_qn = counted("c_qn", 1)
        c_kt = counted("c_kt", 4); c_kta = counted("c_kta", 4)
        c_qt = counted("c_qt", 3); c_qtc = counted("c_qtc", 3)
        c_ctx = counted("c_ctx", 1); c_cba = counted("c_cba", 1); c_cbd = counted("c_cbd", 1)
        c_m = counted("c_m", 1); c_rk = counted("c_rk", 1); c_ms = counted("c_ms", 1)
        c_fin = counted("c_fin", 1); c_o = counted("c_o", 1); c_ss = counted("c_ss", 3); c_rs2 = counted("c_rs2", 1); c_ro = counted("c_ro", 2)
        c_on = counted("c_on", 3); c_h2 = counted("c_h2", 1)
        c_bn2 = counted("c_bn2", 3); c_mv2 = counted("c_mv2", 1); c_var2 = counted("c_var2", 1); c_rs3 = counted("c_rs3", 1); c_xf = counted("c_xf", 1)
        c_xft = counted("c_xft", 1); c_xfc = counted("c_xfc", 1); c_lg = counted("c_lg", 1); c_lb = counted("c_lb", 1)
        c_mx = counted("c_mx", 1); c_eq = counted("c_eq", 2); c_rm = counted("c_rm", 1); c_oh = counted("c_oh", 1)
        c_ls = counted("c_ls", 1); c_le = counted("c_le", 1); c_sume = counted("c_sume", 1); c_rp = counted("c_rp", 1)
        c_cnt = counted("c_cnt", 4); c_pos = counted("c_pos", 1); c_pp = counted("c_pp", 2)
        c_keep = counted("c_keep", 1); c_idx = counted("c_idx", 9); c_sct = counted("c_sct", 48)
        c_ck = counted("c_ck", 2); c_base = counted("c_base", 3)

        s_sx = [sem(f"s_sx{i}") for i in range(2)]
        s_ext = sem("s_ext"); s_exc = sem("s_exc"); s_ey = sem("s_ey"); s_eyb = sem("s_eyb")
        s_yst = sem("s_yst"); s_yg = [sem(f"s_yg{b}") for b in range(LAST)]
        s_res = sem("s_res"); s_out = sem("s_out")
        s_rmw = sem("s_rmw"); s_rmt = sem("s_rmt"); s_only = sem("s_only"); s_dense = sem("s_dense")

        ROW_ORDER = list(range(GATHERED_FIRST)) + [LAST] + list(range(GATHERED_FIRST, LAST))

        block = ctx.enter_context(nc.Block())

        def bank_xf(b):
            return psC[2] if row_is(b, LAST) else psA[1]

        def bank_lg(b):
            return psC[3] if row_is(b, LAST) else psA[0]

        def bank_pos(b):
            return psB[1] if row_is(b, LAST - 1) else psC[1]

        def row_is(b, row):
            return b == row

        def ends(b):
            return row_is(b, LAST - 1) or row_is(b, LAST)

        def bank_warp(b):
            return psA[0] if row_is(b, LAST) else psC[2]

        def bank_xn(b):
            return psB[1] if row_is(b, LAST) else psC[1]

        def bank_vq(b, j):
            return psB[0] if row_is(b, LAST) and j == 2 else psC[(2 + j) % 4]

        def h2_slot(j):
            return j % 4

        def h2_before(j):
            return j + 4 if j < 2 else j

        def half_cols(j):
            c = (j % GJ) * TP
            return j // GJ, slice(c, c + TP)

        def before(b):
            return None if b == 0 else b - 1

        def has_next(m):
            return m < LAST

        def pipeline(eng, step, ending, setup):
            def rows(i):
                return [b if 0 <= b < B else None for b in (i + 1, i, i - 1, i - 2)]

            step(*rows(-1))
            setup()
            for i in range(2):
                step(*rows(i))
            for i in range(2, B - 2):
                step(i + 1, i, i - 1, i - 2)
            step(*rows(B - 2))
            ending(LAST, LAST - 1, LAST - 2)
            ending(None, LAST, LAST - 1)
            ending(None, None, LAST)

        @block.sync
        def _(sp):
            def load_tokens(b, prev):
                if prev is not None:
                    after(sp, c_xt, prev, 2)
                    after(sp, c_dx, prev, 1)
                sp.dma_start(xt[:], x[bass.ds(b, 1)].rearrange("o (j p) c -> p (o j) c", p=TP)).then_inc(c_x.sem, 16)

            def load_next_tokens(b, prev):
                if prev is not None:
                    after(sp, c_dx, prev, 1)
                sp.dma_start(xs[:, 0:TJ - 1, :],
                             x[bass.ds(b, 1), 1:1 + (TJ - 1) * TP].rearrange("o (j p) c -> p (o j) c", p=TP)).then_inc(c_xs.sem, 16)
                sp.dma_start(xs[0:TP - 1, TJ - 1, :],
                             x[bass.ds(b, 1), 1 + (TJ - 1) * TP:T].rearrange("o p c -> p (o c)")).then_inc(c_xs.sem, 16)

            sp.dma_start(W1f[:], W1).then_inc(s_w1, 16)
            load_tokens(0, None)
            sp.dma_start(b1c[:], b1.rearrange("(k p) -> p k", p=128), allow_slow_non_contiguous=True).then_inc(s_b1, 16)
            sp.dma_start(W2f, W2.rearrange("(k p) n -> p k n", p=128)).then_inc(s_w2, 16)
            for dst, src in ((b2r[:], b2.partition_broadcast(TP)), (W3r[:], W3.rearrange("h o -> (o h)").partition_broadcast(TP))):
                sp.dma_start(dst, src).then_inc(s_w3, 16)
            sp.wait_ge(s_zero, 1)
            load_next_tokens(0, None)
            for dst, src in ((b3r[:], b3.partition_broadcast(TP)),
                             (nwc[:], norm_w.rearrange("a b c -> c (a b)")), (Wqf, w_qkv),
                             (mkv[:, 0], mem_kv[0].rearrange("(p a) d n -> (a d) p n", a=2)),
                             (mkv[:, 1], mem_kv[1].rearrange("(p a) d n -> (a d) p n", a=2)),
                             (wo[:], w_out.rearrange("(p k) c -> k p c", k=128)),
                             (bor[:], b_out.partition_broadcast(TP)),
                             (onr[:], out_norm_w.rearrange("a b c -> (a b c)").partition_broadcast(TP)),
                             (ebs[:], expert_b), (swf[:], switch_w), (swbr[:], switch_b.partition_broadcast(TP)),
                             (ewf[:], expert_w.rearrange("e f d -> f e d"))):
                sp.dma_start(dst, src, allow_slow_non_contiguous=True).then_inc(s_wr, 16)
            sp.wait_ge(s_zero, 2)
            for i in range(2):
                rows = SLOTS // 2
                sp.dma_start(slot_x[i * rows:(i + 1) * rows].rearrange("(p r) c -> p r c", r=15), zero).then_inc(s_zfill, 16)
            load_tokens(1, 0)
            load_next_tokens(1, 0)
            sp.wait_ge(s_zfill, 32)
            sp.dma_start(ebr[:].rearrange("p e c -> p (e c)"),
                         expert_b.rearrange("e c -> (e c)").partition_broadcast(128)).then_inc(s_eb, 16)
            for b in range(2, B):
                load_tokens(b, b - 1)
                load_next_tokens(b, b - 1)

            after(sp, c_sct, LAST - 1, 48)
            after(sp, c_z, LAST, TJ)
            for i in range(2):
                part = slot_x[i * 8 * CAP:(i + 1) * 8 * CAP].rearrange("(e s) c -> s e c", s=CAP)
                sp.dma_start(sx_a[:, 8 * i:8 * i + 8, :], part[0:SA]).then_inc(s_sx[i], 16)
                sp.dma_start(sx_b[:, 8 * i:8 * i + 8, :], part[SA:CAP]).then_inc(s_sx[i], 16)
            for i in range(4):
                sp.wait_ge(s_eyb, 2 * (i + 1))
                part = slot_y[i * 4 * CAP:(i + 1) * 4 * CAP].rearrange("(e s) c -> s e c", s=CAP)
                sp.dma_start(part[0:SA], ya[:, 4 * i:4 * i + 4, :]).then_inc(s_yst, 16)
                sp.dma_start(part[SA:CAP], yb[:, 4 * i:4 * i + 4, :]).then_inc(s_yst, 16)
            for n, b in enumerate(ROW_ORDER):
                sp.wait_ge(s_res, n + 1)
                sp.dma_start(out[b].rearrange("(j p) c -> p j c", p=TP), yg[b]).then_inc(s_out, 16)
            sp.wait_ge(s_out, 16 * B)

        @block.gpsimd
        def _(pool):
            pool.memset(ident[:], 0.0).then_inc(s_csel, 1)
            pool.wait_ge(s_csel, 1)
            pool.affine_select(out=ident[:], in_=ident[:], compare_op=ALU.not_equal, fill=1.0, base=0,
                               pattern=[[-1, 128]], channel_multiplier=1).then_inc(s_ident, 1)
            pool.memset(xTh[:, :, HALF:HP].bitcast(F32), 0.0).then_inc(s_const, 1)
            pool.memset(xTl[:, :, HALF:HP].bitcast(F32), 0.0).then_inc(s_const, 1)
            pool.memset(xs[:, TJ - 1, :], 0.0).then_inc(s_zero, 1)
            pool.memset(ebr[:], 0.0).then_inc(s_zero, 1)
            pool.memset(ones[:], 1.0).then_inc(s_csel, 1)
            pool.memset(ones_b[:], 1.0).then_inc(s_csel, 1)
            pool.wait_ge(s_csel, 3)
            pool.affine_select(out=tri[:], in_=ones[0:TP, 0:TP], compare_op=ALU.is_ge, fill=0.0, base=0,
                               pattern=[[1, TP]], channel_multiplier=-1).then_inc(s_const, 1)
            pool.affine_select(out=tri_b[:], in_=ones_b[:], compare_op=ALU.is_ge, fill=0.0, base=0,
                               pattern=[[1, TP]], channel_multiplier=-1).then_inc(s_const, 1)
            pool.iota(neg_g[:], pattern=[[-1, G]], base=0, channel_multiplier=0,
                      allow_small_or_imprecise_dtypes=True).then_inc(s_const, 1)
            pool.iota(rank[:], pattern=[[-1, E]], base=E, channel_multiplier=0,
                      allow_small_or_imprecise_dtypes=True).then_inc(s_const, 1)
            pool.iota(tok[:], pattern=[[TP, GJ]], base=SLOTS, channel_multiplier=1,
                      allow_small_or_imprecise_dtypes=True).then_inc(s_const, 1)
            pool.iota(rank_e[:], pattern=[[0, 1]], base=E, channel_multiplier=-1,
                      allow_small_or_imprecise_dtypes=True).then_inc(s_const, 1)
            pool.memset(p_half, 0.5).then_inc(s_const, 1)
            pool.memset(m_half, -0.5).then_inc(s_const, 1)
            pool.memset(euler[:], float(np.e)).then_inc(s_const, 1)
            pool.memset(sx[:], 0.0).then_inc(s_const, 1)
            pool.memset(pre[:], 0.0).then_inc(s_const, 1)
            pool.memset(cbd[:], 0.0).then_inc(s_const, 1)
            pool.memset(cnt[:], 0.0).then_inc(s_const, 1)
            pool.memset(xh[:, G:G + 1].bitcast(F32), 0.0).then_inc(s_const, 1)
            pool.memset(xl[:, G:G + 1].bitcast(F32), 0.0).then_inc(s_const, 1)
            pool.wait_ge(s_const, N_CONST)

            def differences(b, prev):
                after(pool, c_x, b, 16)
                after(pool, c_xs, b, 32)
                if prev is not None:
                    after(pool, c_warp, prev, 1)
                pool.tensor_tensor(dx[:], xt[:], xs[:], ALU.subtract).then_inc(c_dx.sem, 1)

            def setup():
                pool.wait_ge(s_const, N_CONST)

            def sigmoid_pow(b, prev):
                after(pool, c_nz, b, 1)
                if prev is not None:
                    after(pool, c_s, prev, 1)
                pool.tensor_tensor(sg[:, 1], euler[:], sg[:, 0], ALU.pow).then_inc(c_sig.sem, 1)

            def norm1(b, prev):
                after(pool, c_var, b, 2)
                if prev is not None:
                    after(pool, c_sc, prev, 4)
                pool.tensor_tensor(rs1[:, 2:4], rs1[:, 0:2], half[:], ALU.pow).then_inc(c_rs1.sem, 1)

            def norm2(b, prev):
                after(pool, c_ss, b, 3)
                if prev is not None:
                    after(pool, c_ro, prev, 1)
                pool.tensor_tensor(rs2[:, 0], ss[:], p_half, ALU.pow).then_inc(c_rs2.sem, 1)

            def norm3(b, prev):
                after(pool, c_var2, b, 1)
                if prev is not None:
                    after(pool, c_xf, prev, 1)
                pool.tensor_tensor(rs3[:, 1], rs3[:, 0], m_half, ALU.pow).then_inc(c_rs3.sem, 1)

            def counts(b, prev):
                if prev is not None:
                    after(pool, c_cnt, prev, 4)
                    after(pool, c_pos, prev, 1)
                pool.tensor_copy(cnt[:, 0, :], cnt[:, GJ, :]).then_inc(c_cnt.sem, 1)
                after(pool, c_oh, b, 1)
                for j in range(GJ):
                    after(pool, c_cnt, b, j + 1)
                    pool.tensor_tensor(cnt[:, j + 1, :], cnt[:, j, :], oh[:, j, :], ALU.add).then_inc(c_cnt.sem, 1)

            def scatter(b, prev):
                pool.wait_ge(s_zfill, 32)
                after(pool, c_pp, b, 2)
                after(pool, c_rm, b, 1)
                if prev is not None:
                    after(pool, c_sct, prev, 48)
                    after(pool, c_idx, prev, 9)
                after(pool, c_keep, b, 1)
                pool.tensor_scalar(place[:, 0], rm[:], -float(CAP), float(SLOTS - 1), ALU.mult, ALU.add).then_inc(c_idx.sem, 1)
                after(pool, c_idx, b, 1)
                pool.tensor_tensor(place[:, 1], place[:, 0], pos[:], ALU.add).then_inc(c_idx.sem, 1)
                after(pool, c_idx, b, 2)
                pool.tensor_tensor(place[:, 2], place[:, 1], tok[:], ALU.subtract).then_inc(c_idx.sem, 1)
                after(pool, c_idx, b, 3)
                pool.tensor_tensor(place[:, 3], place[:, 2], keep[:], ALU.mult).then_inc(c_idx.sem, 1)
                after(pool, c_idx, b, 4)
                pool.tensor_tensor(place[:, 4], place[:, 3], tok[:], ALU.add).then_inc(c_idx.sem, 1)
                after(pool, c_idx, b, 5)
                pool.tensor_copy(idx_s[:], place[:, 4]).then_inc(c_idx.sem, 1)
                pool.tensor_scalar(place[:, 2], place[:, 4], float(SLOTS - 1), None, ALU.min).then_inc(c_idx.sem, 1)
                pool.tensor_scalar(tok[:], tok[:], float(G), None, ALU.add).then_inc(c_idx.sem, 1)
                after(pool, c_idx, b, 8)
                pool.tensor_copy(idx_g[:, bass.ds(b * GJ, GJ)], place[:, 2]).then_inc(c_idx.sem, 1)
                for j in range(GJ):
                    pool.indirect_dma_start(out=slot_x, out_offset=bass.IndirectOffsetOnAxis(ap=idx_s[:, j:j + 1], axis=0),
                                            in_=xf[:, j, :], in_offset=None,
                                            bounds_check=SLOTS + N - 1, oob_is_err=True).then_inc(c_sct.sem, 16)

            def step(m, f, k, r):
                if f is not None:
                    sigmoid_pow(f, before(f))
                if r is not None:
                    scatter(r, before(r))
                if f is not None:
                    norm1(f, before(f))
                if k is not None:
                    norm2(k, before(k))
                if m is not None:
                    differences(m, before(m))
                if k is not None:
                    norm3(k, before(k))
                    counts(k, before(k))

            def ending(f, k, r):
                if f is not None:
                    sigmoid_pow(f, before(f))
                if r is not None and r < LAST:
                    scatter(r, before(r))
                if f is not None:
                    norm1(f, before(f))
                if k is not None:
                    norm2(k, before(k))
                    norm3(k, before(k))
                    counts(k, before(k))

            pipeline(pool, step, ending, setup)

            after(pool, c_idx, LAST - 1, 9)
            after(pool, c_warp, LAST, 1)
            after(pool, c_ctx, LAST, 1)
            pool.wait_ge(s_yst, 128)
            for b in range(LAST):
                for j in range(GJ):
                    pool.indirect_dma_start(out=yg[b][:, j, :], out_offset=None, in_=slot_y,
                                            in_offset=bass.IndirectOffsetOnAxis(ap=idx_g[:, b * GJ + j:b * GJ + j + 1], axis=0),
                                            bounds_check=SLOTS - 1, oob_is_err=True).then_inc(s_yg[b], 16)

        @block.scalar
        def _(act):
            def copy(out_, in_):
                return nc.scalar.activation(out_, in_, ACT.Copy)

            def x_hi(b, prev, i):
                after(act, c_xt, b, i + 1)
                if prev is not None:
                    after(act, c_l1, prev, 8)
                copy(xTh[:, i, 0:HALF], psA[i][:, 0:HALF]).then_inc(c_xth.sem, 1)

            def gelu1(b, prev, i, k):
                n = i * HK + k
                after(act, c_l1, b, n + 1)
                if prev is not None and k == 0:
                    after(act, c_h1l, prev, i + 1)
                nc.scalar.activation(h1[:, k, i, :], psA[n % 2][:, 0:HP], ACT.Gelu, bias=b1c[:, k:k + 1]).then_inc(c_g1.sem, 1)

            def gelu2(b, j):
                after(act, c_b2, b, j + 1)
                slot = h2b[:, h2_slot(j), :]
                nc.scalar.activation(slot, slot, ACT.Gelu).then_inc(c_g2.sem, 1)

            def take_h(b, prev):
                after(act, c_warp, b, 1)
                if prev is not None:
                    after(act, c_xn, prev, 1)
                    after(act, c_hres, prev, 1)
                copy(h[:].rearrange("p j c -> p (j c)"), bank_warp(b)[0:TP, 0:GJ * C]).then_inc(c_h.sem, 1)

            def xn_hi(b, prev):
                after(act, c_xnt, b, 1)
                if prev is not None:
                    after(act, c_k, prev, 4)
                copy(xh[:, 0:G], bank_xn(b)[:, 0:G]).then_inc(c_xh.sem, 1)

            def take_v(b, prev, j):
                after(act, c_v, b, j + 1)
                if prev is not None:
                    after(act, c_ctx, prev, 1)
                copy(v[:, j, :], bank_vq(b, j)[0:TP, :]).then_inc(c_vc.sem, 1)

            def query_exp(b, j):
                after(act, c_qs, b, j + 1)
                nc.scalar.activation(q[:, j, :], q[:, j, :], ACT.Exp).then_inc(c_qe.sem, 1)

            def key_exp(b, prev, p):
                after(act, c_km, b, p + 1)
                if prev is not None and p == 0:
                    after(act, c_kt, prev, 4)
                    after(act, c_rk, prev, 1)
                nc.scalar.activation(ek[:, p, :], psC[(1 + p) % 4][:, 0:NK], ACT.Exp, bias=nkm[:, p:p + 1],
                                     accum_out=ksum[:, p:p + 1]).then_inc(c_ke.sem, 1)

            def route_exp(b, prev):
                after(act, c_ls, b, 1)
                nc.scalar.activation(le[:].rearrange("p j e -> p (j e)"), le[:].rearrange("p j e -> p (j e)"),
                                     ACT.Exp).then_inc(c_le.sem, 1)

            def take_kt(b, prev, j):
                after(act, c_kt, b, j + 1)
                if prev is not None:
                    after(act, c_ctx, prev, 1)
                if j < GJ:
                    copy(kT[:, j, :], psC[j][0:TP, :]).then_inc(c_kta.sem, 1)
                else:
                    copy(kTm[:], psC[j][0:NM, :]).then_inc(c_kta.sem, 1)

            def take_qt(b, prev, j):
                after(act, c_qt, b, j + 1)
                if prev is not None:
                    after(act, c_fin, prev, 1)
                copy(qT[:, j, :, :].rearrange("p a t -> p (a t)"), psC[j][:, 0:PAIRS * TP]).then_inc(c_qtc.sem, 1)

            def take_ctx(b, prev):
                after(act, c_ctx, b, 1)
                if prev is not None:
                    after(act, c_m, prev, 1)
                copy(cbd[D:128, :, D:128], psC[0][D:128, :].rearrange("p (a d) -> p a d", a=PAIRS)[:, :, D:128]).then_inc(c_cba.sem, 1)
                if ends(b):
                    copy(cbd[0:D, :, 0:D], psC[0][0:D, :].rearrange("p (a d) -> p a d", a=PAIRS)[:, :, 0:D]).then_inc(c_cbd.sem, 1)

            def take_xft(b, prev):
                after(act, c_xft, b, 1)
                if prev is not None:
                    after(act, c_lg, prev, 1)
                copy(xfT[:], bank_xf(b)[:, 0:G]).then_inc(c_xfc.sem, 1)

            def setup():
                act.wait_ge(s_prept, 1)
                copy(mvT[:], psC[0][0:NM, 0:HID]).then_inc(s_prepc, 1)
                act.wait_ge(s_prept, 2)
                copy(swT[:], psC[1][:, 0:E]).then_inc(s_prepc, 1)
                for i in range(4):
                    act.wait_ge(s_prept, 3 + i)
                    copy(ewT[:, 4 * i:4 * i + 4, :], psC[2 + i % 2][:].rearrange("p (e f) -> p e f", e=4)).then_inc(s_prepc, 1)

            def x_hi_next(m):
                if has_next(m):
                    for i in range(2):
                        x_hi(m + 1, m, i)

            def take_tokens(p):
                act.wait_ge(s_ext, p + 1)
                if p == 0:
                    after(act, c_kt, LAST, 4)
                if p >= 2:
                    act.wait_ge(s_ey, p - 1)
                copy(sxT[:, p % 2, :], psA[p % 2][:, 0:2 * CAP]).then_inc(s_exc, 1)

            def step(m, f, k, r):
                if m is not None:
                    gelu1(m, before(m), 0, 0)
                    gelu1(m, before(m), 0, 1)
                if f is not None:
                    gelu2(f, 5)
                if k is not None:
                    take_kt(k, before(k), 0)
                if m is not None:
                    gelu1(m, before(m), 0, 2)
                if k is not None:
                    take_kt(k, before(k), 1)
                if m is not None:
                    gelu1(m, before(m), 0, 3)
                if k is not None:
                    take_kt(k, before(k), 2)
                if m is not None:
                    gelu1(m, before(m), 1, 0)
                if k is not None:
                    take_kt(k, before(k), 3)
                if m is not None:
                    gelu1(m, before(m), 1, 1)
                if k is not None:
                    for j in range(GJ):
                        take_qt(k, before(k), j)
                    take_ctx(k, before(k))
                if m is not None:
                    gelu1(m, before(m), 1, 2)
                    gelu1(m, before(m), 1, 3)
                    gelu2(m, 0)
                if f is not None:
                    take_h(f, before(f))
                if m is not None:
                    gelu2(m, 1)
                    gelu2(m, 2)
                if f is not None:
                    xn_hi(f, before(f))
                    for j in range(GJ):
                        take_v(f, before(f), j)
                if m is not None:
                    gelu2(m, 3)
                if f is not None:
                    query_exp(f, 0)
                if k is not None:
                    take_xft(k, before(k))
                if f is not None:
                    query_exp(f, 1)
                    query_exp(f, 2)
                    for p in range(3):
                        key_exp(f, before(f), p)
                if m is not None:
                    x_hi_next(m)
                if f is not None:
                    key_exp(f, before(f), 3)
                if k is not None:
                    route_exp(k, before(k))
                if m is not None:
                    gelu2(m, 4)

            def ending(f, k, r):
                if f is not None:
                    gelu2(f, 5)
                if k is not None:
                    for j in range(4):
                        take_kt(k, before(k), j)
                    take_ctx(k, before(k))
                if f is not None:
                    take_h(f, before(f))
                if k == LAST:
                    take_tokens(0)
                    take_tokens(1)
                if k is not None:
                    for j in range(GJ):
                        take_qt(k, before(k), j)
                if k == LAST:
                    take_tokens(2)
                    take_tokens(3)
                if f is not None:
                    xn_hi(f, before(f))
                    for j in range(GJ):
                        take_v(f, before(f), j)
                if k == LAST:
                    for p in range(4, E // 2):
                        take_tokens(p)
                if k is not None:
                    take_xft(k, before(k))
                if f is not None:
                    for j in range(GJ):
                        query_exp(f, j)
                    for p in range(PAIRS):
                        key_exp(f, before(f), p)
                if k is not None:
                    route_exp(k, before(k))

            for i in range(2):
                x_hi(0, None, i)
            act.wait_ge(s_b1, 16)
            pipeline(act, step, ending, setup)

        @block.tensor
        def _(pe):
            mm = nc.tensor.matmul

            def split(ps, wh, wl, mh, ml):
                mm(ps, wh, ml, start=True, stop=False)
                mm(ps, wl, mh, start=False, stop=False)
                return mm(ps, wh, mh, start=False, stop=True)

            def x_transposed(b, prev, i, k):
                after(pe, c_x, b, 16)
                if prev is not None:
                    after(pe, c_g1, prev, 7 + i)
                if k is not None:
                    after(pe, c_lb if i == 0 else c_xfc, k, 1)
                for j in range(GJ):
                    last = nc.tensor.transpose(psA[i][:, j * TP:(j + 1) * TP], xt[:, GJ * i + j, :], ident[0:TP, 0:TP])
                last.then_inc(c_xt.sem, 1)

            def layer1(b, prev, i, k):
                n = i * HK + k
                after(pe, c_xtl, b, i + 1)
                if n < 2:
                    after(pe, c_xtl, b, n + 1)
                else:
                    after(pe, c_g1, b, n - 1)
                w = slice(k * 128, (k + 1) * 128)
                split(psA[n % 2][:, 0:HP], W1h[:, w], W1l[:, w], xTh[:, i, :], xTl[:, i, :]).then_inc(c_l1.sem, 1)

            def layer2(b, prev, j):
                i, cols = half_cols(j)
                after(pe, c_h1l, b, i + 1)
                if prev is None and j == 0:
                    pe.wait_ge(s_prep, 4)
                if j >= 2:
                    after(pe, c_b2, b, j - 1)
                elif prev is not None:
                    after(pe, c_b2, prev, TJ - 1 + j)
                ps = psB[j % 2][0:TP, :]
                for k in range(HK):
                    hi, lo = h1h[:, k, i, cols], h1l[:, k, i, cols]
                    mm(ps, lo, W2h[:, k, :], start=k == 0, stop=False)
                    mm(ps, hi, W2l[:, k, :], start=False, stop=False)
                    last = mm(ps, hi, W2h[:, k, :], start=False, stop=k == HK - 1)
                last.then_inc(c_l2.sem, 1)

            def sums(b, prev):
                if prev is None:
                    pe.wait_ge(s_prepc, 6)
                after(pe, c_s, b, 2)
                after(pe, c_scan, b, 1)
                if prev is not None:
                    after(pe, c_kta, prev, 4)
                mm(psC[3][0:TP, 0:TJ + 1], tri[:], sx[:], start=True, stop=False)
                mm(psC[3][0:TP, 0:TJ + 1], ones[0:TP, 0:TP], pre[:], start=False, stop=True).then_inc(c_cs.sem, 1)

            def warp(b, prev):
                after(pe, c_clip, b, 1)
                after(pe, c_dx, b, 1)
                if row_is(b, LAST):
                    after(pe, c_g1, b, 7)
                elif prev is not None:
                    after(pe, c_qtc, prev, 3)
                for g in range(GJ):
                    for j in range(TJ):
                        last = mm(bank_warp(b)[0:TP, g * C:(g + 1) * C], A[:, j, g * TP:(g + 1) * TP], dx[:, j, :],
                                  start=j == 0, stop=j == TJ - 1)
                last.then_inc(c_warp.sem, 1)

            def xn_transposed(b, prev):
                after(pe, c_xn, b, 1)
                if row_is(b, LAST):
                    after(pe, c_b2, b, TJ)
                elif prev is not None:
                    after(pe, c_ms, prev, 1)
                for j in range(GJ):
                    last = nc.tensor.transpose(bank_xn(b)[:, j * TP:(j + 1) * TP], xn[:, j, :], ident[0:TP, 0:TP])
                last.then_inc(c_xnt.sem, 1)

            def values(b, prev, j):
                after(pe, c_xl, b, 1)
                if prev is None:
                    pe.wait_ge(s_prep, N_PREP)
                if j == 0 and row_is(b, LAST):
                    after(pe, c_qtc, prev, 3)
                elif j == 0:
                    after(pe, c_h, b, 1)
                elif j == 1:
                    after(pe, c_csn, b, 1)
                elif row_is(b, LAST):
                    after(pe, c_b2, b, 5)
                elif prev is not None:
                    after(pe, c_o, prev, 1)
                ps = bank_vq(b, j)[0:TP, :]
                cols, w = slice(j * TP, (j + 1) * TP), slice(2 * HID, 3 * HID)
                split(ps, xh[:, cols], xl[:, cols], Wqh[:, w], Wql[:, w]).then_inc(c_v.sem, 1)

            def queries(b, prev, j):
                after(pe, c_vc, b, j + 1)
                ps = bank_vq(b, j)[0:TP, :]
                cols, w = slice(j * TP, (j + 1) * TP), slice(0, HID)
                split(ps, xh[:, cols], xl[:, cols], Wqh[:, w], Wql[:, w]).then_inc(c_q.sem, 1)

            def keys(b, prev, p):
                if p >= 1:
                    after(pe, c_qs, b, p)
                else:
                    after(pe, c_xl, b, 1)
                if row_is(b, LAST) and p in (0, 3):
                    after(pe, c_ms if p == 0 else c_o, b - 1, 1)
                bank = psC[(1 + p) % 4]
                w = slice(HID + p * 128, HID + (p + 1) * 128)
                split(bank[:, 0:G + 1], Wqh[:, w], Wql[:, w], xh[:], xl[:])
                mm(bank[:, G:NK], ident[:], mkv[:, 0, p, :], start=True, stop=True).then_inc(c_k.sem, 1)

            def k_transposed(b, prev, j):
                after(pe, c_ke, b, 4)
                if j == 1 and prev is not None:
                    after(pe, c_pp, prev, 1)
                cols = slice(j * TP, (j + 1) * TP) if j < GJ else slice(G, NK)
                rows = TP if j < GJ else NM
                for p in range(PAIRS):
                    last = nc.tensor.transpose(psC[j][0:rows, p * 128:(p + 1) * 128], ek[:, p, cols], ident[:])
                last.then_inc(c_kt.sem, 1)

            def q_transposed(b, prev, j):
                after(pe, c_qn, b, 1)
                after(pe, c_kta, b, j + 1)
                if ends(b) and j == 0:
                    after(pe, c_cba, b, 1)
                    after(pe, c_cbd, b, 1)
                for p in range(PAIRS):
                    last = nc.tensor.transpose(psC[j][:, p * TP:(p + 1) * TP], q[:, j, p * 128:(p + 1) * 128],
                                               ident[0:TP, 0:TP])
                last.then_inc(c_qt.sem, 1)

            def context(b, prev):
                after(pe, c_vc, b, 3)
                after(pe, c_kta, b, 4)
                if not ends(b):
                    after(pe, c_qtc, b, 1)
                for p in range(PAIRS):
                    d = slice(p * 128, (p + 1) * 128)
                    for j in range(GJ):
                        mm(psC[0][:, d], v[:, j, d], kT[:, j, d], start=j == 0, stop=False)
                    last = mm(psC[0][:, d], mvT[:, d], kTm[:, d], start=False, stop=True)
                last.then_inc(c_ctx.sem, 1)

            def fold(b, prev):
                after(pe, c_cba, b, 1)
                after(pe, c_cbd, b, 1)
                after(pe, c_qtc, b, 2)
                for p in range(PAIRS):
                    last = mm(psC[1][:, p * C:(p + 1) * C], cbd[:, p, :], wo[:, p, :], start=True, stop=True)
                last.then_inc(c_m.sem, 1)

            def attend(b, prev):
                after(pe, c_ms, b, 1)
                after(pe, c_qtc, b, 3)
                for j in range(GJ):
                    for p in range(PAIRS):
                        last = mm(psC[0][0:TP, j * C:(j + 1) * C], qT[:, j, p, :], m[:, p, :], start=p == 0, stop=p == PAIRS - 1)
                last.then_inc(c_fin.sem, 1)

            def xf_transposed(b, m):
                after(pe, c_xf, b, 1)
                if m is not None:
                    after(pe, c_g1, m, 8)
                if row_is(b, LAST):
                    after(pe, c_qtc, b, 3)
                for j in range(GJ):
                    last = nc.tensor.transpose(bank_xf(b)[:, j * TP:(j + 1) * TP], xf[:, j, :], ident[0:TP, 0:TP])
                last.then_inc(c_xft.sem, 1)

            def logits(b, m):
                after(pe, c_xfc, b, 1)
                if m is not None:
                    after(pe, c_g1, m, 7)
                if row_is(b, LAST - 1):
                    after(pe, c_h, LAST, 1)
                if row_is(b, LAST):
                    after(pe, c_kta, b, 4)
                for j in range(GJ):
                    last = mm(bank_lg(b)[0:TP, j * E:(j + 1) * E], xfT[:, j * TP:(j + 1) * TP], swT[:], start=True, stop=True)
                last.then_inc(c_lg.sem, 1)

            def positions(b, f):
                after(pe, c_oh, b, 1)
                after(pe, c_cnt, b, 4)
                if row_is(b, LAST - 1):
                    after(pe, c_xl, f, 1)
                elif f is not None:
                    after(pe, c_ke, f, 1)
                ps = bank_pos(b)[0:TP, 0:GJ * E]
                mm(ps, tri_b[:], oh[:].rearrange("p j e -> p (j e)"), start=True, stop=False)
                mm(ps, ones_b[:], cnt[:, 0:GJ, :].rearrange("p j e -> p (j e)"), start=False, stop=True).then_inc(c_pos.sem, 1)

            def setup():
                pe.wait_ge(s_wr, 16 * N_WR)
                for p in range(PAIRS):
                    last = nc.tensor.transpose(psC[0][0:NM, p * 128:(p + 1) * 128], mkv[:, 1, p, :], ident[:])
                last.then_inc(s_prept, 1)
                nc.tensor.transpose(psC[1][:, 0:E], swf[:], ident[0:E, 0:E]).then_inc(s_prept, 1)
                for i in range(4):
                    if i >= 2:
                        pe.wait_ge(s_prepc, 1 + i)
                    for k in range(4):
                        last = nc.tensor.transpose(psC[2 + i % 2][:, k * 128:(k + 1) * 128], ewf[:, 4 * i + k, :], ident[:])
                    last.then_inc(s_prept, 1)
                pe.wait_ge(s_const, N_CONST)

            def x_next(m, k):
                if has_next(m):
                    for i in range(2):
                        x_transposed(m + 1, m, i, k)

            def expert_tokens(p):
                if p % 4 == 0:
                    pe.wait_ge(s_sx[p // 4], 32)
                if p < 2:
                    after(pe, c_lb, LAST - 1, 1)
                    after(pe, c_xfc, LAST - 1, 1)
                    after(pe, c_g1, LAST, 8)
                else:
                    pe.wait_ge(s_exc, p - 1)
                ps = psA[p % 2]
                for i in range(2):
                    nc.tensor.transpose(ps[:, i * CAP:i * CAP + SA], sx_a[:, 2 * p + i, :], ident[0:SA, 0:SA])
                    last = nc.tensor.transpose(ps[:, i * CAP + SA:(i + 1) * CAP], sx_b[:, 2 * p + i, :], ident[0:SB, 0:SB])
                last.then_inc(s_ext, 1)

            def expert_products(p):
                pe.wait_ge(s_exc, p + 1)
                if p < 2:
                    after(pe, c_b2, LAST, TJ)
                    after(pe, c_pp, LAST - 1, 1)
                else:
                    pe.wait_ge(s_eyb, p - 1)
                ps, xT = psB[p % 2], sxT[:, p % 2, :]
                for i in range(2):
                    w = ewT[:, 2 * p + i, :]
                    mm(ps[0:SA, i * C:(i + 1) * C], xT[:, i * CAP:i * CAP + SA], w, start=True, stop=True)
                    last = mm(ps[0:SB, (2 + i) * C:(3 + i) * C], xT[:, i * CAP + SA:(i + 1) * CAP], w, start=True, stop=True)
                last.then_inc(s_ey, 1)

            def chosen_on_rows():
                pe.wait_ge(s_rmw, 1)
                for j in range(GJ):
                    last = nc.tensor.transpose(psC[2][:, j * TP:(j + 1) * TP], rmw[:, j, :], ident[0:TP, 0:TP])
                last.then_inc(s_rmt, 1)

            def dense():
                banks = (psC[0], psC[1], psC[3])
                after(pe, c_o, LAST, 1)
                after(pe, c_pp, LAST, 1)
                after(pe, c_lb, LAST, 1)
                pe.wait_ge(s_only, 1)
                for j in range(GJ):
                    mm(banks[j][0:TP, 0:C], ohT[:, j * TP:(j + 1) * TP], ebs[:], start=True, stop=False)
                for e in range(E):
                    pe.wait_ge(s_only, e + 2)
                    for j in range(GJ):
                        last = mm(banks[j][0:TP, 0:C], only[e][:, j * TP:(j + 1) * TP], ewT[:, e, :], start=False, stop=e == E - 1)
                last.then_inc(s_dense, 1)

            def step(m, f, k, r):
                if m is not None:
                    layer1(m, before(m), 0, 0)
                    layer1(m, before(m), 0, 1)
                if k is not None:
                    k_transposed(k, before(k), 0)
                    k_transposed(k, before(k), 1)
                if m is not None:
                    layer1(m, before(m), 0, 2)
                if k is not None:
                    k_transposed(k, before(k), 2)
                if m is not None:
                    layer1(m, before(m), 0, 3)
                if k is not None:
                    k_transposed(k, before(k), 3)
                if m is not None:
                    layer1(m, before(m), 1, 0)
                    layer1(m, before(m), 1, 1)
                if k is not None:
                    for j in range(GJ):
                        q_transposed(k, before(k), j)
                    context(k, before(k))
                if f is not None:
                    sums(f, before(f))
                if m is not None:
                    layer1(m, before(m), 1, 2)
                    layer1(m, before(m), 1, 3)
                    layer2(m, before(m), 0)
                if k is not None:
                    fold(k, before(k))
                if f is not None:
                    warp(f, before(f))
                if k is not None:
                    attend(k, before(k))
                if m is not None:
                    layer2(m, before(m), 1)
                    layer2(m, before(m), 2)
                if f is not None:
                    xn_transposed(f, before(f))
                if m is not None:
                    layer2(m, before(m), 3)
                if f is not None:
                    for j in range(GJ):
                        values(f, before(f), j)
                    for j in range(GJ):
                        queries(f, before(f), j)
                if m is not None:
                    layer2(m, before(m), 4)
                if k is not None:
                    xf_transposed(k, m)
                if f is not None:
                    keys(f, before(f), 0)
                if k is not None:
                    logits(k, m)
                if f is not None:
                    for p in range(1, PAIRS):
                        keys(f, before(f), p)
                if m is not None:
                    x_next(m, k)
                    layer2(m, before(m), 5)
                if k is not None:
                    positions(k, f)

            def ending(f, k, r):
                if k is not None:
                    for j in range(4):
                        k_transposed(k, before(k), j)
                if f is not None:
                    sums(f, before(f))
                if k is not None:
                    context(k, before(k))
                if f is not None:
                    warp(f, before(f))
                if k == LAST:
                    expert_tokens(0)
                    expert_tokens(1)
                if k is not None:
                    for j in range(GJ):
                        q_transposed(k, before(k), j)
                if k == LAST:
                    expert_products(0)
                    expert_tokens(2)
                if k is not None:
                    fold(k, before(k))
                if k == LAST:
                    expert_products(1)
                    expert_tokens(3)
                if k is not None:
                    attend(k, before(k))
                if k == LAST:
                    expert_products(2)
                if f is not None:
                    xn_transposed(f, before(f))
                    for j in range(GJ):
                        values(f, before(f), j)
                    for j in range(GJ):
                        queries(f, before(f), j)
                if k == LAST:
                    for p in range(3, E // 2 - 1):
                        expert_tokens(p + 1)
                        expert_products(p)
                    expert_products(E // 2 - 1)
                if f is not None:
                    keys(f, before(f), 0)
                if k is not None:
                    xf_transposed(k, None)
                    logits(k, None)
                if k == LAST:
                    chosen_on_rows()
                if k is not None:
                    positions(k, f)
                if f is not None:
                    for p in range(1, PAIRS):
                        keys(f, before(f), p)
                if r == LAST:
                    dense()

            pe.wait_ge(s_ident, 1)
            for i in range(2):
                x_transposed(0, None, i, None)
            pe.wait_ge(s_const, 2)
            pe.wait_ge(s_prep, 2)
            pipeline(pe, step, ending, setup)

        @block.vector
        def _(dve):
            vec = nc.vector

            def setup():
                dve.wait_ge(s_wr, 16 * N_WR)
                vec.tensor_scalar(Wqf, Wqf, nwc[:, 0:1], ROOT_C, ALU.mult, ALU.mult).then_inc(s_prep, 1)
                vec.tensor_scalar(onr[:], onr[:], ROOT_C, None, ALU.mult).then_inc(s_prep, 1)
                dve.wait_ge(s_prep, 6)
                vec.tensor_copy(Wqh[:], Wqf).then_inc(s_prep, 1)
                dve.wait_ge(s_prep, 7)
                vec.tensor_tensor(Wql[:], Wqf, Wqh[:], ALU.subtract).then_inc(s_prep, 1)
                dve.wait_ge(s_const, N_CONST)
                dve.wait_ge(s_prep, N_PREP)

            def x_lo(b, prev, i):
                after(dve, c_xth, b, i + 1)
                if prev is not None:
                    after(dve, c_l1, prev, 8)
                vec.tensor_tensor(xTl[:, i, 0:HALF], psA[i][:, 0:HALF], xTh[:, i, 0:HALF], ALU.subtract).then_inc(c_xtl.sem, 1)

            def split_h1(b, prev, i):
                after(dve, c_g1, b, HK * (i + 1))
                if prev is not None:
                    after(dve, c_l2, prev, GJ * (i + 1))
                vec.tensor_copy(h1h[:, :, i, :], h1[:, :, i, :]).then_inc(c_h1h.sem, 1)
                after(dve, c_h1h, b, i + 1)
                vec.tensor_tensor(h1l[:, :, i, :], h1[:, :, i, :], h1h[:, :, i, :], ALU.subtract).then_inc(c_h1l.sem, 1)

            def bias2(b, prev, j):
                after(dve, c_l2, b, j + 1)
                if j >= 4:
                    after(dve, c_z, b, j - 3)
                elif prev is not None:
                    after(dve, c_z, prev, h2_before(j) + 1)
                vec.tensor_tensor(h2b[:, h2_slot(j), :], psB[j % 2][0:TP, :], b2r[:], ALU.add).then_inc(c_b2.sem, 1)

            def dot3(b, prev, j):
                after(dve, c_g2, b, j + 1)
                if prev is not None and j == 0:
                    after(dve, c_nz, prev, 1)
                vec.tensor_tensor_reduce(h2b[:, h2_slot(j), :], h2b[:, h2_slot(j), :], W3r[:], 1.0, 0.0, ALU.mult, ALU.add,
                                         z[:, j:j + 1]).then_inc(c_z.sem, 1)

            def minus_z(b, prev):
                after(dve, c_z, b, TJ)
                if prev is not None:
                    after(dve, c_sig, prev, 1)
                vec.tensor_scalar(sg[:, 0], z[:], b3r[:, 0:1], -1.0, ALU.add, ALU.mult).then_inc(c_nz.sem, 1)

            def scan(b, prev):
                after(dve, c_sig, b, 1)
                if prev is not None:
                    after(dve, c_s, prev, 2)
                vec.tensor_scalar(sg[:, 2], sg[:, 1], 1.0, None, ALU.add).then_inc(c_s.sem, 1)
                after(dve, c_s, b, 1)
                if prev is not None:
                    after(dve, c_cs, prev, 1)
                vec.reciprocal(sx[:, 0:TJ], sg[:, 2]).then_inc(c_s.sem, 1)
                after(dve, c_s, b, 2)
                vec.tensor_tensor_scan(pre[:, 1:TJ + 1], ones[0:TP, 0:TJ], sx[:, 0:TJ], 0.0, ALU.mult, ALU.add).then_inc(c_scan.sem, 1)

            def lengths(b, prev):
                after(dve, c_cs, b, 1)
                vec.reciprocal(rt[:], psC[3][0:TP, TJ:TJ + 1]).then_inc(c_rt.sem, 1)
                after(dve, c_rt, b, 1)
                if prev is not None:
                    after(dve, c_rel, prev, 1)
                vec.tensor_scalar(cs[:], psC[3][0:TP, 0:TJ], rt[:, 0:1], float(G), ALU.mult, ALU.mult).then_inc(c_csn.sem, 1)

            def warp_weights(b, prev):
                after(dve, c_csn, b, 1)
                if prev is not None:
                    after(dve, c_warp, prev, 1)
                for j in range(TJ):
                    last = vec.tensor_scalar(A[:, j, :], neg_g[:], cs[:, j:j + 1], 0.0, ALU.add, ALU.max)
                last.then_inc(c_rel.sem, 1)
                after(dve, c_rel, b, 1)
                vec.tensor_scalar(A[:, :, 0:G - 1], A[:, :, 0:G - 1], 1.0, None, ALU.min).then_inc(c_clip.sem, 1)

            def keep_h(b, prev):
                after(dve, c_h, b, 1)
                if prev is not None:
                    after(dve, c_h2, prev, 1)
                vec.tensor_copy(hres[:], h[:]).then_inc(c_hres.sem, 1)

            def moments1(b, prev):
                after(dve, c_h, b, 1)
                for j in range(GJ):
                    vec.bn_stats(st[:, j, :], h[:, j, :]).then_inc(c_bn.sem, 1)
                after(dve, c_bn, b, 3)
                dve.wait_ge(s_const, N_CONST)
                for j in range(GJ):
                    last = vec.bn_aggr(mv1[:, j, :], st[:, j, :])
                last.then_inc(c_mv.sem, 1)
                after(dve, c_mv, b, 1)
                if prev is not None:
                    after(dve, c_rs1, prev, 1)
                vec.tensor_scalar(rs1[:, 0], mv1[:, :, 1], EPS, None, ALU.add).then_inc(c_var.sem, 1)
                vec.tensor_scalar(rs1[:, 1], mv1[:, :, 1], float(C), None, ALU.mult).then_inc(c_var.sem, 1)

            def normal1(b, prev):
                after(dve, c_rs1, b, 1)
                if prev is not None:
                    after(dve, c_xn, prev, 1)
                vec.tensor_tensor(rs1[:, 4], rs1[:, 2], rs1[:, 3], ALU.mult).then_inc(c_sc.sem, 1)
                after(dve, c_sc, b, 1)
                vec.tensor_scalar(rs1[:, 5], rs1[:, 4], 1e-12, None, ALU.max).then_inc(c_sc.sem, 1)
                after(dve, c_sc, b, 2)
                vec.reciprocal(rs1[:, 6], rs1[:, 5]).then_inc(c_sc.sem, 1)
                after(dve, c_sc, b, 3)
                vec.tensor_tensor(rs1[:, 7], rs1[:, 6], rs1[:, 2], ALU.mult).then_inc(c_sc.sem, 1)
                after(dve, c_sc, b, 4)
                if prev is not None:
                    after(dve, c_xnt, prev, 1)
                after(dve, c_mv, b, 1)
                for j in range(GJ):
                    last = vec.tensor_scalar(xn[:, j, :], h[:, j, :], mv1[:, j, 0:1], rs1[:, 7, j:j + 1], ALU.subtract, ALU.mult)
                last.then_inc(c_xn.sem, 1)

            def xn_lo(b, prev):
                after(dve, c_xh, b, 1)
                vec.tensor_tensor(xl[:, 0:G], bank_xn(b)[:, 0:G], xh[:, 0:G], ALU.subtract).then_inc(c_xl.sem, 1)

            def query_max(b, prev, j):
                after(dve, c_q, b, j + 1)
                ps = bank_vq(b, j)[0:TP, :].rearrange("p (h d) -> p h d", h=HEADS)
                vec.tensor_reduce(qm[:, j, :], ps, AX.X, ALU.max).then_inc(c_qm.sem, 1)
                after(dve, c_qm, b, j + 1)
                if prev is not None:
                    after(dve, c_qt, prev, 3)
                vec.tensor_tensor(q[:, j, :].rearrange("p (h d) -> p h d", h=HEADS), ps,
                                  qm[:, j, :].unsqueeze(2).to_broadcast([TP, HEADS, D]), ALU.subtract).then_inc(c_qs.sem, 1)

            def key_max(b, prev, p):
                after(dve, c_k, b, p + 1)
                if prev is not None:
                    after(dve, c_ke, prev, 4)
                vec.tensor_reduce(nkm[:, p:p + 1], psC[(1 + p) % 4][:, 0:NK], AX.X, ALU.max, negate=True).then_inc(c_km.sem, 1)

            q3 = q.rearrange("p j (h d) -> p (j h) d", d=D)

            def query_sum(b, prev):
                after(dve, c_qe, b, GJ)
                if prev is not None:
                    after(dve, c_rq, prev, 1)
                vec.tensor_reduce(qsum[:], q3, AX.X, ALU.add).then_inc(c_qsum.sem, 1)
                after(dve, c_qsum, b, 1)
                vec.reciprocal(rq[:], qsum[:]).then_inc(c_rq.sem, 1)

            def query_norm(b, prev):
                after(dve, c_rq, b, 1)
                vec.scalar_tensor_tensor(q3, q3, float(D) ** -0.5, rq[:].unsqueeze(2).to_broadcast([TP, GJ * HEADS, D]),
                                         ALU.mult, ALU.mult).then_inc(c_qn.sem, 1)

            def take_ctx(b, prev):
                after(dve, c_ctx, b, 1)
                if prev is not None:
                    after(dve, c_m, prev, 1)
                vec.tensor_copy(cbd[0:D, :, 0:D], psC[0][0:D, :].rearrange("p (a d) -> p a d", a=PAIRS)[:, :, 0:D]).then_inc(c_cbd.sem, 1)

            def key_sum(b, prev):
                after(dve, c_ke, b, 4)
                if prev is not None:
                    after(dve, c_ms, prev, 1)
                vec.reciprocal(rk[:], ksum[:]).then_inc(c_rk.sem, 1)

            def take_m(b, prev):
                after(dve, c_m, b, 1)
                after(dve, c_rk, b, 1)
                if prev is not None:
                    after(dve, c_fin, prev, 1)
                vec.tensor_tensor(m[:], psC[1][:].rearrange("p (a c) -> p a c", a=PAIRS),
                                  rk[:].unsqueeze(2).to_broadcast([128, PAIRS, C]), ALU.mult).then_inc(c_ms.sem, 1)

            def out_norm(b, prev):
                after(dve, c_fin, b, 1)
                if prev is not None:
                    after(dve, c_on, prev, 3)
                vec.tensor_tensor(o[:], psC[0][0:TP, 0:GJ * C].rearrange("p (j c) -> p j c", j=GJ),
                                  bor[:].unsqueeze(1).to_broadcast([TP, GJ, C]), ALU.add).then_inc(c_o.sem, 1)
                after(dve, c_o, b, 1)
                if prev is not None:
                    after(dve, c_rs2, prev, 1)
                    after(dve, c_h2, prev, 1)
                for j in range(GJ):
                    vec.tensor_tensor_reduce(osq[:, j, :], o[:, j, :], o[:, j, :], 1.0, 0.0, ALU.mult, ALU.add,
                                             ss[:, j:j + 1]).then_inc(c_ss.sem, 1)

            def residual(b, prev):
                after(dve, c_ss, b, 3)
                after(dve, c_rs2, b, 1)
                if prev is not None:
                    after(dve, c_on, prev, 3)
                vec.tensor_scalar(rs2[:, 1], rs2[:, 0], 1e-12, None, ALU.max).then_inc(c_ro.sem, 1)
                after(dve, c_ro, b, 1)
                vec.reciprocal(rs2[:, 2], rs2[:, 1]).then_inc(c_ro.sem, 1)
                after(dve, c_ro, b, 2)
                for j in range(GJ):
                    vec.scalar_tensor_tensor(osq[:, j, :], o[:, j, :], rs2[:, 2, j:j + 1], onr[:], ALU.mult, ALU.mult).then_inc(c_on.sem, 1)
                after(dve, c_on, b, 3)
                after(dve, c_hres, b, 1)
                if prev is not None:
                    after(dve, c_base, prev, 3)
                vec.tensor_tensor(h2[:], hres[:], osq[:], ALU.add).then_inc(c_h2.sem, 1)

            def moments2(b, prev):
                after(dve, c_h2, b, 1)
                for j in range(GJ):
                    vec.bn_stats(st2[:, j, :], h2[:, j, :]).then_inc(c_bn2.sem, 1)
                after(dve, c_bn2, b, 3)
                dve.wait_ge(s_const, N_CONST)
                for j in range(GJ):
                    last = vec.bn_aggr(mv2[:, j, :], st2[:, j, :])
                last.then_inc(c_mv2.sem, 1)
                after(dve, c_mv2, b, 1)
                if prev is not None:
                    after(dve, c_rs3, prev, 1)
                vec.tensor_scalar(rs3[:, 0], mv2[:, :, 1], EPS, None, ALU.add).then_inc(c_var2.sem, 1)

            def normal2(b, prev):
                after(dve, c_mv2, b, 1)
                after(dve, c_rs3, b, 1)
                if prev is not None:
                    after(dve, c_xft, prev, 1)
                    after(dve, c_sct, prev, 48)
                    after(dve, c_base, prev, 3)
                for j in range(GJ):
                    last = vec.tensor_scalar(xf[:, j, :], h2[:, j, :], mv2[:, j, 0:1], rs3[:, 1, j:j + 1], ALU.subtract, ALU.mult)
                last.then_inc(c_xf.sem, 1)

            def take_logits(b, prev):
                after(dve, c_lg, b, 1)
                if prev is not None:
                    after(dve, c_ls, prev, 1)
                vec.tensor_tensor(lg[:], bank_lg(b)[0:TP, 0:GJ * E].rearrange("p (j e) -> p j e", j=GJ),
                                  swbr[:].unsqueeze(1).to_broadcast([TP, GJ, E]), ALU.add).then_inc(c_lb.sem, 1)

            def route(b, prev):
                after(dve, c_lb, b, 1)
                vec.tensor_reduce(mx[:], lg[:], AX.X, ALU.max).then_inc(c_mx.sem, 1)
                after(dve, c_mx, b, 1)
                mxb = mx[:].unsqueeze(2).to_broadcast([TP, GJ, E])
                rkb = rank[:].unsqueeze(1).to_broadcast([TP, GJ, E])
                vec.tensor_tensor(eq[:], lg[:], mxb, ALU.is_equal).then_inc(c_eq.sem, 1)
                if prev is not None:
                    after(dve, c_sume, prev, 1)
                vec.tensor_tensor(le[:], lg[:], mxb, ALU.subtract).then_inc(c_ls.sem, 1)
                after(dve, c_eq, b, 1)
                vec.tensor_tensor(eq[:], eq[:], rkb, ALU.mult).then_inc(c_eq.sem, 1)
                after(dve, c_eq, b, 2)
                if prev is not None:
                    after(dve, c_idx, prev, 1)
                vec.tensor_reduce(rm[:], eq[:], AX.X, ALU.max).then_inc(c_rm.sem, 1)
                after(dve, c_rm, b, 1)
                if prev is not None:
                    after(dve, c_cnt, prev, 4)
                    after(dve, c_pos, prev, 1)
                vec.tensor_tensor(oh[:], rkb, rm[:].unsqueeze(2).to_broadcast([TP, GJ, E]), ALU.is_equal).then_inc(c_oh.sem, 1)

            def place_in_expert(b, prev):
                after(dve, c_pos, b, 1)
                vec.tensor_tensor(pp[:], bank_pos(b)[0:TP, 0:GJ * E].rearrange("p (j e) -> p j e", j=GJ), oh[:], ALU.mult).then_inc(c_pp.sem, 1)
                after(dve, c_pp, b, 1)
                if prev is not None:
                    after(dve, c_idx, prev, 2)
                vec.tensor_reduce(pos[:], pp[:], AX.X, ALU.add).then_inc(c_pp.sem, 1)
                after(dve, c_pp, b, 2)
                if prev is not None:
                    after(dve, c_idx, prev, 4)
                    after(dve, c_ck, prev, 1)
                vec.tensor_scalar(keep[:], pos[:], float(CAP), None, ALU.is_le).then_inc(c_keep.sem, 1)

            def probability(b, prev):
                after(dve, c_le, b, 1)
                vec.tensor_reduce(sume[:], le[:], AX.X, ALU.add).then_inc(c_sume.sem, 1)
                after(dve, c_sume, b, 1)
                vec.reciprocal(rp[:], sume[:]).then_inc(c_rp.sem, 1)

            def keep_base(b, prev):
                after(dve, c_rp, b, 1)
                after(dve, c_keep, b, 1)
                ckb = ck[:, bass.ds(b * GJ, GJ)]
                vec.tensor_tensor(ckb, keep[:], rp[:], ALU.mult).then_inc(c_ck.sem, 1)
                after(dve, c_ck, b, 1)
                vec.tensor_tensor(nk[:], rp[:], ckb, ALU.subtract).then_inc(c_ck.sem, 1)
                after(dve, c_ck, b, 2)
                for j in range(GJ):
                    vec.scalar_tensor_tensor(base[:, bass.ds(b * GJ + j, 1), :].rearrange("p o c -> p (o c)"), xf[:, j, :], nk[:, j:j + 1], h2[:, j, :],
                                             ALU.mult, ALU.add).then_inc(c_base.sem, 1)

            def x_lo_next(m):
                if has_next(m):
                    for i in range(2):
                        x_lo(m + 1, m, i)

            def expert_bias(p):
                if p == 0:
                    dve.wait_ge(s_eb, 16)
                    after(dve, c_h1l, LAST, 2)
                    after(dve, c_warp, LAST, 1)
                dve.wait_ge(s_ey, p + 1)
                pair = slice(2 * p, 2 * p + 2)
                ps = psB[p % 2][:].rearrange("p (e c) -> p e c", c=C)
                vec.tensor_tensor(ya[:, pair, :], ps[0:SA, 0:2, :], ebr[0:SA, pair, :], ALU.add)
                vec.tensor_tensor(yb[:, pair, :], ps[0:SB, 2:4, :], ebr[0:SB, pair, :], ALU.add).then_inc(s_eyb, 1)

            def spread_choice():
                after(dve, c_rm, LAST, 1)
                after(dve, c_h2, LAST, 1)
                vec.tensor_copy(rmw[:], rm[:].unsqueeze(2).to_broadcast([TP, GJ, C])).then_inc(s_rmw, 1)

            def only_own():
                dve.wait_ge(s_rmt, 1)
                after(dve, c_fin, LAST, 1)
                after(dve, c_ctx, LAST, 1)
                vec.tensor_scalar(ohT, psC[2][0:E, 0:G], rank_e[:, 0:1], None, ALU.is_equal).then_inc(s_only, 1)
                after(dve, c_xfc, LAST, 1)
                for e in range(E):
                    if e == IN_QT:
                        dve.wait_ge(s_eyb, E // 2)
                    vec.scalar_tensor_tensor(only[e], psC[2][:, 0:G], float(E - e), xfT[:], ALU.is_equal, ALU.mult).then_inc(s_only, 1)

            def finish_row(b):
                if b < LAST:
                    dve.wait_ge(s_yg[b], 16 * GJ)
                    y = [yg[b][:, j, :] for j in range(GJ)]
                else:
                    dve.wait_ge(s_dense, 1)
                    y = [ps[0:TP, 0:C] for ps in (psC[0], psC[1], psC[3])]
                    after(dve, c_xt, LAST, 2)
                    after(dve, c_dx, LAST, 1)
                after(dve, c_base, b, 3)
                for j in range(GJ):
                    i = b * GJ + j
                    last = vec.scalar_tensor_tensor(yg[b][:, j, :], y[j], ck[:, i:i + 1], base[:, i, :], ALU.mult, ALU.add)
                last.then_inc(s_res, 1)

            def step(m, f, k, r):
                if k is not None:
                    key_sum(k, before(k))
                    query_sum(k, before(k))
                    query_norm(k, before(k))
                if f is not None:
                    dot3(f, before(f), 4)
                    dot3(f, before(f), 5)
                    minus_z(f, before(f))
                if m is not None:
                    split_h1(m, before(m), 0)
                if f is not None:
                    scan(f, before(f))
                if k is not None:
                    take_ctx(k, before(k))
                if f is not None:
                    lengths(f, before(f))
                    warp_weights(f, before(f))
                if m is not None:
                    bias2(m, before(m), 0)
                if k is not None:
                    take_m(k, before(k))
                if m is not None:
                    split_h1(m, before(m), 1)
                if r is not None:
                    probability(r, before(r))
                    keep_base(r, before(r))
                if m is not None:
                    dot3(m, before(m), 0)
                if f is not None:
                    moments1(f, before(f))
                if k is not None:
                    out_norm(k, before(k))
                if m is not None:
                    bias2(m, before(m), 1)
                if f is not None:
                    normal1(f, before(f))
                if m is not None:
                    dot3(m, before(m), 1)
                    bias2(m, before(m), 2)
                if f is not None:
                    xn_lo(f, before(f))
                if k is not None:
                    residual(k, before(k))
                    moments2(k, before(k))
                if f is not None:
                    keep_h(f, before(f))
                if m is not None:
                    dot3(m, before(m), 2)
                    bias2(m, before(m), 3)
                if f is not None:
                    query_max(f, before(f), 0)
                if k is not None:
                    normal2(k, before(k))
                if f is not None:
                    query_max(f, before(f), 1)
                    query_max(f, before(f), 2)
                if m is not None:
                    dot3(m, before(m), 3)
                if f is not None:
                    key_max(f, before(f), 0)
                if k is not None:
                    take_logits(k, before(k))
                if f is not None:
                    for p in range(1, PAIRS):
                        key_max(f, before(f), p)
                if k is not None:
                    route(k, before(k))
                if m is not None:
                    x_lo_next(m)
                    bias2(m, before(m), 4)
                    bias2(m, before(m), 5)
                if k is not None:
                    place_in_expert(k, before(k))

            def ending(f, k, r):
                if k is not None:
                    key_sum(k, before(k))
                if f is not None:
                    dot3(f, before(f), 4)
                    dot3(f, before(f), 5)
                    minus_z(f, before(f))
                if k is not None:
                    query_sum(k, before(k))
                if f is not None:
                    scan(f, before(f))
                if k is not None:
                    query_norm(k, before(k))
                if f is not None:
                    lengths(f, before(f))
                    warp_weights(f, before(f))
                if r is not None:
                    probability(r, before(r))
                    keep_base(r, before(r))
                if f is not None:
                    moments1(f, before(f))
                if k == LAST:
                    expert_bias(0)
                if k is not None:
                    take_m(k, before(k))
                if k == LAST:
                    expert_bias(1)
                if f is not None:
                    normal1(f, before(f))
                if k is not None:
                    out_norm(k, before(k))
                if f is not None:
                    xn_lo(f, before(f))
                if k == LAST:
                    expert_bias(2)
                if k is not None:
                    residual(k, before(k))
                if k == LAST:
                    expert_bias(3)
                    expert_bias(4)
                if k is not None:
                    moments2(k, before(k))
                if f is not None:
                    query_max(f, before(f), 0)
                if k == LAST:
                    expert_bias(5)
                    expert_bias(6)
                if k is not None:
                    normal2(k, before(k))
                if k == LAST:
                    expert_bias(7)
                if f is not None:
                    keep_h(f, before(f))
                if k is not None:
                    take_logits(k, before(k))
                    route(k, before(k))
                if f is not None:
                    query_max(f, before(f), 1)
                    query_max(f, before(f), 2)
                if k == LAST:
                    spread_choice()
                if k is not None:
                    place_in_expert(k, before(k))
                if f is not None:
                    key_max(f, before(f), 0)
                    for p in range(1, PAIRS):
                        key_max(f, before(f), p)
                if k == LAST:
                    only_own()
                if r == LAST:
                    for b in range(GATHERED_FIRST):
                        finish_row(b)
                    finish_row(LAST)

            dve.wait_ge(s_w1, 16)
            vec.tensor_copy(W1h[:], W1f[:]).then_inc(s_prep, 1)
            dve.wait_ge(s_prep, 1)
            vec.tensor_tensor(W1l[:], W1f[:], W1h[:], ALU.subtract).then_inc(s_prep, 1)
            for i in range(2):
                x_lo(0, None, i)
            dve.wait_ge(s_w2, 16)
            vec.tensor_copy(W2h[:], W2f).then_inc(s_prep, 1)
            dve.wait_ge(s_prep, 3)
            vec.tensor_tensor(W2l[:], W2f, W2h[:], ALU.subtract).then_inc(s_prep, 1)
            dve.wait_ge(s_w3, 32)
            pipeline(dve, step, ending, setup)

            for b in range(GATHERED_FIRST, LAST):
                finish_row(b)


N_CONST = 17
N_WR = 12
N_PREP = 8

_INS = ['x', 'L0_tok_W1', 'L0_tok_b1', 'L0_tok_W2', 'L0_tok_b2', 'L0_tok_W3', 'L0_tok_b3', 'L0_attn_norm_w',
        'L0_attn_w_qkv', 'L0_attn_mem_kv', 'L0_attn_w_out', 'L0_attn_b_out', 'L0_attn_out_norm_w',
        'L0_ffn_switch_w', 'L0_ffn_switch_b', 'L0_ffn_expert_w', 'L0_ffn_expert_b']


def kernel(**inputs):
    import concourse.bacc as _bacc
    from concourse.bass_utils import run_bass_kernel_spmd as _run

    nc = _bacc.Bacc("TRN2", target_bir_lowering=False, num_devices=1)
    arrays, args = {}, []
    for name in _INS:
        a = np.ascontiguousarray(inputs[name])
        arrays[f"in_{name}"] = a
        args.append(nc.dram_tensor(f"in_{name}", a.shape, mybir.dt.from_np(a.dtype), kind="ExternalInput").ap())
    rows, tokens, channels = inputs["x"].shape
    args.append(nc.dram_tensor("out_0", (rows, tokens // 2, channels), F32, kind="ExternalOutput").ap())
    audio_tower(nc, *args)
    r = _run(nc, [arrays], core_ids=[0])
    return r.results[0]["out_0"]
```
